# Optimizing a Trainium2 kernel written in Bass

```python
import numpy as np
import jax
import jax.numpy as jnp

def _softmax(x, axis=-1):
    return jax.nn.softmax(x, axis=axis)

def _gelu(x):
    return jax.nn.gelu(x, approximate=True)

def _silu(x):
    return jax.nn.silu(x)

def _sigmoid(x):
    return jax.nn.sigmoid(x)

def _layernorm(x, axis=-1, eps=1e-05):
    m = jnp.mean(x, axis=axis, keepdims=True)
    v = jnp.var(x, axis=axis, keepdims=True)
    return (x - m) / jnp.sqrt(v + eps)

def _scatter_add(tgt, idx, src, axis=0):
    return tgt.at[idx].add(src)

def _segment_sum(src, seg, n):
    return jax.ops.segment_sum(src, seg, n)
kernel_name = 'mk_adaln_d1_jaxref_r8_b4f02f'

def setup_inputs(seed: int=0):
    np.random.seed(seed)
    _w = jnp.asarray

    def _L0_attn_setup():
        import jax, jax.numpy as jnp
        import numpy as np
        HID = 256
        NH = 16
        HD = 128
        R = 16
        WIN = 128
        ROPE = HD // 2
        EPS = 1e-06

        def rmsnorm(x, w):
            return x * jax.lax.rsqrt(jnp.mean(x * x, axis=-1, keepdims=True) + EPS) * w

        def apply_rope(x, pos):
            half = ROPE // 2
            inv_freq = 1.0 / 10000.0 ** (jnp.arange(half, dtype=jnp.float32) * 2.0 / ROPE)
            ang = pos.astype(jnp.float32)[:, None] * inv_freq[None, :]
            cos, sin = (jnp.cos(ang), jnp.sin(ang))
            x1, x2, rest = (x[..., :half], x[..., half:ROPE], x[..., ROPE:])
            return jnp.concatenate([x1 * cos - x2 * sin, x1 * sin + x2 * cos, rest], axis=-1)
        key = jax.random.key(seed)
        ks = jax.random.split(key, 16)
        s = 0.02
        return {'hidden_states': jax.random.normal(ks[0], (1, 256, HID), jnp.float32), 'Wq': jax.random.normal(ks[1], (HID, NH * HD), jnp.float32) * s, 'bq': jnp.zeros((NH * HD,), jnp.float32), 'Wc': jax.random.normal(ks[2], (HID, 1), jnp.float32) * s, 'bc': jnp.zeros((1,), jnp.float32), 'Wk': jax.random.normal(ks[3], (HID, HD), jnp.float32) * s, 'bk': jnp.zeros((HD,), jnp.float32), 'Wv': jax.random.normal(ks[4], (HID, HD), jnp.float32) * s, 'bv': jnp.zeros((HD,), jnp.float32), 'Wlk': jax.random.normal(ks[5], (HID, NH * HD), jnp.float32) * s, 'blk': jnp.zeros((NH * HD,), jnp.float32), 'Wlv': jax.random.normal(ks[6], (HID, NH * HD), jnp.float32) * s, 'blv': jnp.zeros((NH * HD,), jnp.float32), 'qn_w': jnp.ones((HD,), jnp.float32), 'kn_w': jnp.ones((HD,), jnp.float32), 'sink_k': jax.random.normal(ks[7], (NH, HD), jnp.float32) * s, 'sink_v': jax.random.normal(ks[8], (NH, HD), jnp.float32) * s, 'Wo': jax.random.normal(ks[9], (NH * HD, HID), jnp.float32) * s, 'bo': jnp.zeros((HID,), jnp.float32)}
    _L0_attn_in = _L0_attn_setup()

    def _L0_ffn_setup():
        import jax, jax.numpy as jnp
        import numpy as np
        B, S, H = (2, 256, 256)
        E, K = (16, 4)
        I_MOE, I_SH = (176, 704)
        key = jax.random.key(seed)
        ks = jax.random.split(key, 9)

        def w(k, shape, fan_in):
            return jax.random.normal(k, shape, jnp.float32) * fan_in ** (-0.5)
        return {'hidden_states': jax.random.normal(ks[0], (B, S, H), jnp.float32), 'router_w': w(ks[1], (E, H), H), 'w_gate': w(ks[2], (E, H, I_MOE), H), 'w_up': w(ks[3], (E, H, I_MOE), H), 'w_down': w(ks[4], (E, I_MOE, H), I_MOE), 'sh_gate': w(ks[5], (H, I_SH), H), 'sh_up': w(ks[6], (H, I_SH), H), 'sh_down': w(ks[7], (I_SH, H), I_SH), 'sh_gate_w': w(ks[8], (H, 1), H)}
    _L0_ffn_in = _L0_ffn_setup()
    _L0_c = _w((lambda *s: np.random.randn(*s).astype(np.float32) * 0.05)(1, 256))
    _L0_wmod = _w((lambda *s: np.random.randn(*s).astype(np.float32) * 0.05)(256, 6 * 256) * 256 ** (-0.5))
    _d = {'L0_attn_hidden_states': _L0_attn_in['hidden_states'], 'L0_attn_Wq': _L0_attn_in['Wq'], 'L0_attn_bq': _L0_attn_in['bq'], 'L0_attn_Wc': _L0_attn_in['Wc'], 'L0_attn_bc': _L0_attn_in['bc'], 'L0_attn_Wk': _L0_attn_in['Wk'], 'L0_attn_bk': _L0_attn_in['bk'], 'L0_attn_Wv': _L0_attn_in['Wv'], 'L0_attn_bv': _L0_attn_in['bv'], 'L0_attn_Wlk': _L0_attn_in['Wlk'], 'L0_attn_blk': _L0_attn_in['blk'], 'L0_attn_Wlv': _L0_attn_in['Wlv'], 'L0_attn_blv': _L0_attn_in['blv'], 'L0_attn_qn_w': _L0_attn_in['qn_w'], 'L0_attn_kn_w': _L0_attn_in['kn_w'], 'L0_attn_sink_k': _L0_attn_in['sink_k'], 'L0_attn_sink_v': _L0_attn_in['sink_v'], 'L0_attn_Wo': _L0_attn_in['Wo'], 'L0_attn_bo': _L0_attn_in['bo'], 'L0_ffn_router_w': _L0_ffn_in['router_w'], 'L0_ffn_w_gate': _L0_ffn_in['w_gate'], 'L0_ffn_w_up': _L0_ffn_in['w_up'], 'L0_ffn_w_down': _L0_ffn_in['w_down'], 'L0_ffn_sh_gate': _L0_ffn_in['sh_gate'], 'L0_ffn_sh_up': _L0_ffn_in['sh_up'], 'L0_ffn_sh_down': _L0_ffn_in['sh_down'], 'L0_ffn_sh_gate_w': _L0_ffn_in['sh_gate_w'], 'L0_c': _L0_c, 'L0_wmod': _L0_wmod}
    _x0 = _d['L0_attn_hidden_states']
    _d['L0_attn_hidden_states'] = jax.random.normal(jax.random.fold_in(jax.random.key(seed), 1), (1, 2048, 256), dtype=_x0.dtype)
    del _x0
    return _d

def reference(L0_attn_hidden_states, L0_attn_Wq, L0_attn_bq, L0_attn_Wc, L0_attn_bc, L0_attn_Wk, L0_attn_bk, L0_attn_Wv, L0_attn_bv, L0_attn_Wlk, L0_attn_blk, L0_attn_Wlv, L0_attn_blv, L0_attn_qn_w, L0_attn_kn_w, L0_attn_sink_k, L0_attn_sink_v, L0_attn_Wo, L0_attn_bo, L0_ffn_router_w, L0_ffn_w_gate, L0_ffn_w_up, L0_ffn_w_down, L0_ffn_sh_gate, L0_ffn_sh_up, L0_ffn_sh_down, L0_ffn_sh_gate_w, L0_c, L0_wmod):

    def _L0_attn_ref(hidden_states, Wq, bq, Wc, bc, Wk, bk, Wv, bv, Wlk, blk, Wlv, blv, qn_w, kn_w, sink_k, sink_v, Wo, bo):
        import jax, jax.numpy as jnp
        import numpy as np
        HID = 256
        NH = 16
        HD = 128
        R = 16
        WIN = 128
        ROPE = HD // 2
        EPS = 1e-06

        def rmsnorm(x, w):
            return x * jax.lax.rsqrt(jnp.mean(x * x, axis=-1, keepdims=True) + EPS) * w

        def apply_rope(x, pos):
            half = ROPE // 2
            inv_freq = 1.0 / 10000.0 ** (jnp.arange(half, dtype=jnp.float32) * 2.0 / ROPE)
            ang = pos.astype(jnp.float32)[:, None] * inv_freq[None, :]
            cos, sin = (jnp.cos(ang), jnp.sin(ang))
            x1, x2, rest = (x[..., :half], x[..., half:ROPE], x[..., ROPE:])
            return jnp.concatenate([x1 * cos - x2 * sin, x1 * sin + x2 * cos, rest], axis=-1)
        B, S, _ = hidden_states.shape
        pos = jnp.arange(S)
        scale = 1.0 / jnp.sqrt(jnp.float32(HD))
        q = (hidden_states @ Wq + bq).reshape(B, S, NH, HD).transpose(0, 2, 1, 3)
        q = apply_rope(rmsnorm(q, qn_w), pos)
        C = S // R
        w = jax.nn.softmax((hidden_states @ Wc + bc).reshape(B, C, R), axis=-1)
        entries = jnp.einsum('bcr,bcrh->bch', w, hidden_states.reshape(B, C, R, HID))
        block_ends = jnp.arange(C) * R + (R - 1)
        ck = apply_rope(rmsnorm(entries @ Wk + bk, kn_w), block_ends)
        cv = entries @ Wv + bv
        cs = jnp.einsum('bhsd,bcd->bhsc', q, ck) * scale
        cmask = block_ends[None, :] <= pos[:, None]
        cs = jnp.where(cmask, cs, -1000000000.0)
        sink_s = jnp.einsum('bhsd,hd->bhs', q, sink_k) * scale
        attn = jax.nn.softmax(jnp.concatenate([cs, sink_s[..., None]], axis=-1), axis=-1)
        ctx_c = jnp.einsum('bhsc,bcd->bhsd', attn[..., :C], cv) + attn[..., C:] * sink_v[None, :, None, :]
        lk = (hidden_states @ Wlk + blk).reshape(B, S, NH, HD).transpose(0, 2, 1, 3)
        lk = apply_rope(rmsnorm(lk, kn_w), pos)
        lv = (hidden_states @ Wlv + blv).reshape(B, S, NH, HD).transpose(0, 2, 1, 3)
        ls = jnp.einsum('bhsd,bhtd->bhst', q, lk) * scale
        d = pos[:, None] - pos[None, :]
        lmask = (d >= 0) & (d <= WIN)
        lattn = jax.nn.softmax(jnp.where(lmask, ls, -1000000000.0), axis=-1)
        ctx_l = jnp.einsum('bhst,bhtd->bhsd', lattn, lv)
        merged = 0.5 * (ctx_c + ctx_l)
        out = merged.transpose(0, 2, 1, 3).reshape(B, S, NH * HD) @ Wo + bo
        return out

    def _L0_ffn_ref(hidden_states, router_w, w_gate, w_up, w_down, sh_gate, sh_up, sh_down, sh_gate_w):
        import jax, jax.numpy as jnp
        import numpy as np
        B, S, H = (2, 256, 256)
        E, K = (16, 4)
        I_MOE, I_SH = (176, 704)
        orig = hidden_states.shape
        h = hidden_states.reshape(-1, orig[-1])
        N = h.shape[0]
        logits = h @ router_w.T
        probs = jax.nn.softmax(logits.astype(jnp.float32), axis=-1)
        top_vals, top_idx = jax.lax.top_k(probs, K)
        top_vals = top_vals / jnp.maximum(top_vals.sum(-1, keepdims=True), 1e-09)
        top_vals = top_vals.astype(h.dtype)
        comb = jnp.zeros((N, E), h.dtype).at[jnp.arange(N)[:, None], top_idx].add(top_vals)
        g = jnp.einsum('nh,ehi->eni', h, w_gate)
        u = jnp.einsum('nh,ehi->eni', h, w_up)
        y = jnp.einsum('eni,eih->enh', jax.nn.silu(g) * u, w_down)
        routed = jnp.einsum('enh,ne->nh', y, comb)
        shared = jax.nn.silu(h @ sh_gate) * (h @ sh_up) @ sh_down
        sg = jax.nn.sigmoid(h @ sh_gate_w)
        return (routed + sg * shared).reshape(orig)
    x = L0_attn_hidden_states
    mod = (_silu(L0_c) @ L0_wmod).reshape(L0_c.shape[0], 6, 1, -1)
    sa, ca, ga, sb, cb, gb = (mod[:, 0], mod[:, 1], mod[:, 2], mod[:, 3], mod[:, 4], mod[:, 5])
    ga = (2 * (ga >= 0) - 1) * jnp.maximum(jnp.abs(ga), 0.25)
    gb = (2 * (gb >= 0) - 1) * jnp.maximum(jnp.abs(gb), 0.25)
    h = _layernorm(x, axis=-1) * (1 + ca) + sa
    x = x + ga * _L0_attn_ref(h, L0_attn_Wq, L0_attn_bq, L0_attn_Wc, L0_attn_bc, L0_attn_Wk, L0_attn_bk, L0_attn_Wv, L0_attn_bv, L0_attn_Wlk, L0_attn_blk, L0_attn_Wlv, L0_attn_blv, L0_attn_qn_w, L0_attn_kn_w, L0_attn_sink_k, L0_attn_sink_v, L0_attn_Wo, L0_attn_bo)
    h = _layernorm(x, axis=-1) * (1 + cb) + sb
    x = x + gb * _L0_ffn_ref(h, L0_ffn_router_w, L0_ffn_w_gate, L0_ffn_w_up, L0_ffn_w_down, L0_ffn_sh_gate, L0_ffn_sh_up, L0_ffn_sh_down, L0_ffn_sh_gate_w)
    return x

_drawn_inputs = setup_inputs


def setup_inputs(seed=0):
    import zlib

    import numpy as np

    out = dict(_drawn_inputs(seed))
    spreads = {'L0_attn_bq': (0.0, 0.8),
     'L0_attn_bk': (0.0, 0.8),
     'L0_attn_bv': (0.0, 0.655),
     'L0_attn_blk': (0.0, 0.8),
     'L0_attn_blv': (0.0, 0.622),
     'L0_attn_qn_w': (1.0, 0.6),
     'L0_attn_kn_w': (1.0, 0.6),
     'L0_attn_bo': (0.0, 0.317)}
    factors = {'L0_attn_Wq': 8.0,
     'L0_attn_Wc': 8.0,
     'L0_attn_Wk': 8.0,
     'L0_attn_Wv': 8.0,
     'L0_attn_Wlk': 8.0,
     'L0_attn_Wlv': 8.0,
     'L0_attn_sink_k': 64.0,
     'L0_attn_sink_v': 64.0,
     'L0_attn_Wo': 3.093}
    for name, (base, spread) in spreads.items():
        noise = np.random.default_rng([zlib.crc32(name.encode()), seed]).standard_normal(out[name].shape)
        drawn = base * np.exp(spread * noise) if base else spread * noise
        out[name] = jnp.asarray(drawn.astype(out[name].dtype))
    for name, factor in factors.items():
        out[name] = (out[name] * factor).astype(out[name].dtype)
    return out
```

```python
from contextlib import ExitStack

import numpy as np

import concourse.bass as bass
from concourse import mybir

P = 128
S = 2048
HID = 256
KH = HID // P
NH = 16
HD = 128
NT = S // P
HG = 4
NG = NH // HG
NU = NG * NT
GW = HG * HD
R = 16
C = S // R
WIN = 128
ROPE = HD // 2
HALF = ROPE // 2
EPS_RMS = 1e-6
EPS_LN = 1e-5
MASKED = -1e30
E = 16
TOPK = 4
I_MOE = 176
I_SH = 704
NF = -(-(E * I_MOE + I_SH) // P)
FW = NF * P
EG = E + 1
PADK = TOPK
NC4 = S // 512
LW = 2 * P + C

F32 = mybir.dt.float32
BF16 = mybir.dt.bfloat16
ALU = mybir.AluOpType
ACT = mybir.ActivationFunctionType
AX = mybir.AxisListType.X


def bc(ap, dim, n):
    ap = ap.unsqueeze(dim)
    shape = list(ap.shape)
    shape[dim] = n
    return ap.to_broadcast(shape)


def build(nc, d):
    with ExitStack() as ctx:
        def sb(name, shape, dt=F32, stack=ctx):
            return stack.enter_context(nc.sbuf_tensor(name, shape, dt))

        def sem(name, stack=ctx):
            return stack.enter_context(nc.semaphore(name))

        psum = ctx.enter_context(nc.psum_tensor("psum", [P, 8, 512], F32))

        ident = sb("ident", [P, P])
        mod = sb("mod", [P, 6, HID])
        x_acc = sb("x_acc", [P, NT, HID])
        hT = sb("hT", [P, KH, S])
        out_bias = sb("out_bias", [P, HID])
        sink_out = sb("sink_out", [NH, HID])
        sink_prob = sb("sink_prob", [P, NT, NH])
        half_const = sb("half_const", [P, 32])
        stats = sb("stats", [P, NT, 6])
        ln_mean = sb("ln_mean", [P, NT])
        ln_rstd = sb("ln_rstd", [P, NT])
        ln_tmp = sb("ln_tmp", [P, 3, NT])
        h_tok = sb("h_tok", [P, 2, HID])

        def layer_norm_stats_small(chain, stats_all):
            dv = nc.vector
            me, m2e, mo, m2o = (stats[:, :, c] for c in (1, 2, 4, 5))
            a, b, v = (ln_tmp[:, c, :] for c in range(3))
            stats_all()
            chain(dv.tensor_tensor(a, me, mo, ALU.add))
            chain(dv.tensor_scalar(ln_mean[:], a, 0.5, None, ALU.mult))
            chain(dv.tensor_tensor(b, me, mo, ALU.subtract))
            chain(dv.tensor_tensor(b, b, b, ALU.mult))
            chain(dv.tensor_scalar(b, b, 0.25, EPS_LN, ALU.mult, ALU.add))
            chain(dv.tensor_tensor(a, m2e, m2o, ALU.add))
            return dv.scalar_tensor_tensor(v, a, 1.0 / HID, b, ALU.mult, ALU.add)

        def chain_on(eng, s):
            n = [0]

            def link(ins):
                n[0] += 1
                ins.then_inc(s, 1)
                eng.wait_ge(s, n[0])
            return link

        att = ctx.enter_context(ExitStack())

        w_qkv = sb("w_qkv", [P, 3, KH, NH * HD], stack=att)
        w_o = sb("w_o", [P, NH, HID], stack=att)
        bias_qk = sb("bias_qk", [P, NG, 2 * GW], stack=att)
        rope_same = sb("rope_same", [P, NT, 2, HD], stack=att)
        rope_swap = sb("rope_swap", [P, NT, 2, ROPE], stack=att)
        masks = sb("masks", [P, NT, LW], BF16, stack=att)
        ident_b = sb("ident_b", [P, P], BF16, stack=att)
        ckT = sb("ckT", [P, C], stack=att)
        cv = sb("cv", [P, HD], stack=att)
        sink_kT = sb("sink_kT", [P, NH], stack=att)
        k_ring = sb("k_ring", [P, HG, 2 * P], stack=att)
        v_ring = sb("v_ring", [P, 2, GW], stack=att)

        with ExitStack() as pre:
            cT = sb("cT", [P, KH], stack=pre)
            c_tmp = sb("c_tmp", [P, 3, KH], stack=pre)
            c_rep = sb("c_rep", [P, KH, P], stack=pre)
            w_mod = sb("w_mod", [P, KH, 6 * HID], stack=pre)
            gate_tmp = sb("gate_tmp", [P, 2, HID], stack=pre)
            wcT = sb("wcT", [P, KH], stack=pre)
            wc_rep = sb("wc_rep", [P, KH, P], stack=pre)
            b_c = sb("b_c", [P, 1], stack=pre)
            w_kv = sb("w_kv", [P, 2, KH, HD], stack=pre)
            rows = sb("rows", [P, 4, HD], stack=pre)
            trig = sb("trig", [P, NT + 1, 3, HALF], stack=pre)
            sink_vT = sb("sink_vT", [P, NH], stack=pre)
            blvT = sb("blvT", [P, NH], stack=pre)
            sv_diag = sb("sv_diag", [P, NH * NH], stack=pre)
            spare = bias_qk[:].rearrange("p g n -> p (g n)")
            blv_rep = spare[:, 0:NH * P].rearrange("p (h t) -> p h t", h=NH)
            bo_row = sb("bo_row", [P, HID], stack=pre)
            pool_w = spare[:, NH * P:NH * P + S].rearrange("p (c r) -> p c r", r=R)
            pool_m = sb("pool_m", [P, 2, C], stack=pre)
            entT = sb("entT", [P, KH, C], stack=pre)
            ck = sb("ck", [P, 2, HD], stack=pre)
            ck_t = sb("ck_t", [P, 4], stack=pre)
            ck_r = sb("ck_r", [P, 4, HALF], stack=pre)

            c_in = sem("c_in", pre)
            x_in = sem("x_in", pre)
            tables_in = sem("tables_in", pre)
            wo_in = sem("wo_in", pre)
            late_in = sem("late_in", pre)
            exp_c = sem("exp_c", pre)
            c_spread = sem("c_spread", pre)
            mod_done = sem("mod_done", pre)
            mod_raw = sem("mod_raw", pre)
            dve_step = sem("dve_step", pre)
            stats_done = sem("stats_done", pre)
            var_done = sem("var_done", pre)
            rstd_done = sem("rstd_done", pre)
            pool_const = sem("pool_const", pre)
            pool_step = sem("pool_step", pre)
            norm_step = sem("norm_step", pre)
            h_ready = sem("h_ready", pre)
            h_turned = sem("h_turned", pre)
            hT_ready = sem("hT_ready", pre)
            wc_ready = sem("wc_ready", pre)
            logits_done = sem("logits_done", pre)
            shifted = sem("shifted", pre)
            exp_pool = sem("exp_pool", pre)
            ent_ready = sem("ent_ready", pre)
            kv_done = sem("kv_done", pre)
            ck_biased = sem("ck_biased", pre)
            ck_ss = sem("ck_ss", pre)
            ck_var = sem("ck_var", pre)
            ck_rstd = sem("ck_rstd", pre)
            ck_ready = sem("ck_ready", pre)
            ck_turned = sem("ck_turned", pre)
            ckT_ready = sem("ckT_ready", pre)
            wo_ready = sem("wo_ready", pre)
            sink_done = sem("sink_done", pre)
            bias_done = sem("bias_done", pre)
            evac = sem("evac", pre)
            zeroed = sem("zeroed", pre)

            with nc.Block() as block:
                @block.sync
                def _(sp):
                    sp.dma_start(cT[:], d["cT"]).then_inc(c_in, 16)
                    sp.dma_start(w_mod[:], d["wmod"].rearrange("(k p) n -> p k n", p=P)).then_inc(c_in, 16)
                    sp.dma_start(x_acc[:], d["x"].rearrange("(t p) n -> p t n", p=P)).then_inc(x_in, 16)
                    sp.dma_start(ident[:], d["ident"]).then_inc(x_in, 16)
                    sp.dma_start(w_o[:], d["Wo"].rearrange("(h p) n -> p h n", p=P)).then_inc(wo_in, 16)
                    sp.dma_start(sink_vT[:], d["sink_vT"]).then_inc(wo_in, 16)
                    sp.dma_start(blvT[:], d["blvT"]).then_inc(wo_in, 16)
                    sp.dma_start(bo_row[:], d["bo"].partition_broadcast(P)).then_inc(wo_in, 16)
                    for m, name in enumerate(("Wq", "Wlk", "Wlv")):
                        sp.dma_start(w_qkv[:, m, :, :], d[name].rearrange("(k p) n -> p k n", p=P)).then_inc(late_in, 16)
                    sp.dma_start(masks[:], d["masks"]).then_inc(late_in, 16)
                    sp.dma_start(ident_b[:], d["ident_b"]).then_inc(late_in, 16)
                    sp.dma_start(sink_kT[:], d["sink_kT"]).then_inc(late_in, 16)
                    sp.wait_ge(late_in, 16 * 6)

                @block.scalar
                def _(act):
                    act.dma_start(wcT[:], d["wcT"]).then_inc(tables_in, 16)
                    act.dma_start(b_c[:], d["bc"].partition_broadcast(P)).then_inc(tables_in, 16)
                    act.dma_start(w_kv[:, 0, :, :], d["Wk"].rearrange("(k p) n -> p k n", p=P)).then_inc(tables_in, 16)
                    act.dma_start(w_kv[:, 1, :, :], d["Wv"].rearrange("(k p) n -> p k n", p=P)).then_inc(tables_in, 16)
                    act.dma_start(rows[:], d["rows"].partition_broadcast(P)).then_inc(tables_in, 16)
                    act.dma_start(trig[:], d["trig"]).then_inc(tables_in, 16)
                    act.wait_ge(c_in, 32)
                    nc.scalar.activation(c_tmp[:, 0, :], cT[:], ACT.Exp, scale=-1.0).then_inc(exp_c, 1)
                    def pair(j):
                        for par in range(2):
                            act.wait_ge(h_turned, 2 * j + par + 1)
                            nc.scalar.copy(hT[:, :, bass.ds((2 * j + par) * P, P)],
                                           psum[:, 4 + par, 0:2 * P].rearrange("p (k t) -> p k t", k=KH)).then_inc(hT_ready, 1)
                    pair(0)
                    with act.Fori(1, NT // 2) as j:
                        pair(j)
                    act.wait_ge(shifted, 1)
                    nc.scalar.activation(pool_w, pool_w, ACT.Exp).then_inc(exp_pool, 1)
                    act.wait_ge(ck_biased, 1)
                    nc.scalar.activation(ck[:, 1, :], ck[:, 0, :], ACT.Square, accum_out=ck_t[:, 0:1]).then_inc(ck_ss, 1)
                    act.wait_ge(ck_turned, 1)
                    nc.scalar.copy(ckT[:], psum[:, 6, 0:C]).then_inc(ckT_ready, 1)

                @block.tensor
                def _(pe):
                    pe.wait_ge(c_spread, 1)
                    for n in range(3):
                        for k in range(KH):
                            last = nc.tensor.matmul(psum[:, n, :], c_rep[:, k, :], w_mod[:, k, n * 512:(n + 1) * 512],
                                                    start=(k == 0), stop=(k == KH - 1))
                    last.then_inc(mod_done, 1)
                    pe.wait_ge(x_in, 32)
                    def pair(j):
                        for par in range(2):
                            pe.wait_ge(h_ready, 2 * j + par + 1)
                            pe.wait_ge(hT_ready, 2 * j + 0)
                            for k in range(KH):
                                last = nc.tensor.transpose(psum[:, 4 + par, k * P:(k + 1) * P], h_tok[:, par, k * P:(k + 1) * P], ident[:])
                            last.then_inc(h_turned, 1)
                    pair(0)
                    with pe.Fori(1, NT // 2) as j:
                        pair(j)
                    pe.wait_ge(hT_ready, NT)
                    pe.wait_ge(wc_ready, 1)
                    pe.wait_ge(mod_raw, 1)
                    for n in range(4):
                        for k in range(KH):
                            last = nc.tensor.matmul(psum[:, n, :], wc_rep[:, k, :], hT[:, k, n * 512:(n + 1) * 512],
                                                    start=(k == 0), stop=(k == KH - 1))
                    last.then_inc(logits_done, 1)
                    pe.wait_ge(wo_ready, 1)
                    for h in range(NH):
                        last = nc.tensor.matmul(psum[0:NH, 4, 0:HID], sv_diag[:, h * NH:(h + 1) * NH], w_o[:, h, :],
                                                start=(h == 0), stop=(h == NH - 1))
                    last.then_inc(sink_done, 1)
                    for h in range(NH):
                        last = nc.tensor.matmul(psum[:, 5, 0:HID], blv_rep[:, h, :], w_o[:, h, :],
                                                start=(h == 0), stop=(h == NH - 1))
                    last.then_inc(bias_done, 1)
                    pe.wait_ge(ent_ready, 1)
                    for m in range(2):
                        for k in range(KH):
                            last = nc.tensor.matmul(psum[:, 6 + m, 0:HD], entT[:, k, :], w_kv[:, m, k, :],
                                                    start=(k == 0), stop=(k == KH - 1))
                    last.then_inc(kv_done, 1)
                    pe.wait_ge(ck_ready, 1)
                    nc.tensor.transpose(psum[:, 6, 0:C], ck[:, 1, :], ident[:]).then_inc(ck_turned, 1)

                @block.gpsimd
                def _(pool):
                    g = nc.gpsimd
                    g.memset(half_const[:], -0.5).then_inc(pool_const, 1)
                    g.memset(k_ring[:], 0.0).then_inc(zeroed, 1)
                    g.memset(v_ring[:], 0.0).then_inc(zeroed, 1)
                    pool.wait_ge(tables_in, 96)
                    cos, sin, nsin = (trig[:, 0:NT, c, :] for c in range(3))
                    for m in range(2):
                        w1, w2 = rows[:, 2 + m, 0:HALF], rows[:, 2 + m, HALF:ROPE]
                        g.tensor_tensor(rope_same[:, :, m, 0:HALF], cos, bc(w1, 1, NT), ALU.mult)
                        g.tensor_tensor(rope_same[:, :, m, HALF:ROPE], cos, bc(w2, 1, NT), ALU.mult)
                        g.tensor_copy(rope_same[:, :, m, ROPE:HD], bc(rows[:, 2 + m, ROPE:HD], 1, NT))
                        g.tensor_tensor(rope_swap[:, :, m, 0:HALF], nsin, bc(w2, 1, NT), ALU.mult)
                        g.tensor_tensor(rope_swap[:, :, m, HALF:ROPE], sin, bc(w1, 1, NT), ALU.mult).then_inc(zeroed, 1)
                    pool.wait_ge(pool_const, 1)
                    pool.wait_ge(var_done, 1)
                    g.tensor_tensor(ln_rstd[:], ln_tmp[:, 2, :], half_const[:, 0:NT], ALU.pow).then_inc(rstd_done, 1)
                    pool.wait_ge(ck_var, 1)
                    g.tensor_tensor(ck_t[:, 2:3], ck_t[:, 1:2], half_const[:, 0:1], ALU.pow).then_inc(ck_rstd, 1)

                @block.vector
                def _(dve):
                    v = nc.vector
                    link = chain_on(dve, dve_step)
                    dve.wait_ge(exp_c, 1)
                    link(v.tensor_scalar(c_tmp[:, 1, :], c_tmp[:, 0, :], 1.0, None, ALU.add))
                    link(v.reciprocal(c_tmp[:, 2, :], c_tmp[:, 1, :]))
                    link(v.tensor_tensor(c_tmp[:, 1, :], cT[:], c_tmp[:, 2, :], ALU.mult))
                    v.tensor_copy(c_rep[:], bc(c_tmp[:, 1, :], 2, P)).then_inc(c_spread, 1)
                    dve.wait_ge(tables_in, 96)
                    v.tensor_copy(wc_rep[:], bc(wcT[:], 2, P)).then_inc(wc_ready, 1)
                    dve.wait_ge(x_in, 32)
                    def tile(i):
                        v.bn_stats(stats[:, i, :], x_acc[:, i, :]).then_inc(stats_done, 1)
                    tile(0)
                    with dve.Fori(1, NT) as i:
                        tile(i)
                    layer_norm_stats_small(link, lambda: dve.wait_ge(stats_done, NT)).then_inc(var_done, 1)
                    dve.wait_ge(mod_done, 1)
                    v.tensor_copy(mod[:].rearrange("p a b -> p (a b)"), psum[:, 0:3, :].rearrange("p a b -> p (a b)")).then_inc(mod_raw, 1)
                    dve.wait_ge(mod_raw, 1)
                    for scale_row, gate_row in ((1, 2), (4, 5)):
                        link(v.tensor_scalar(mod[:, scale_row, :], mod[:, scale_row, :], 1.0, None, ALU.add))
                        gate = mod[:, gate_row, :]
                        link(v.tensor_scalar(gate_tmp[:, 0, :], gate, 0.0, 2.0, ALU.is_ge, ALU.mult))
                        link(v.scalar_tensor_tensor(gate_tmp[:, 1, :], gate, -1.0, gate, ALU.mult, ALU.max))
                        link(v.tensor_scalar(gate_tmp[:, 1, :], gate_tmp[:, 1, :], 0.25, None, ALU.max))
                        link(v.scalar_tensor_tensor(gate, gate_tmp[:, 0, :], -1.0, gate_tmp[:, 1, :], ALU.add, ALU.mult))
                    dve.wait_ge(rstd_done, 1)
                    def pair(j):
                        for par in range(2):
                            i = 2 * j + par
                            h = h_tok[:, par, :]
                            dve.wait_ge(h_turned, 2 * j + 0)
                            v.tensor_scalar(h, x_acc[:, i, :], ln_mean[:, bass.ds(i, 1)], ln_rstd[:, bass.ds(i, 1)],
                                            ALU.subtract, ALU.mult).then_inc(norm_step, 1)
                            dve.wait_ge(norm_step, 4 * j + 2 * par + 1)
                            v.tensor_tensor(h, h, mod[:, 1, :], ALU.mult).then_inc(norm_step, 1)
                            dve.wait_ge(norm_step, 4 * j + 2 * par + 2)
                            v.tensor_tensor(h, h, mod[:, 0, :], ALU.add).then_inc(h_ready, 1)
                    pair(0)
                    with dve.Fori(1, NT // 2) as j:
                        pair(j)
                    dve.wait_ge(wo_in, 64)
                    link(v.memset(sv_diag[:], 0.0))
                    link(v.tensor_copy(sv_diag[:, 0:NH * NH:NH + 1], sink_vT[:]))
                    link(v.tensor_copy(blv_rep, bc(blvT[:], 2, P)))
                    v.tensor_tensor(w_o[:], w_o[:], bc(mod[:, 2, :], 1, NH), ALU.mult).then_inc(wo_ready, 1)
                    link(v.tensor_tensor(bo_row[:], bo_row[:], mod[:, 2, :], ALU.mult))
                    dve.wait_ge(logits_done, 1)
                    link(v.tensor_scalar(pool_w.rearrange("p c r -> p (c r)"), psum[:, 0:4, :].rearrange("p a b -> p (a b)"),
                                         b_c[:, 0:1], None, ALU.add))
                    link(v.tensor_reduce(pool_m[:, 0, :], pool_w, AX, ALU.max))
                    v.tensor_tensor(pool_w, pool_w, bc(pool_m[:, 0, :], 2, R), ALU.subtract).then_inc(shifted, 1)
                    dve.wait_ge(sink_done, 1)
                    v.tensor_copy(sink_out[:], psum[0:NH, 4, 0:HID]).then_inc(evac, 1)
                    dve.wait_ge(bias_done, 1)
                    v.scalar_tensor_tensor(out_bias[:], psum[:, 5, 0:HID], 0.5, bo_row[:], ALU.mult, ALU.add).then_inc(evac, 1)
                    dve.wait_ge(exp_pool, 1)
                    link(v.tensor_reduce(pool_m[:, 0, :], pool_w, AX, ALU.add))
                    link(v.reciprocal(pool_m[:, 1, :], pool_m[:, 0, :]))
                    link(v.tensor_tensor(pool_w, pool_w, bc(pool_m[:, 1, :], 2, R), ALU.mult))
                    dve.wait_ge(hT_ready, NT)
                    prod = w_mod[:].rearrange("p k n -> p (k n)")[:, 0:S].rearrange("p (c r) -> p c r", r=R)
                    for k in range(KH):
                        link(v.tensor_tensor(prod, hT[:, k, :].rearrange("p (c r) -> p c r", r=R), pool_w, ALU.mult))
                        ins = v.tensor_reduce(entT[:, k, :], prod, AX, ALU.add)
                        if k < KH - 1:
                            link(ins)
                    ins.then_inc(ent_ready, 1)
                    dve.wait_ge(kv_done, 1)
                    v.tensor_tensor(ck[:, 0, :], psum[:, 6, 0:HD], rows[:, 0, :], ALU.add).then_inc(ck_biased, 1)
                    v.tensor_tensor(cv[:], psum[:, 7, 0:HD], rows[:, 1, :], ALU.add).then_inc(evac, 1)
                    dve.wait_ge(ck_ss, 1)
                    v.tensor_scalar(ck_t[:, 1:2], ck_t[:, 0:1], 1.0 / HD, EPS_RMS, ALU.mult, ALU.add).then_inc(ck_var, 1)
                    dve.wait_ge(ck_rstd, 1)
                    dve.wait_ge(ck_biased, 1)
                    link(v.scalar_tensor_tensor(ck[:, 0, :], ck[:, 0, :], ck_t[:, 2:3], rows[:, 3, :], ALU.mult, ALU.mult))
                    x1, x2 = ck[:, 0, 0:HALF], ck[:, 0, HALF:ROPE]
                    cos, sin = trig[:, NT, 0, :], trig[:, NT, 1, :]
                    link(v.tensor_tensor(ck_r[:, 0, :], x1, cos, ALU.mult))
                    link(v.tensor_tensor(ck_r[:, 1, :], x2, sin, ALU.mult))
                    link(v.tensor_tensor(ck_r[:, 2, :], x1, sin, ALU.mult))
                    link(v.tensor_tensor(ck_r[:, 3, :], x2, cos, ALU.mult))
                    link(v.tensor_tensor(ck[:, 1, 0:HALF], ck_r[:, 0, :], ck_r[:, 1, :], ALU.subtract))
                    link(v.tensor_tensor(ck[:, 1, HALF:ROPE], ck_r[:, 2, :], ck_r[:, 3, :], ALU.add))
                    v.tensor_copy(ck[:, 1, ROPE:HD], ck[:, 0, ROPE:HD]).then_inc(ck_ready, 1)

        with ExitStack() as un:
            qk_tok = sb("qk_tok", [P, 2, HG, HD], stack=un)
            qk_sq = sb("qk_sq", [P, 2, HG, HD], stack=un)
            qk_rot = sb("qk_rot", [P, 2, HG, HD], stack=un)
            qk_swp = sb("qk_swp", [P, 2, HG, ROPE], stack=un)
            ms = sb("ms", [P, 2, HG], stack=un)
            ms_eps = sb("ms_eps", [P, 2, HG], stack=un)
            rstd = sb("rstd", [P, 2, HG], stack=un)
            qT = sb("qT", [P, HG, P], stack=un)
            v_new = sb("v_new", [P, GW], stack=un)
            h_now = sb("h_now", [P, KH, P], stack=un)
            mx = sb("mx", [P, 2, HG], stack=un)
            nmx = sb("nmx", [P, 2, HG], stack=un)
            sink_d = sb("sink_d", [P, 3, HG], stack=un)
            sums = sb("sums", [P, 2, HG], stack=un)
            inv = sb("inv", [P, 2, HG], stack=un)
            prob = sb("prob", [P, HG, LW], stack=un)
            probT = sb("probT", [P, 3, HG, P], stack=un)
            ctxT = sb("ctxT", [P, HG, P], stack=un)

            names = ("h_copied qk_projected v_projected qk_biased qk_squared ms_summed ms_ready rstd_ready swap_ready rot_q rot_added "
                     "rot_ready qk_turned qk_ready v_out v_placed scored max_done max_sink max_ready nmax_ready sinkd_ready exps_done sink_exp "
                     "sums_ready inv_done inv_ready prob_ready p_turned p_ready ctx_done ctx_ready out_done acc_done")
            s = {n: sem(n, un) for n in names.split()}

            Q_BANK, V_BANK, L_BANK, C_BANK, SINK_BANK, T_BANK = 0, 2, 3, 5, 7, 6
            t_banks = (T_BANK, 0, 1)

            def tile_of(u):
                return u & (NT - 1) if not isinstance(u, int) else u % NT

            def group_of(u):
                return (u >> 4) & (NG - 1)

            def par_of(u):
                return u & 1

            bias_in = sem("bias_in", un)
            with nc.Block() as block:
                @block.sync
                def _(sp):
                    sp.dma_start(bias_qk[:], d["bias_qk"].partition_broadcast(P)).then_inc(bias_in, 16)

                @block.tensor
                def _(pe):
                    t = nc.tensor

                    def project(u):
                        pe.wait_ge(s["h_copied"], u + 1)
                        g = group_of(u)
                        for m in range(3):
                            if m == 2 and not (isinstance(u, int) and u == 0):
                                pe.wait_ge(s["acc_done"], u - 1)
                            for k in range(KH):
                                ins = t.matmul(psum[:, m, :], h_now[:, k, :], w_qkv[:, m, k, bass.ds(g * GW, GW)],
                                               start=(k == 0), stop=(k == KH - 1))
                            if m == 1:
                                ins.then_inc(s["qk_projected"], 1)
                        ins.then_inc(s["v_projected"], 1)

                    def turn_qk(u):
                        pe.wait_ge(s["rot_ready"], u + 1)
                        for m in range(2):
                            for h in range(HG):
                                ins = t.transpose(psum[:, m, h * P:(h + 1) * P], qk_rot[:, m, h, :], ident[:])
                        ins.then_inc(s["qk_turned"], 1)

                    def score(u):
                        pe.wait_ge(s["qk_ready"], 2 * u + 2)
                        pe.wait_ge(s["exps_done"], u)
                        i, g = tile_of(u), group_of(u)
                        for h in range(HG):
                            loc = psum[:, L_BANK + h // 2, (h % 2) * 2 * P:(h % 2 + 1) * 2 * P]
                            t.matmul(loc, ident_b[:], masks[:, i, 0:2 * P], start=True, stop=False)
                            t.matmul(loc, qT[:, h, :], k_ring[:, h, :], start=False, stop=True)
                        for h in range(HG):
                            cmp_ = psum[:, C_BANK, h * C:(h + 1) * C]
                            t.matmul(cmp_, ident_b[:], masks[:, i, 2 * P:LW], start=True, stop=False)
                            t.matmul(cmp_, qT[:, h, :], ckT[:], start=False, stop=True)
                        for h in range(HG):
                            ins = t.matmul(psum[:, SINK_BANK, h:h + 1], qT[:, h, :], sink_kT[:, bass.ds(g * HG + h, 1)],
                                           start=True, stop=True)
                        ins.then_inc(s["scored"], 1)

                    def turn_probs(u, nxt):
                        pe.wait_ge(s["prob_ready"], u + 1)
                        if nxt:
                            pe.wait_ge(s["qk_biased"], u + 2)
                        for c in range(3):
                            for h in range(HG):
                                ins = t.transpose(psum[:, t_banks[c], h * P:(h + 1) * P], prob[:, h, c * P:(c + 1) * P], ident[:])
                            ins.then_inc(s["p_turned"], 1)

                    def context(u, nxt):
                        pe.wait_ge(s["v_placed"], u + 1)
                        pe.wait_ge(s["p_ready"], 3 * u + 3)
                        if nxt:
                            pe.wait_ge(s["v_out"], u + 2)
                        t.matmul(psum[:, V_BANK, :], cv[:], probT[:, 2, :, :].rearrange("p h t -> p (h t)"), start=True, stop=True)
                        for h in range(HG):
                            for c in range(2):
                                ins = t.matmul(psum[:, V_BANK, h * P:(h + 1) * P], v_ring[:, c, h * HD:(h + 1) * HD], probT[:, c, h, :],
                                               start=False, stop=True, skip_group_check=True)
                        ins.then_inc(s["ctx_done"], 1)

                    def output(u):
                        g = group_of(u)
                        pe.wait_ge(s["ctx_ready"], u + 1)
                        for h in range(HG):
                            ins = t.matmul(psum[:, V_BANK, 0:HID], ctxT[:, h, :], w_o[:, g * HG + h, :], start=(h == 0), stop=(h == HG - 1))
                        ins.then_inc(s["out_done"], 1)

                    def step(u, nxt=True):
                        score(u)
                        if nxt:
                            project(u + 1)
                        turn_probs(u, nxt)
                        context(u, nxt)
                        if nxt:
                            turn_qk(u + 1)
                        output(u)

                    project(0)
                    turn_qk(0)
                    step(0)
                    with pe.Fori(1, NU - 1) as u:
                        step(u)
                    step(NU - 1, False)

                @block.scalar
                def _(act):
                    a = nc.scalar

                    def square(u):
                        act.wait_ge(s["qk_biased"], u + 1)
                        a.activation(qk_sq[:], qk_tok[:], ACT.Square).then_inc(s["qk_squared"], 1)

                    def v_evac(u):
                        act.wait_ge(s["v_projected"], u + 1)
                        act.wait_ge(s["v_placed"], u)
                        a.copy(v_new[:], psum[:, V_BANK, :]).then_inc(s["v_out"], 1)

                    def qk_evac(u):
                        act.wait_ge(s["qk_turned"], u + 1)
                        a.copy(qT[:].rearrange("p h t -> p (h t)"), psum[:, 0, :]).then_inc(s["qk_ready"], 1)
                        a.copy(k_ring[:, :, bass.ds(par_of(u) * P, P)], psum[:, 1, :].rearrange("p (h t) -> p h t", h=HG)).then_inc(s["qk_ready"], 1)

                    def exps(u):
                        act.wait_ge(s["nmax_ready"], u + 1)
                        act.wait_ge(s["p_turned"], 3 * u)
                        for c in range(2):
                            for h in range(HG):
                                if c == 0:
                                    src = psum[:, L_BANK + h // 2, (h % 2) * 2 * P:(h % 2 + 1) * 2 * P]
                                    dst = prob[:, h, 0:2 * P]
                                else:
                                    src, dst = psum[:, C_BANK, h * C:(h + 1) * C], prob[:, h, 2 * P:LW]
                                ins = a.activation(dst, src, ACT.Exp, bias=nmx[:, c, h:h + 1], scale=rstd[:, 0, h:h + 1],
                                                   accum_out=sums[:, c, h:h + 1])
                        ins.then_inc(s["exps_done"], 1)
                        act.wait_ge(s["sinkd_ready"], u + 1)
                        a.activation(sink_d[:, 2, :], sink_d[:, 1, :], ACT.Exp).then_inc(s["sink_exp"], 1)

                    def probs_evac(u):
                        for c in range(3):
                            act.wait_ge(s["p_turned"], 3 * u + c + 1)
                            a.copy(probT[:, c, :, :].rearrange("p h t -> p (h t)"), psum[:, t_banks[c], :]).then_inc(s["p_ready"], 1)

                    def ctx_evac(u):
                        act.wait_ge(s["ctx_done"], u + 1)
                        a.copy(ctxT[:].rearrange("p h t -> p (h t)"), psum[:, V_BANK, :]).then_inc(s["ctx_ready"], 1)

                    def step(u, nxt=True):
                        exps(u)
                        if nxt:
                            square(u + 1)
                            v_evac(u + 1)
                        probs_evac(u)
                        ctx_evac(u)
                        if nxt:
                            qk_evac(u + 1)

                    square(0)
                    v_evac(0)
                    qk_evac(0)
                    step(0)
                    with act.Fori(1, NU - 1) as u:
                        step(u)
                    step(NU - 1, False)

                @block.vector
                def _(dve):
                    v = nc.vector

                    def bias(u):
                        dve.wait_ge(s["qk_projected"], u + 1)
                        v.tensor_tensor(qk_tok[:].rearrange("p m h d -> p (m h d)"), psum[:, 0:2, :].rearrange("p a b -> p (a b)"),
                                        bias_qk[:, group_of(u), :], ALU.add).then_inc(s["qk_biased"], 1)

                    def rotate(u):
                        dve.wait_ge(s["qk_squared"], u + 1)
                        v.tensor_reduce(ms[:], qk_sq[:], AX, ALU.add).then_inc(s["ms_summed"], 1)
                        dve.wait_ge(s["ms_summed"], u + 1)
                        v.tensor_scalar(ms_eps[:, 0, :], ms[:, 0, :], 1.0, EPS_RMS * HD, ALU.mult, ALU.add)
                        v.tensor_scalar(ms_eps[:, 1, :], ms[:, 1, :], 1.0 / HD, EPS_RMS, ALU.mult, ALU.add).then_inc(s["ms_ready"], 1)
                        v.tensor_tensor(qk_rot[:], qk_tok[:], bc(rope_same[:, tile_of(u), :, :], 2, HG), ALU.mult).then_inc(s["rot_q"], 1)
                        dve.wait_ge(s["swap_ready"], u + 1)
                        dve.wait_ge(s["rot_q"], u + 1)
                        v.tensor_tensor(qk_rot[:, :, :, 0:ROPE], qk_rot[:, :, :, 0:ROPE], qk_swp[:], ALU.add).then_inc(s["rot_added"], 1)

                    def maxima(u):
                        dve.wait_ge(s["scored"], u + 1)
                        v.tensor_reduce(mx[:, 0, :], psum[:, L_BANK:L_BANK + 2, :].rearrange("p b (h t) -> p (b h) t", h=2), AX, ALU.max)
                        v.tensor_reduce(mx[:, 1, :], psum[:, C_BANK, :].rearrange("p (h t) -> p h t", h=HG), AX, ALU.max).then_inc(s["max_done"], 1)
                        dve.wait_ge(s["max_done"], u + 1)
                        v.tensor_tensor(mx[:, 1, :], mx[:, 1, :], psum[:, SINK_BANK, 0:HG], ALU.max).then_inc(s["max_sink"], 1)
                        dve.wait_ge(s["max_sink"], u + 1)
                        dve.wait_ge(s["rstd_ready"], u + 1)
                        v.scalar_tensor_tensor(nmx[:], mx[:], -1.0, bc(rstd[:, 0, :], 1, 2), ALU.mult, ALU.mult).then_inc(s["nmax_ready"], 1)
                        v.scalar_tensor_tensor(sink_d[:, 0, :], mx[:, 1, :], -1.0, psum[:, SINK_BANK, 0:HG], ALU.mult, ALU.add).then_inc(s["max_ready"], 1)
                        dve.wait_ge(s["max_ready"], u + 1)
                        v.tensor_tensor(sink_d[:, 1, :], sink_d[:, 0, :], rstd[:, 0, :], ALU.mult).then_inc(s["sinkd_ready"], 1)

                    def inverses(u):
                        dve.wait_ge(s["exps_done"], u + 1)
                        dve.wait_ge(s["sink_exp"], u + 1)
                        v.tensor_tensor(sums[:, 1, :], sums[:, 1, :], sink_d[:, 2, :], ALU.add).then_inc(s["sums_ready"], 1)
                        dve.wait_ge(s["sums_ready"], 3 * u + 1)
                        v.tensor_scalar(sums[:], sums[:], 2.0, None, ALU.mult).then_inc(s["sums_ready"], 1)
                        dve.wait_ge(s["sums_ready"], 3 * u + 2)
                        v.reciprocal(inv[:], sums[:]).then_inc(s["inv_ready"], 1)
                        dve.wait_ge(s["inv_ready"], u + 1)
                        v.tensor_tensor(sink_prob[:, tile_of(u), bass.ds(group_of(u) * HG, HG)], sink_d[:, 2, :], inv[:, 1, :], ALU.mult).then_inc(s["sums_ready"], 1)

                    def accumulate(u):
                        dve.wait_ge(s["out_done"], u + 1)
                        i = tile_of(u)
                        v.tensor_tensor(x_acc[:, i, :], x_acc[:, i, :], psum[:, V_BANK, 0:HID], ALU.add).then_inc(s["acc_done"], 1)

                    def step(u, nxt=True):
                        maxima(u)
                        if nxt:
                            bias(u + 1)
                        inverses(u)
                        if nxt:
                            rotate(u + 1)
                        accumulate(u)

                    dve.wait_ge(bias_in, 16)
                    bias(0)
                    rotate(0)
                    step(0)
                    with dve.Fori(1, NU - 1) as u:
                        step(u)
                    step(NU - 1, False)

                @block.gpsimd
                def _(pool):
                    g = nc.gpsimd

                    def copy_h(u):
                        pool.wait_ge(s["v_projected"], u)
                        g.tensor_copy(h_now[:], hT[:, :, bass.ds(tile_of(u) * P, P)]).then_inc(s["h_copied"], 1)

                    def normalise(u):
                        pool.wait_ge(s["inv_ready"], u + 1)
                        for c, (lo, hi) in enumerate(((0, 2 * P), (2 * P, LW))):
                            ins = g.tensor_tensor(prob[:, :, lo:hi], prob[:, :, lo:hi], bc(inv[:, c, :], 2, hi - lo), ALU.mult)
                        ins.then_inc(s["prob_ready"], 1)

                    def swap_parts(u):
                        pool.wait_ge(s["qk_biased"], u + 1)
                        i = tile_of(u)
                        for m in range(2):
                            g.tensor_tensor(qk_swp[:, m, :, 0:HALF], qk_tok[:, m, :, HALF:ROPE], bc(rope_swap[:, i, m, 0:HALF], 1, HG), ALU.mult)
                            ins = g.tensor_tensor(qk_swp[:, m, :, HALF:ROPE], qk_tok[:, m, :, 0:HALF], bc(rope_swap[:, i, m, HALF:ROPE], 1, HG), ALU.mult)
                        ins.then_inc(s["swap_ready"], 1)

                    def scale_k(u):
                        pool.wait_ge(s["ms_ready"], u + 1)
                        g.tensor_tensor(rstd[:], ms_eps[:], half_const[:, 0:2 * HG].rearrange("p (m h) -> p m h", m=2), ALU.pow).then_inc(s["rstd_ready"], 1)
                        pool.wait_ge(s["rot_added"], u + 1)
                        pool.wait_ge(s["rstd_ready"], u + 1)
                        g.tensor_tensor(qk_rot[:, 1, :, :], qk_rot[:, 1, :, :], bc(rstd[:, 1, :], 2, HD), ALU.mult).then_inc(s["rot_ready"], 1)

                    def place_v(u):
                        pool.wait_ge(s["v_out"], u + 1)
                        pool.wait_ge(s["ctx_done"], u)
                        g.tensor_copy(v_ring[:, par_of(u), :], v_new[:]).then_inc(s["v_placed"], 1)

                    def step(u, nxt=True):
                        if nxt:
                            copy_h(u + 1)
                        normalise(u)
                        if nxt:
                            swap_parts(u + 1)
                            scale_k(u + 1)
                            place_v(u + 1)

                    copy_h(0)
                    swap_parts(0)
                    scale_k(0)
                    place_v(0)
                    step(0)
                    with pool.Fori(1, NU - 1) as u:
                        step(u)
                    step(NU - 1, False)

        att.close()

        with ExitStack() as ff:
            w_gu = sb("w_gu", [P, 2, KH, FW], stack=ff)
            w_down = sb("w_down", [P, NF, HID], stack=ff)
            pick = sb("pick", [EG, FW], stack=ff)
            w_rt = sb("w_rt", [P, KH, EG], stack=ff)
            combT = sb("combT", [EG, S], stack=ff)
            w_gu_in = sem("w_gu_in", ff)
            w_down_in = sem("w_down_in", ff)
            rt_in = sem("rt_in", ff)
            with ExitStack() as rt:
                spT = sb("spT", [NH, S], stack=rt)
                lgT = sb("lgT", [EG, S], stack=rt)
                lg = sb("lg", [P, NT, EG], stack=rt)
                pr = sb("pr", [P, NT, E + PADK], stack=rt)
                rep = sb("rep", [P, NT, E + PADK], stack=rt)
                top = sb("top", [P, NT, 8], stack=rt)
                comb = sb("comb", [P, NT, EG], stack=rt)
                row_t = sb("row_t", [P, 4, NT], stack=rt)
                sp_turned = sem("sp_turned", rt)
                spT_ready = sem("spT_ready", rt)
                sink_added = sem("sink_added", rt)
                acc_step = sem("acc_step", rt)
                x1_ready = sem("x1_ready", rt)
                stats2 = sem("stats2", rt)
                var2 = sem("var2", rt)
                rstd2 = sem("rstd2", rt)
                step2 = sem("step2", rt)
                norm2 = sem("norm2", rt)
                h2_ready = sem("h2_ready", rt)
                h2_turned = sem("h2_turned", rt)
                h2T_ready = sem("h2T_ready", rt)
                lgT_done = sem("lgT_done", rt)
                lgT_ready = sem("lgT_ready", rt)
                lg_turned = sem("lg_turned", rt)
                lg_shifted = sem("lg_shifted", rt)
                lg_exp = sem("lg_exp", rt)
                comb_ready = sem("comb_ready", rt)
                comb_turned = sem("comb_turned", rt)
                combT_ready = sem("combT_ready", rt)
                with nc.Block() as block:
                    @block.sync
                    def _(sp):
                        sp.dma_start(w_rt[:], d["w_rt"].rearrange("(k p) n -> p k n", p=P)).then_inc(rt_in, 16)
                        for m, name in enumerate(("w_gate", "w_up")):
                            sp.dma_start(w_gu[:, m, :, :], d[name].rearrange("(k p) n -> p k n", p=P)).then_inc(w_gu_in, 16)
                        sp.dma_start(pick[:], d["pick"]).then_inc(w_gu_in, 16)
                        sp.dma_start(w_down[:], d["w_down"].rearrange("(j p) n -> p j n", p=P)).then_inc(w_down_in, 16)

                    @block.tensor
                    def _(pe):
                        t = nc.tensor
                        for i in range(NT):
                            ins = t.transpose(psum[0:NH, i // 4, (i % 4) * P:(i % 4 + 1) * P], sink_prob[:, i, :], ident[:])
                        ins.then_inc(sp_turned, 1)
                        pe.wait_ge(spT_ready, 1)
                        for i in range(NT):
                            if i >= 2:
                                pe.wait_ge(sink_added, i - 1)
                            t.matmul(psum[:, 4 + i % 2, 0:HID], spT[:, i * P:(i + 1) * P], sink_out[:], start=True, stop=True).then_inc(acc_step, 1)
                        def pair(j):
                            for par in range(2):
                                pe.wait_ge(h2_ready, 2 * j + par + 1)
                                pe.wait_ge(h2T_ready, 2 * j + 0)
                                for k in range(KH):
                                    ins = t.transpose(psum[:, 6 + par, k * P:(k + 1) * P], h_tok[:, par, k * P:(k + 1) * P], ident[:])
                                ins.then_inc(h2_turned, 1)
                        pair(0)
                        with pe.Fori(1, NT // 2) as j:
                            pair(j)
                        pe.wait_ge(h2T_ready, NT)
                        pe.wait_ge(rt_in, 16)
                        for n in range(NC4):
                            for k in range(KH):
                                ins = t.matmul(psum[0:EG, n, :], w_rt[:, k, :], hT[:, k, n * 512:(n + 1) * 512], start=(k == 0), stop=(k == KH - 1))
                        ins.then_inc(lgT_done, 1)
                        pe.wait_ge(lgT_ready, 1)
                        for i in range(NT):
                            ins = t.transpose(psum[:, 4, i * 32:i * 32 + EG], lgT[:, i * P:(i + 1) * P], ident[0:EG, 0:EG])
                        ins.then_inc(lg_turned, 1)
                        pe.wait_ge(comb_ready, 1)
                        for i in range(NT):
                            ins = t.transpose(psum[0:EG, i // 4, (i % 4) * P:(i % 4 + 1) * P], comb[:, i, :], ident[:])
                        ins.then_inc(comb_turned, 1)

                    @block.scalar
                    def _(act):
                        a = nc.scalar
                        act.wait_ge(sp_turned, 1)
                        a.copy(spT[:], psum[0:NH, 0:4, :].rearrange("p a b -> p (a b)")).then_inc(spT_ready, 1)
                        def pair(j):
                            for par in range(2):
                                act.wait_ge(h2_turned, 2 * j + par + 1)
                                a.copy(hT[:, :, bass.ds((2 * j + par) * P, P)],
                                       psum[:, 6 + par, 0:2 * P].rearrange("p (k t) -> p k t", k=KH)).then_inc(h2T_ready, 1)
                        pair(0)
                        with act.Fori(1, NT // 2) as j:
                            pair(j)
                        act.wait_ge(lgT_done, 1)
                        a.copy(lgT[:], psum[0:EG, 0:4, :].rearrange("p a b -> p (a b)")).then_inc(lgT_ready, 1)
                        act.wait_ge(lg_shifted, 1)
                        a.activation(pr[:, :, 0:E], pr[:, :, 0:E], ACT.Exp)
                        a.activation(lg[:, :, E:EG], lg[:, :, E:EG], ACT.Exp, scale=-1.0).then_inc(lg_exp, 1)
                        act.wait_ge(comb_turned, 1)
                        a.copy(combT[:], psum[0:EG, 0:4, :].rearrange("p a b -> p (a b)")).then_inc(combT_ready, 1)

                    @block.gpsimd
                    def _(pool):
                        pool.wait_ge(var2, 1)
                        nc.gpsimd.tensor_tensor(ln_rstd[:], ln_tmp[:, 2, :], half_const[:, 0:NT], ALU.pow).then_inc(rstd2, 1)

                    @block.vector
                    def _(dve):
                        v = nc.vector
                        link = chain_on(dve, step2)
                        for i in range(NT):
                            dve.wait_ge(acc_step, i + 1)
                            v.tensor_tensor(x_acc[:, i, :], x_acc[:, i, :], psum[:, 4 + i % 2, 0:HID], ALU.add).then_inc(sink_added, 1)
                        def tile(i):
                            dve.wait_ge(sink_added, NT)
                            v.tensor_tensor(x_acc[:, i, :], x_acc[:, i, :], out_bias[:], ALU.add).then_inc(x1_ready, 1)
                            dve.wait_ge(x1_ready, i + 1)
                            v.bn_stats(stats[:, i, :], x_acc[:, i, :]).then_inc(stats2, 1)
                        tile(0)
                        with dve.Fori(1, NT) as i:
                            tile(i)
                        layer_norm_stats_small(link, lambda: dve.wait_ge(stats2, NT)).then_inc(var2, 1)
                        dve.wait_ge(rstd2, 1)
                        def pair(j):
                            for par in range(2):
                                i = 2 * j + par
                                h = h_tok[:, par, :]
                                dve.wait_ge(h2_turned, 2 * j + 0)
                                v.tensor_scalar(h, x_acc[:, i, :], ln_mean[:, bass.ds(i, 1)], ln_rstd[:, bass.ds(i, 1)],
                                                ALU.subtract, ALU.mult).then_inc(norm2, 1)
                                dve.wait_ge(norm2, 4 * j + 2 * par + 1)
                                v.tensor_tensor(h, h, mod[:, 4, :], ALU.mult).then_inc(norm2, 1)
                                dve.wait_ge(norm2, 4 * j + 2 * par + 2)
                                v.tensor_tensor(h, h, mod[:, 3, :], ALU.add).then_inc(h2_ready, 1)
                        pair(0)
                        with dve.Fori(1, NT // 2) as j:
                            pair(j)
                        link(v.memset(pr[:], -1.0))
                        dve.wait_ge(lg_turned, 1)
                        link(v.tensor_copy(lg[:], psum[:, 4, :].rearrange("p (i e) -> p i e", e=32)[:, :, 0:EG]))
                        link(v.tensor_reduce(row_t[:, 0, :], lg[:, :, 0:E], AX, ALU.max))
                        v.tensor_tensor(pr[:, :, 0:E], lg[:, :, 0:E], bc(row_t[:, 0, :], 2, E), ALU.subtract).then_inc(lg_shifted, 1)
                        dve.wait_ge(lg_exp, 1)
                        link(v.tensor_reduce(row_t[:, 1, :], pr[:, :, 0:E], AX, ALU.add))
                        link(v.reciprocal(row_t[:, 2, :], row_t[:, 1, :]))
                        link(v.tensor_tensor(pr[:, :, 0:E], pr[:, :, 0:E], bc(row_t[:, 2, :], 2, E), ALU.mult))
                        for i in range(NT):
                            ins = v.max(top[:, i, :], pr[:, i, :])
                        link(ins)
                        link(v.memset(top[:, :, TOPK:8], -1.0))
                        for i in range(NT):
                            ins = v.match_replace(rep[:, i, :], top[:, i, :], pr[:, i, :], -2.0)
                        link(ins)
                        link(v.tensor_tensor(comb[:, :, 0:E], rep[:, :, 0:E], pr[:, :, 0:E], ALU.not_equal))
                        link(v.tensor_tensor(comb[:, :, 0:E], comb[:, :, 0:E], pr[:, :, 0:E], ALU.mult))
                        link(v.tensor_reduce(row_t[:, 1, :], comb[:, :, 0:E], AX, ALU.add))
                        link(v.tensor_scalar(row_t[:, 1, :], row_t[:, 1, :], 1e-9, None, ALU.max))
                        link(v.reciprocal(row_t[:, 2, :], row_t[:, 1, :]))
                        link(v.tensor_tensor(comb[:, :, 0:E], comb[:, :, 0:E], bc(row_t[:, 2, :], 2, E), ALU.mult))
                        link(v.tensor_scalar(lg[:, :, E:EG], lg[:, :, E:EG], 1.0, None, ALU.add))
                        v.reciprocal(comb[:, :, E:EG], lg[:, :, E:EG]).then_inc(comb_ready, 1)

            silu = sb("silu", [P, 2, 512], stack=ff)
            su = sb("su", [P, 2, 512], stack=ff)
            act_w = sb("act_w", [P, 2, 512], stack=ff)
            yT = sb("yT", [P, KH, 512], stack=ff)
            y_out = sb("y_out", [P, 2, 4, HID], stack=ff)
            gu_done = sem("gu_done", ff)
            pick_done = sem("pick_done", ff)
            silu_done = sem("silu_done", ff)
            su_done = sem("su_done", ff)
            act_ready = sem("act_ready", ff)
            down_done = sem("down_done", ff)
            yT_ready = sem("yT_ready", ff)
            y_turned = sem("y_turned", ff)
            y_gated = sem("y_gated", ff)
            y_ready = sem("y_ready", ff)
            y_stored = sem("y_stored", ff)
            G_BANK, U_BANK, W_BANK, Y_BANK = 0, 2, 4, 6
            with nc.Block() as block:
                @block.tensor
                def _(pe):
                    t = nc.tensor
                    pe.wait_ge(w_gu_in, 48)
                    pe.wait_ge(w_down_in, 16)

                    def up(n, j):
                        rhs = [hT[:, k, bass.ds(n * 512, 512)] for k in range(KH)]
                        b = j % 2
                        if j < 2:
                            pe.wait_ge(act_ready, n * NF)
                            pe.wait_ge(y_gated, 4 * n)
                        else:
                            pe.wait_ge(act_ready, n * NF + j - 1)
                        for m, bank in ((0, G_BANK), (1, U_BANK)):
                            for k in range(KH):
                                ins = t.matmul(psum[:, bank + b, :], w_gu[:, m, k, j * P:(j + 1) * P], rhs[k], start=(k == 0), stop=(k == KH - 1))
                        ins.then_inc(gu_done, 1)
                        t.matmul(psum[:, W_BANK + b, :], pick[:, j * P:(j + 1) * P], combT[:, bass.ds(n * 512, 512)],
                                 start=True, stop=True).then_inc(pick_done, 1)

                    def down(n, j):
                        pe.wait_ge(act_ready, n * NF + j + 1)
                        if j == 0:
                            pe.wait_ge(yT_ready, n)
                        for m in range(KH):
                            ins = t.matmul(psum[:, Y_BANK + m, :], w_down[:, j, m * P:(m + 1) * P], act_w[:, j % 2, :], start=(j == 0), stop=(j == NF - 1))
                        ins.then_inc(down_done, 1)

                    def group(n):
                        up(n, 0)
                        for j in range(NF):
                            if j + 1 < NF:
                                up(n, j + 1)
                            down(n, j)
                        pe.wait_ge(yT_ready, n + 1)
                        for q in range(4):
                            for k in range(KH):
                                ins = t.transpose(psum[:, G_BANK + q // 2, (q % 2) * HID + k * P:(q % 2) * HID + (k + 1) * P],
                                                  yT[:, k, q * P:(q + 1) * P], ident[:])
                        ins.then_inc(y_turned, 1)
                    group(0)
                    with pe.Fori(1, NC4) as n:
                        group(n)

                @block.scalar
                def _(act):
                    a = nc.scalar
                    def group(n):
                        for j in range(NF):
                            act.wait_ge(gu_done, n * NF + j + 1)
                            if j < 2:
                                act.wait_ge(su_done, n * NF)
                            else:
                                act.wait_ge(su_done, n * NF + j - 1)
                            a.activation(silu[:, j % 2, :], psum[:, G_BANK + j % 2, :], ACT.Silu).then_inc(silu_done, 1)
                        act.wait_ge(down_done, n * NF + NF)
                        a.copy(yT[:].rearrange("p k t -> p (k t)"), psum[:, Y_BANK:Y_BANK + 2, :].rearrange("p a b -> p (a b)")).then_inc(yT_ready, 1)
                    group(0)
                    with act.Fori(1, NC4) as n:
                        group(n)

                @block.vector
                def _(dve):
                    v = nc.vector
                    def group(n):
                        for j in range(NF):
                            dve.wait_ge(silu_done, n * NF + j + 1)
                            v.tensor_tensor(su[:, j % 2, :], silu[:, j % 2, :], psum[:, U_BANK + j % 2, :], ALU.mult).then_inc(su_done, 1)
                            dve.wait_ge(su_done, n * NF + j + 1)
                            dve.wait_ge(pick_done, n * NF + j + 1)
                            if j < 2:
                                dve.wait_ge(down_done, n * NF)
                            else:
                                dve.wait_ge(down_done, n * NF + j - 1)
                            v.tensor_tensor(act_w[:, j % 2, :], su[:, j % 2, :], psum[:, W_BANK + j % 2, :], ALU.mult).then_inc(act_ready, 1)
                        dve.wait_ge(y_turned, n + 1)
                        dve.wait_ge(y_stored, 16 * n)
                        for q in range(4):
                            y = y_out[:, 0, q, :]
                            v.tensor_tensor(y, psum[:, G_BANK + q // 2, (q % 2) * HID:(q % 2 + 1) * HID], mod[:, 5, :], ALU.mult).then_inc(y_gated, 1)
                        dve.wait_ge(y_gated, 4 * n + 4)
                        v.tensor_tensor(y_out[:, 1, :, :], y_out[:, 0, :, :], x_acc[:, bass.ds(n * 4, 4), :], ALU.add).then_inc(y_ready, 1)
                    group(0)
                    with dve.Fori(1, NC4) as n:
                        group(n)

                @block.sync
                def _(sp):
                    out = d["out"].rearrange("(t p) n -> p t n", p=P)
                    def group(n):
                        sp.wait_ge(y_ready, n + 1)
                        sp.dma_start(out[:, bass.ds(n * 4, 4), :], y_out[:, 1, :, :]).then_inc(y_stored, 16)
                    group(0)
                    with sp.Fori(1, NC4) as n:
                        group(n)
                    sp.wait_ge(y_stored, 16 * NC4)


def shape_constants():
    bf16 = mybir.dt.np(BF16)
    f = np.float32
    half = np.arange(HALF, dtype=f)
    inv_freq = (f(1.0) / np.power(f(10000.0), half * f(2.0) / f(ROPE))).astype(f)
    pos = np.arange(S, dtype=f).reshape(NT, P)
    ends = (np.arange(C, dtype=f) * R + (R - 1)).reshape(1, C)
    ang = np.concatenate([pos, ends])[:, :, None] * inv_freq
    trig = np.stack([np.cos(ang), np.sin(ang), -np.sin(ang)], 2).transpose(1, 0, 2, 3)
    masks = np.zeros((P, NT, LW), f)
    s = np.arange(P)[:, None]
    t = np.arange(P)[None, :]
    for i in range(NT):
        cur, prev = (i % 2) * P, (1 - i % 2) * P
        masks[:, i, cur:cur + P] = np.where(t <= s, 0, MASKED)
        masks[:, i, prev:prev + P] = np.where((s + P - t <= WIN) & (i > 0), 0, MASKED)
        masks[:, i, 2 * P:] = np.where(R * t + R - 1 <= P * i + s, 0, MASKED)
    owner = np.minimum(np.arange(FW) // I_MOE, E)
    pick = (owner[None, :] == np.arange(EG)[:, None]).astype(f)
    return {"ident": np.eye(P, dtype=f), "ident_b": np.eye(P).astype(bf16), "pick": pick,
            "trig": np.ascontiguousarray(trig.astype(f)), "masks": masks.astype(bf16)}


def kernel(**inputs):
    import concourse.bacc as bacc
    from concourse.bass_utils import run_bass_kernel_spmd

    a = {k.replace("L0_attn_", "").replace("L0_ffn_", ""): np.asarray(v) for k, v in inputs.items()}
    zeros = np.zeros((HID, FW - E * I_MOE - I_SH), np.float32)

    def up_layout(experts, shared):
        return np.concatenate([experts.transpose(1, 0, 2).reshape(HID, E * I_MOE), shared, zeros], 1)

    arrays = {
        "x": a["hidden_states"].reshape(S, HID), "Wq": a["Wq"], "Wlk": a["Wlk"], "Wlv": a["Wlv"], "Wo": a["Wo"],
        "Wk": a["Wk"], "Wv": a["Wv"], "wcT": a["Wc"].reshape(KH, P).T, "bc": a["bc"],
        "bias_qk": np.concatenate([a["bq"].reshape(NG, GW), a["blk"].reshape(NG, GW)], 1),
        "rows": np.stack([a["bk"], a["bv"], a["qn_w"], a["kn_w"]]),
        "sink_kT": a["sink_k"].T, "sink_vT": a["sink_v"].T, "blvT": a["blv"].reshape(NH, HD).T, "bo": a["bo"],
        "w_rt": np.concatenate([a["router_w"].T, a["sh_gate_w"]], 1),
        "w_gate": up_layout(a["w_gate"], a["sh_gate"]), "w_up": up_layout(a["w_up"], a["sh_up"]),
        "w_down": np.concatenate([a["w_down"].reshape(E * I_MOE, HID), a["sh_down"], zeros.T]),
        "cT": a["L0_c"].reshape(KH, P).T, "wmod": a["L0_wmod"],
    }
    arrays.update(shape_constants())
    nc = bacc.Bacc("TRN2", target_bir_lowering=False, num_devices=1)
    d, feed = {}, {}
    for name, arr in arrays.items():
        arr = np.ascontiguousarray(arr)
        feed[f"in_{name}"] = arr
        d[name] = nc.dram_tensor(f"in_{name}", arr.shape, mybir.dt.from_np(arr.dtype), kind="ExternalInput").ap()
    d["out"] = nc.dram_tensor("out_x", (S, HID), F32, kind="ExternalOutput").ap()
    build(nc, d)
    r = run_bass_kernel_spmd(nc, [feed], core_ids=[0])
    return r.results[0]["out_x"].reshape(1, S, HID)
```

```python
from contextlib import ExitStack

import numpy as np

import concourse.bass as bass
from concourse import mybir

P = 128
S = 2048
HID = 256
KH = HID // P
NH = 16
HD = 128
NT = S // P
HG = 4
NG = NH // HG
NU = NG * NT
GW = HG * HD
R = 16
C = S // R
WIN = 128
ROPE = HD // 2
HALF = ROPE // 2
EPS_RMS = 1e-6
EPS_LN = 1e-5
MASKED = -1e30
E = 16
TOPK = 4
I_MOE = 176
I_SH = 704
NF = -(-(E * I_MOE + I_SH) // P)
FW = NF * P
EG = E + 1
PADK = TOPK
TG = 512
NTG = S // TG
CT = 4
NCH = NF // CT
GU = KH * CT * P
FCOLS = 2 * GU + CT * HID
LW = 2 * P + C + 2
WCOLS = 3 * KH * GW
WCH = WCOLS // NT

F32 = mybir.dt.float32
BF16 = mybir.dt.bfloat16
F32R = mybir.dt.float32r
ALU = mybir.AluOpType
ACT = mybir.ActivationFunctionType
AX = mybir.AxisListType.X


def bc(ap, dim, n):
    ap = ap.unsqueeze(dim)
    shape = list(ap.shape)
    shape[dim] = n
    return ap.to_broadcast(shape)


def build(nc, d):
    with ExitStack() as ctx:
        def sb(name, shape, dt=F32, stack=ctx):
            return stack.enter_context(nc.sbuf_tensor(name, shape, dt))

        def sem(name, stack=ctx):
            return stack.enter_context(nc.semaphore(name))

        psum = ctx.enter_context(nc.psum_tensor("psum", [P, 8, 512], F32))

        ident = sb("ident", [P, P])
        mod = sb("mod", [P, 6, HID])
        x_acc = sb("x_acc", [P, NT, HID])
        hT = sb("hT", [P, KH, S])
        out_bias = sb("out_bias", [P, HID])
        sink_out = sb("sink_out", [NH, HID])
        sink_prob = sb("sink_prob", [P, NT, NH])
        half_const = sb("half_const", [P, 32])
        stats = sb("stats", [P, NT, 6])
        ln_mean = sb("ln_mean", [P, NT])
        ln_rstd = sb("ln_rstd", [P, NT])
        ln_tmp = sb("ln_tmp", [P, 3, NT])

        def layer_norm_stats_small(chain, stats_all):
            dv = nc.vector
            me, m2e, mo, m2o = (stats[:, :, c] for c in (1, 2, 4, 5))
            a, b, v = (ln_tmp[:, c, :] for c in range(3))
            stats_all()
            chain(dv.tensor_tensor(a, me, mo, ALU.add))
            chain(dv.tensor_scalar(ln_mean[:], a, 0.5, None, ALU.mult))
            chain(dv.tensor_tensor(b, me, mo, ALU.subtract))
            chain(dv.tensor_tensor(b, b, b, ALU.mult))
            chain(dv.tensor_scalar(b, b, 0.25, EPS_LN, ALU.mult, ALU.add))
            chain(dv.tensor_tensor(a, m2e, m2o, ALU.add))
            return dv.scalar_tensor_tensor(v, a, 1.0 / HID, b, ALU.mult, ALU.add)

        def chain_on(eng, s):
            n = [0]

            def link(ins):
                n[0] += 1
                ins.then_inc(s, 1)
                eng.wait_ge(s, n[0])
            return link

        att = ctx.enter_context(ExitStack())

        w_split = sb("w_split", [P, 2, 2, WCOLS], F32R, stack=att)
        w_o = sb("w_o", [P, NH, HID], stack=att)
        bias_qk = sb("bias_qk", [P, NG, 2 * GW], stack=att)
        rope_same = sb("rope_same", [P, NT, 2, HD], stack=att)
        rope_swap = sb("rope_swap", [P, NT, 2, ROPE], stack=att)
        mask_keys = sb("mask_keys", [P, 4, 2 * P], BF16, stack=att)
        mask_ent = sb("mask_ent", [P, NT, LW - 2 * P], BF16, stack=att)
        ident_b = sb("ident_b", [P, P], BF16, stack=att)
        ckT = sb("ckT", [P, C], stack=att)
        cv = sb("cv", [P, HD], stack=att)
        sink_split = sb("sink_split", [P, 2, NH], F32R, stack=att)
        keys = sb("keys", [P, 2, HG, LW], F32R, stack=att)
        v_ring = sb("v_ring", [P, 2, GW], stack=att)

        with ExitStack() as pre:
            h_tok = sb("h_tok", [P, 2, HID], stack=pre)
            cT = sb("cT", [P, KH], stack=pre)
            c_tmp = sb("c_tmp", [P, 3, KH], stack=pre)
            c_rep = sb("c_rep", [P, KH, P], stack=pre)
            w_mod = sb("w_mod", [P, KH, 6 * HID], stack=pre)
            gate_tmp = sb("gate_tmp", [P, 2, HID], stack=pre)
            wcT = sb("wcT", [P, KH], stack=pre)
            wc_rep = sb("wc_rep", [P, KH, P], stack=pre)
            b_c = sb("b_c", [P, 1], stack=pre)
            w_kv = sb("w_kv", [P, 2, KH, HD], stack=pre)
            rows = sb("rows", [P, 4, HD], stack=pre)
            trig = sb("trig", [P, NT + 1, 3, HALF], stack=pre)
            sink_vT = sb("sink_vT", [P, NH], stack=pre)
            blvT = sb("blvT", [P, NH], stack=pre)
            sv_diag = sb("sv_diag", [P, NH * NH], stack=pre)
            spare = bias_qk[:].rearrange("p g n -> p (g n)")
            blv_rep = spare[:, 0:NH * P].rearrange("p (h t) -> p h t", h=NH)
            bo_row = sb("bo_row", [P, HID], stack=pre)
            pool_w = spare[:, NH * P:NH * P + S].rearrange("p (c r) -> p c r", r=R)
            pool_m = sb("pool_m", [P, 2, C], stack=pre)
            entT = sb("entT", [P, KH, C], stack=pre)
            ck = sb("ck", [P, 2, HD], stack=pre)
            ck_t = sb("ck_t", [P, 4], stack=pre)
            ck_r = sb("ck_r", [P, 4, HALF], stack=pre)

            sink_kT = sb("sink_kT", [P, NH], stack=pre)
            w_first = w_mod[:].rearrange("p k n -> p (k n)")

            c_in = sem("c_in", pre)
            w_high = sem("w_high", pre)
            x_in = sem("x_in", pre)
            tables_in = sem("tables_in", pre)
            wo_in = sem("wo_in", pre)
            late_in = sem("late_in", pre)
            exp_c = sem("exp_c", pre)
            c_spread = sem("c_spread", pre)
            mod_done = sem("mod_done", pre)
            mod_raw = sem("mod_raw", pre)
            dve_step = sem("dve_step", pre)
            stats_done = sem("stats_done", pre)
            var_done = sem("var_done", pre)
            rstd_done = sem("rstd_done", pre)
            pool_const = sem("pool_const", pre)
            pool_step = sem("pool_step", pre)
            norm_step = sem("norm_step", pre)
            h_ready = sem("h_ready", pre)
            h_turned = sem("h_turned", pre)
            hT_ready = sem("hT_ready", pre)
            wc_ready = sem("wc_ready", pre)
            logits_done = sem("logits_done", pre)
            shifted = sem("shifted", pre)
            exp_pool = sem("exp_pool", pre)
            ent_ready = sem("ent_ready", pre)
            kv_done = sem("kv_done", pre)
            ck_biased = sem("ck_biased", pre)
            ck_ss = sem("ck_ss", pre)
            ck_var = sem("ck_var", pre)
            ck_rstd = sem("ck_rstd", pre)
            ck_ready = sem("ck_ready", pre)
            ck_turned = sem("ck_turned", pre)
            ckT_ready = sem("ckT_ready", pre)
            wo_ready = sem("wo_ready", pre)
            sink_done = sem("sink_done", pre)
            bias_done = sem("bias_done", pre)
            evac = sem("evac", pre)
            zeroed = sem("zeroed", pre)

            with nc.Block() as block:
                @block.sync
                def _(sp):
                    sp.dma_start(cT[:], d["cT"]).then_inc(c_in, 16)
                    sp.dma_start(w_mod[:], d["wmod"].rearrange("(k p) n -> p k n", p=P)).then_inc(c_in, 16)
                    sp.dma_start(x_acc[:], d["x"].rearrange("(t p) n -> p t n", p=P)).then_inc(x_in, 16)
                    sp.dma_start(ident[:], d["ident"]).then_inc(x_in, 16)
                    sp.dma_start(w_o[:], d["Wo"].rearrange("(h p) n -> p h n", p=P)).then_inc(wo_in, 16)
                    sp.dma_start(sink_vT[:], d["sink_vT"]).then_inc(wo_in, 16)
                    sp.dma_start(blvT[:], d["blvT"]).then_inc(wo_in, 16)
                    sp.dma_start(bo_row[:], d["bo"].partition_broadcast(P)).then_inc(wo_in, 16)
                    sp.wait_ge(mod_done, 1)
                    sp.dma_start(w_first.rearrange("p (c n) -> p c n", c=NT), d["w_groups"][0].rearrange("c p n -> p c n")).then_inc(late_in, 16)
                    sp.dma_start(mask_keys[:], d["mask_keys"]).then_inc(late_in, 16)
                    sp.dma_start(mask_ent[:], d["mask_ent"]).then_inc(late_in, 16)
                    sp.dma_start(ident_b[:], d["ident_b"]).then_inc(late_in, 16)
                    sp.dma_start(sink_kT[:], d["sink_kT"]).then_inc(late_in, 16)
                    sp.wait_ge(late_in, 16 * 5)

                @block.scalar
                def _(act):
                    act.dma_start(wcT[:], d["wcT"]).then_inc(tables_in, 16)
                    act.dma_start(b_c[:], d["bc"].partition_broadcast(P)).then_inc(tables_in, 16)
                    act.dma_start(w_kv[:, 0, :, :], d["Wk"].rearrange("(k p) n -> p k n", p=P)).then_inc(tables_in, 16)
                    act.dma_start(w_kv[:, 1, :, :], d["Wv"].rearrange("(k p) n -> p k n", p=P)).then_inc(tables_in, 16)
                    act.dma_start(rows[:], d["rows"].partition_broadcast(P)).then_inc(tables_in, 16)
                    act.dma_start(trig[:], d["trig"]).then_inc(tables_in, 16)
                    act.wait_ge(c_in, 32)
                    nc.scalar.activation(c_tmp[:, 0, :], cT[:], ACT.Exp, scale=-1.0).then_inc(exp_c, 1)
                    def pair(j):
                        for par in range(2):
                            act.wait_ge(h_turned, 2 * j + par + 1)
                            nc.scalar.copy(hT[:, :, bass.ds((2 * j + par) * P, P)],
                                           psum[:, 4 + par, 0:2 * P].rearrange("p (k t) -> p k t", k=KH)).then_inc(hT_ready, 1)
                    pair(0)
                    with act.Fori(1, NT // 2) as j:
                        pair(j)
                    act.wait_ge(late_in, 80)
                    nc.scalar.copy(w_split[:, 0, 0, :], w_first)
                    nc.scalar.copy(sink_split[:, 0, :], sink_kT[:]).then_inc(w_high, 1)
                    act.wait_ge(shifted, 1)
                    nc.scalar.activation(pool_w, pool_w, ACT.Exp).then_inc(exp_pool, 1)
                    act.wait_ge(ck_biased, 1)
                    nc.scalar.activation(ck[:, 1, :], ck[:, 0, :], ACT.Square, accum_out=ck_t[:, 0:1]).then_inc(ck_ss, 1)
                    act.wait_ge(ck_turned, 1)
                    nc.scalar.copy(ckT[:], psum[:, 6, 0:C]).then_inc(ckT_ready, 1)

                @block.tensor
                def _(pe):
                    pe.wait_ge(c_spread, 1)
                    for n in range(3):
                        for k in range(KH):
                            last = nc.tensor.matmul(psum[:, n, :], c_rep[:, k, :], w_mod[:, k, n * 512:(n + 1) * 512],
                                                    start=(k == 0), stop=(k == KH - 1))
                    last.then_inc(mod_done, 1)
                    pe.wait_ge(x_in, 32)
                    def pair(j):
                        for par in range(2):
                            pe.wait_ge(h_ready, 2 * j + par + 1)
                            pe.wait_ge(hT_ready, 2 * j + 0)
                            for k in range(KH):
                                last = nc.tensor.transpose(psum[:, 4 + par, k * P:(k + 1) * P], h_tok[:, par, k * P:(k + 1) * P], ident[:])
                            last.then_inc(h_turned, 1)
                    pair(0)
                    with pe.Fori(1, NT // 2) as j:
                        pair(j)
                    pe.wait_ge(hT_ready, NT)
                    pe.wait_ge(wc_ready, 1)
                    pe.wait_ge(mod_raw, 1)
                    for n in range(4):
                        for k in range(KH):
                            last = nc.tensor.matmul(psum[:, n, :], wc_rep[:, k, :], hT[:, k, n * 512:(n + 1) * 512],
                                                    start=(k == 0), stop=(k == KH - 1))
                    last.then_inc(logits_done, 1)
                    pe.wait_ge(wo_ready, 1)
                    for h in range(NH):
                        last = nc.tensor.matmul(psum[0:NH, 4, 0:HID], sv_diag[:, h * NH:(h + 1) * NH], w_o[:, h, :],
                                                start=(h == 0), stop=(h == NH - 1))
                    last.then_inc(sink_done, 1)
                    for h in range(NH):
                        last = nc.tensor.matmul(psum[:, 5, 0:HID], blv_rep[:, h, :], w_o[:, h, :],
                                                start=(h == 0), stop=(h == NH - 1))
                    last.then_inc(bias_done, 1)
                    pe.wait_ge(ent_ready, 1)
                    for m in range(2):
                        for k in range(KH):
                            last = nc.tensor.matmul(psum[:, 6 + m, 0:HD], entT[:, k, :], w_kv[:, m, k, :],
                                                    start=(k == 0), stop=(k == KH - 1))
                    last.then_inc(kv_done, 1)
                    pe.wait_ge(ck_ready, 1)
                    nc.tensor.transpose(psum[:, 6, 0:C], ck[:, 1, :], ident[:]).then_inc(ck_turned, 1)

                @block.gpsimd
                def _(pool):
                    g = nc.gpsimd
                    g.memset(half_const[:], -0.5).then_inc(pool_const, 1)
                    g.memset(keys[:].bitcast(F32), 0.0).then_inc(zeroed, 1)
                    g.memset(v_ring[:], 0.0).then_inc(zeroed, 1)
                    pool.wait_ge(tables_in, 96)
                    cos, sin, nsin = (trig[:, 0:NT, c, :] for c in range(3))
                    for m in range(2):
                        w1, w2 = rows[:, 2 + m, 0:HALF], rows[:, 2 + m, HALF:ROPE]
                        g.tensor_tensor(rope_same[:, :, m, 0:HALF], cos, bc(w1, 1, NT), ALU.mult)
                        g.tensor_tensor(rope_same[:, :, m, HALF:ROPE], cos, bc(w2, 1, NT), ALU.mult)
                        g.tensor_copy(rope_same[:, :, m, ROPE:HD], bc(rows[:, 2 + m, ROPE:HD], 1, NT))
                        g.tensor_tensor(rope_swap[:, :, m, 0:HALF], nsin, bc(w2, 1, NT), ALU.mult)
                        g.tensor_tensor(rope_swap[:, :, m, HALF:ROPE], sin, bc(w1, 1, NT), ALU.mult).then_inc(zeroed, 1)
                    pool.wait_ge(pool_const, 1)
                    pool.wait_ge(var_done, 1)
                    g.tensor_tensor(ln_rstd[:], ln_tmp[:, 2, :], half_const[:, 0:NT], ALU.pow).then_inc(rstd_done, 1)
                    pool.wait_ge(ck_var, 1)
                    g.tensor_tensor(ck_t[:, 2:3], ck_t[:, 1:2], half_const[:, 0:1], ALU.pow).then_inc(ck_rstd, 1)

                @block.vector
                def _(dve):
                    v = nc.vector
                    link = chain_on(dve, dve_step)
                    dve.wait_ge(exp_c, 1)
                    link(v.tensor_scalar(c_tmp[:, 1, :], c_tmp[:, 0, :], 1.0, None, ALU.add))
                    link(v.reciprocal(c_tmp[:, 2, :], c_tmp[:, 1, :]))
                    link(v.tensor_tensor(c_tmp[:, 1, :], cT[:], c_tmp[:, 2, :], ALU.mult))
                    v.tensor_copy(c_rep[:], bc(c_tmp[:, 1, :], 2, P)).then_inc(c_spread, 1)
                    dve.wait_ge(tables_in, 96)
                    v.tensor_copy(wc_rep[:], bc(wcT[:], 2, P)).then_inc(wc_ready, 1)
                    dve.wait_ge(x_in, 32)
                    def tile(i):
                        v.bn_stats(stats[:, i, :], x_acc[:, i, :]).then_inc(stats_done, 1)
                    tile(0)
                    with dve.Fori(1, NT) as i:
                        tile(i)
                    layer_norm_stats_small(link, lambda: dve.wait_ge(stats_done, NT)).then_inc(var_done, 1)
                    dve.wait_ge(mod_done, 1)
                    v.tensor_copy(mod[:].rearrange("p a b -> p (a b)"), psum[:, 0:3, :].rearrange("p a b -> p (a b)")).then_inc(mod_raw, 1)
                    dve.wait_ge(mod_raw, 1)
                    for scale_row, gate_row in ((1, 2), (4, 5)):
                        link(v.tensor_scalar(mod[:, scale_row, :], mod[:, scale_row, :], 1.0, None, ALU.add))
                        gate = mod[:, gate_row, :]
                        link(v.tensor_scalar(gate_tmp[:, 0, :], gate, 0.0, 2.0, ALU.is_ge, ALU.mult))
                        link(v.scalar_tensor_tensor(gate_tmp[:, 1, :], gate, -1.0, gate, ALU.mult, ALU.max))
                        link(v.tensor_scalar(gate_tmp[:, 1, :], gate_tmp[:, 1, :], 0.25, None, ALU.max))
                        link(v.scalar_tensor_tensor(gate, gate_tmp[:, 0, :], -1.0, gate_tmp[:, 1, :], ALU.add, ALU.mult))
                    dve.wait_ge(rstd_done, 1)
                    def pair(j):
                        for par in range(2):
                            i = 2 * j + par
                            h = h_tok[:, par, :]
                            dve.wait_ge(h_turned, 2 * j + 0)
                            v.tensor_scalar(h, x_acc[:, i, :], ln_mean[:, bass.ds(i, 1)], ln_rstd[:, bass.ds(i, 1)],
                                            ALU.subtract, ALU.mult).then_inc(norm_step, 1)
                            dve.wait_ge(norm_step, 4 * j + 2 * par + 1)
                            v.tensor_tensor(h, h, mod[:, 1, :], ALU.mult).then_inc(norm_step, 1)
                            dve.wait_ge(norm_step, 4 * j + 2 * par + 2)
                            v.tensor_tensor(h, h, mod[:, 0, :], ALU.add).then_inc(h_ready, 1)
                    pair(0)
                    with dve.Fori(1, NT // 2) as j:
                        pair(j)
                    dve.wait_ge(wo_in, 64)
                    link(v.memset(sv_diag[:], 0.0))
                    link(v.tensor_copy(sv_diag[:, 0:NH * NH:NH + 1], sink_vT[:]))
                    link(v.tensor_copy(blv_rep, bc(blvT[:], 2, P)))
                    v.scalar_tensor_tensor(w_o[:], w_o[:], 0.5, bc(mod[:, 2, :], 1, NH), ALU.mult, ALU.mult).then_inc(wo_ready, 1)
                    link(v.tensor_tensor(bo_row[:], bo_row[:], mod[:, 2, :], ALU.mult))
                    dve.wait_ge(logits_done, 1)
                    link(v.tensor_scalar(pool_w.rearrange("p c r -> p (c r)"), psum[:, 0:4, :].rearrange("p a b -> p (a b)"),
                                         b_c[:, 0:1], None, ALU.add))
                    link(v.tensor_reduce(pool_m[:, 0, :], pool_w, AX, ALU.max))
                    v.tensor_tensor(pool_w, pool_w, bc(pool_m[:, 0, :], 2, R), ALU.subtract).then_inc(shifted, 1)
                    dve.wait_ge(sink_done, 1)
                    v.tensor_copy(sink_out[:], psum[0:NH, 4, 0:HID]).then_inc(evac, 1)
                    dve.wait_ge(bias_done, 1)
                    v.tensor_tensor(out_bias[:], psum[:, 5, 0:HID], bo_row[:], ALU.add).then_inc(evac, 1)
                    dve.wait_ge(exp_pool, 1)
                    link(v.tensor_reduce(pool_m[:, 0, :], pool_w, AX, ALU.add))
                    link(v.reciprocal(pool_m[:, 1, :], pool_m[:, 0, :]))
                    link(v.tensor_tensor(pool_w, pool_w, bc(pool_m[:, 1, :], 2, R), ALU.mult))
                    dve.wait_ge(w_high, 1)
                    link(v.tensor_tensor(w_split[:, 0, 1, :], w_first, w_split[:, 0, 0, :].bitcast(F32), ALU.subtract))
                    v.tensor_tensor(sink_split[:, 1, :], sink_kT[:], sink_split[:, 0, :].bitcast(F32), ALU.subtract)
                    dve.wait_ge(hT_ready, NT)
                    prod = w_mod[:].rearrange("p k n -> p (k n)")[:, 0:S].rearrange("p (c r) -> p c r", r=R)
                    for k in range(KH):
                        link(v.tensor_tensor(prod, hT[:, k, :].rearrange("p (c r) -> p c r", r=R), pool_w, ALU.mult))
                        ins = v.tensor_reduce(entT[:, k, :], prod, AX, ALU.add)
                        if k < KH - 1:
                            link(ins)
                    ins.then_inc(ent_ready, 1)
                    dve.wait_ge(kv_done, 1)
                    v.tensor_tensor(ck[:, 0, :], psum[:, 6, 0:HD], rows[:, 0, :], ALU.add).then_inc(ck_biased, 1)
                    v.tensor_tensor(cv[:], psum[:, 7, 0:HD], rows[:, 1, :], ALU.add).then_inc(evac, 1)
                    dve.wait_ge(ck_ss, 1)
                    v.tensor_scalar(ck_t[:, 1:2], ck_t[:, 0:1], 1.0 / HD, EPS_RMS, ALU.mult, ALU.add).then_inc(ck_var, 1)
                    dve.wait_ge(ck_rstd, 1)
                    dve.wait_ge(ck_biased, 1)
                    link(v.scalar_tensor_tensor(ck[:, 0, :], ck[:, 0, :], ck_t[:, 2:3], rows[:, 2, :], ALU.mult, ALU.mult))
                    x1, x2 = ck[:, 0, 0:HALF], ck[:, 0, HALF:ROPE]
                    cos, sin = trig[:, NT, 0, :], trig[:, NT, 1, :]
                    link(v.tensor_tensor(ck_r[:, 0, :], x1, cos, ALU.mult))
                    link(v.tensor_tensor(ck_r[:, 1, :], x2, sin, ALU.mult))
                    link(v.tensor_tensor(ck_r[:, 2, :], x1, sin, ALU.mult))
                    link(v.tensor_tensor(ck_r[:, 3, :], x2, cos, ALU.mult))
                    link(v.tensor_tensor(ck[:, 1, 0:HALF], ck_r[:, 0, :], ck_r[:, 1, :], ALU.subtract))
                    link(v.tensor_tensor(ck[:, 1, HALF:ROPE], ck_r[:, 2, :], ck_r[:, 3, :], ALU.add))
                    v.tensor_copy(ck[:, 1, ROPE:HD], ck[:, 0, ROPE:HD]).then_inc(ck_ready, 1)

        with ExitStack() as un:
            qk_tok = sb("qk_tok", [P, 2, HG, HD], stack=un)
            qk_rot = sb("qk_rot", [P, 2, HG, HD], stack=un)
            qk_swp = sb("qk_swp", [P, 2, HG, ROPE], stack=un)
            ms = sb("ms", [P, 2, HG], stack=un)
            ms_eps = sb("ms_eps", [P, 2, HG], stack=un)
            rstd = sb("rstd", [P, 2, HG], stack=un)
            rstd_q = sb("rstd_q", [P, HG], stack=un)
            qT = sb("qT", [P, 2, HG, P], F32R, stack=un)
            v_new = sb("v_new", [P, 2, GW], stack=un)
            h_now = sb("h_now", [P, 2, KH, P], F32R, stack=un)
            mx = sb("mx", [P, 2, HG], stack=un)
            nmx = sb("nmx", [P, 2, HG], stack=un)
            sums = sb("sums", [P, 2, HG], stack=un)
            inv = sb("inv", [P, 2, HG], stack=un)
            prob = sb("prob", [P, HG, LW], stack=un)
            probT = sb("probT", [P, 3, HG, P], stack=un)
            ctxT = sb("ctxT", [P, HG, P], stack=un)
            w_stage = sb("w_stage", [P, WCH], stack=un)

            names = ("bias_in keys_set w_staged w_high w_low h_high h_split k_projected v_projected qk_biased qk_squared ms_summed ms_ready "
                     "rstd_ready rstd_kept swap_ready rot_own rot_added rot_ready k_turned q_turned k_high k_ready q_high qk_ready v_out v_placed "
                     "scored max_done nmax_ready exps_done inv_ready sink_kept prob_ready p_turned p_ready ctx_done ctx_ready "
                     "out_done acc_done")
            s = {n: sem(n, un) for n in names.split()}

            K_BANK, Q_BANK, V_BANK, SC_BANK, T_BANK = 0, 1, 2, 3, 7
            t_banks = (K_BANK, Q_BANK, T_BANK)
            t_order = (2, 0, 1)
            NPRE = NU - NT

            def tile_of(u):
                return u & (NT - 1)

            def group_of(u):
                return (u >> 4) & (NG - 1)

            def par_of(u):
                return u & 1

            def run_steps(eng, step):
                step(0, prev=False)
                with eng.Fori(1, NPRE - 1) as u:
                    step(u)
                with eng.Fori(NPRE - 1, NU - 2) as u:
                    step(u, weights=False)
                step(NU - 2, weights=False, nxt2=False)
                step(NU - 1, weights=False, nxt2=False, nxt=False)

            with nc.Block() as block:
                @block.sync
                def _(sp):
                    sp.dma_start(bias_qk[:], d["bias_qk"].partition_broadcast(P)).then_inc(s["bias_in"], 16)

                    def chunk(e):
                        sp.dma_start(w_stage[:], d["w_groups"][group_of(e + NT), tile_of(e), :, :]).then_inc(s["w_staged"], 16)

                    chunk(0)
                    with sp.Fori(1, NPRE) as e:
                        sp.wait_ge(s["w_low"], e)
                        chunk(e)
                    sp.wait_ge(s["w_staged"], 16 * NPRE)

                @block.tensor
                def _(pe):
                    t = nc.tensor

                    def project(u, weights=True):
                        pe.wait_ge(s["h_split"], u + 1)
                        if weights and not (isinstance(u, int) and u < 2):
                            pe.wait_ge(s["w_low"], u)
                        g = group_of(u)
                        for m in (1, 0, 2):
                            if m == 0:
                                pe.wait_ge(s["k_ready"], u)
                            if m == 2 and not (isinstance(u, int) and u < 2):
                                pe.wait_ge(s["acc_done"], u - 2)
                            for k in range(KH):
                                col = (m * KH + k) * GW
                                w = [w_split[:, g & 1, part, col:col + GW] for part in range(2)]
                                product(psum[:, m, :], [h_now[:, part, k, :] for part in range(2)], w, k == 0, k == KH - 1)
                                ins = last[0]
                            if m == 0:
                                ins.then_inc(s["k_projected"], 1)
                        ins.then_inc(s["v_projected"], 1)

                    last = [None]

                    def product(out, lhs, rhs, start, stop):
                        t.matmul(out, lhs[1], rhs[0], start=start, stop=False)
                        t.matmul(out, lhs[0], rhs[0], start=False, stop=False)
                        last[0] = t.matmul(out, lhs[0], rhs[1], start=False, stop=stop)

                    def turn_qk(u):
                        pe.wait_ge(s["rot_ready"], u + 1)
                        for m, bank in ((0, K_BANK), (1, T_BANK)):
                            for h in range(HG):
                                ins = t.transpose(psum[:, bank, h * P:(h + 1) * P], qk_rot[:, m, h, :], ident[:])
                            ins.then_inc(s["q_turned" if m else "k_turned"], 1)

                    def score(u, heads):
                        i = tile_of(u)
                        which = (i & 1) | (((NT - i) >> 4) << 1)
                        if heads[0] == 0:
                            pe.wait_ge(s["qk_ready"], u + 1)
                            pe.wait_ge(s["keys_set"], HG)
                            pe.wait_ge(s["exps_done"], u)
                        for h in heads:
                            out = psum[:, SC_BANK + h, 0:LW]
                            t.matmul(out[:, 0:2 * P], ident_b[:], mask_keys[:, which, :], start=True, stop=False)
                            t.matmul(out[:, 2 * P:LW], ident_b[:], mask_ent[:, i, :], start=False, stop=False)
                            product(out, [qT[:, part, h, :] for part in range(2)], [keys[:, part, h, :] for part in range(2)], False, True)
                        if heads[-1] == HG - 1:
                            last[0].then_inc(s["scored"], 1)

                    def turn_probs(u, nxt2=True):
                        pe.wait_ge(s["prob_ready"], u + 1)
                        if nxt2:
                            pe.wait_ge(s["qk_biased"], u + 3)
                        for c in t_order:
                            for h in range(HG):
                                ins = t.transpose(psum[:, t_banks[c], h * P:(h + 1) * P], prob[:, h, c * P:(c + 1) * P], ident[:])
                            ins.then_inc(s["p_turned"], 1)

                    def context(u, nxt2=True):
                        pe.wait_ge(s["v_placed"], u + 1)
                        pe.wait_ge(s["p_ready"], 3 * u + 1)
                        if nxt2:
                            pe.wait_ge(s["v_out"], u + 3)
                        t.matmul(psum[:, V_BANK, :], cv[:], probT[:, 2, :, :].rearrange("p h t -> p (h t)"), start=True, stop=True)
                        for c in range(2):
                            pe.wait_ge(s["p_ready"], 3 * u + 2 + c)
                            for h in range(HG):
                                ins = t.matmul(psum[:, V_BANK, h * P:(h + 1) * P], v_ring[:, c, h * HD:(h + 1) * HD], probT[:, c, h, :],
                                               start=False, stop=True, skip_group_check=True)
                        ins.then_inc(s["ctx_done"], 1)

                    def output(u):
                        g = group_of(u)
                        pe.wait_ge(s["ctx_ready"], u + 1)
                        for h in range(HG):
                            ins = t.matmul(psum[:, V_BANK, 0:HID], ctxT[:, h, :], w_o[:, g * HG + h, :], start=(h == 0), stop=(h == HG - 1))
                        ins.then_inc(s["out_done"], 1)

                    def step(u, prev=True, nxt=True, nxt2=True, weights=True):
                        score(u, range(HG - 1))
                        if prev:
                            turn_probs(u - 1, nxt)
                        score(u, (HG - 1,))
                        if prev:
                            context(u - 1, nxt)
                        if nxt:
                            turn_qk(u + 1)
                        if prev:
                            output(u - 1)
                        if nxt2:
                            project(u + 2, weights)

                    project(0)
                    turn_qk(0)
                    project(1)
                    run_steps(pe, step)
                    turn_probs(NU - 1, False)
                    context(NU - 1, False)
                    output(NU - 1)

                @block.scalar
                def _(act):
                    a = nc.scalar

                    def split_weights(e):
                        act.wait_ge(s["w_staged"], 16 * e + 16)
                        act.wait_ge(s["v_projected"], e)
                        a.copy(w_split[:, group_of(e + NT) & 1, 0, bass.ds(tile_of(e) * WCH, WCH)], w_stage[:]).then_inc(s["w_high"], 1)

                    def split_h(u):
                        act.wait_ge(s["v_projected"], u)
                        a.copy(h_now[:, 0, :, :], hT[:, :, bass.ds(tile_of(u) * P, P)]).then_inc(s["h_high"], 1)

                    def square(u):
                        act.wait_ge(s["qk_biased"], u + 1)
                        a.activation(qk_rot[:], qk_tok[:], ACT.Square).then_inc(s["qk_squared"], 1)

                    def v_evac(u):
                        act.wait_ge(s["v_projected"], u + 1)
                        if not (isinstance(u, int) and u < 2):
                            act.wait_ge(s["v_placed"], u - 1)
                        a.copy(v_new[:, par_of(u), :], psum[:, V_BANK, :]).then_inc(s["v_out"], 1)

                    def qk_evac(u):
                        act.wait_ge(s["k_turned"], u + 1)
                        a.copy(keys[:, 0, :, bass.ds(par_of(u) * P, P)], psum[:, K_BANK, :].rearrange("p (h t) -> p h t", h=HG)).then_inc(s["k_high"], 1)
                        act.wait_ge(s["q_turned"], u + 1)
                        a.copy(qT[:, 0, :, :], psum[:, T_BANK, :].rearrange("p (h t) -> p h t", h=HG)).then_inc(s["q_high"], 1)

                    def exps(u):
                        act.wait_ge(s["nmax_ready"], u + 1)
                        for c, (lo, hi) in enumerate(((0, 2 * P), (2 * P, 2 * P + C + 1))):
                            for h in range(HG):
                                ins = a.activation(prob[:, h, lo:hi], psum[:, SC_BANK + h, lo:hi], ACT.Exp, bias=nmx[:, c, h:h + 1],
                                                   scale=rstd_q[:, h:h + 1], accum_out=sums[:, c, h:h + 1])
                        ins.then_inc(s["exps_done"], 1)

                    def probs_evac(u):
                        for n, c in enumerate(t_order):
                            act.wait_ge(s["p_turned"], 3 * u + n + 1)
                            a.copy(probT[:, c, :, :].rearrange("p h t -> p (h t)"), psum[:, t_banks[c], :]).then_inc(s["p_ready"], 1)

                    def ctx_evac(u):
                        act.wait_ge(s["ctx_done"], u + 1)
                        a.copy(ctxT[:].rearrange("p h t -> p (h t)"), psum[:, V_BANK, :]).then_inc(s["ctx_ready"], 1)

                    def step(u, prev=True, nxt=True, nxt2=True, weights=True):
                        if nxt:
                            square(u + 1)
                            v_evac(u + 1)
                        if prev:
                            probs_evac(u - 1)
                        if nxt2:
                            split_h(u + 2)
                        if weights:
                            split_weights(u + 1)
                        if prev:
                            ctx_evac(u - 1)
                        if nxt:
                            qk_evac(u + 1)
                        exps(u)

                    for h in range(HG):
                        a.copy(keys[:, 0, h, 2 * P:2 * P + C], ckT[:]).then_inc(s["keys_set"], 1)
                    split_h(0)
                    square(0)
                    v_evac(0)
                    split_h(1)
                    qk_evac(0)
                    split_weights(0)
                    run_steps(act, step)
                    probs_evac(NU - 1)
                    ctx_evac(NU - 1)

                @block.vector
                def _(dve):
                    v = nc.vector

                    def bias(u):
                        dve.wait_ge(s["k_projected"], u + 1)
                        v.tensor_tensor(qk_tok[:].rearrange("p m h d -> p (m h d)"), psum[:, 0:2, :].rearrange("p a b -> p (a b)"),
                                        bias_qk[:, group_of(u), :], ALU.add).then_inc(s["qk_biased"], 1)

                    def mean_squares(u):
                        dve.wait_ge(s["qk_squared"], u + 1)
                        v.tensor_reduce(ms[:], qk_rot[:], AX, ALU.add).then_inc(s["ms_summed"], 1)
                        dve.wait_ge(s["ms_summed"], u + 1)
                        v.tensor_scalar(ms_eps[:, 0, :], ms[:, 0, :], 1.0 / HD, EPS_RMS, ALU.mult, ALU.add)
                        v.tensor_scalar(ms_eps[:, 1, :], ms[:, 1, :], EPS_RMS * HD, None, ALU.add).then_inc(s["ms_ready"], 1)

                    def rotate(u):
                        v.tensor_tensor(qk_rot[:], qk_tok[:], bc(rope_same[:, tile_of(u), :, :], 2, HG), ALU.mult).then_inc(s["rot_own"], 1)
                        dve.wait_ge(s["swap_ready"], u + 1)
                        dve.wait_ge(s["rot_own"], u + 1)
                        v.tensor_tensor(qk_rot[:, :, :, 0:ROPE], qk_rot[:, :, :, 0:ROPE], qk_swp[:], ALU.add).then_inc(s["rot_added"], 1)

                    def keep_rstd(u):
                        dve.wait_ge(s["rstd_ready"], u + 1)
                        dve.wait_ge(s["exps_done"], u)
                        v.tensor_copy(rstd_q[:], rstd[:, 1, :]).then_inc(s["rstd_kept"], 1)

                    def maxima(u):
                        dve.wait_ge(s["scored"], u + 1)
                        sc = psum[:, SC_BANK:SC_BANK + HG, :]
                        v.tensor_reduce(mx[:, 0, :], sc[:, :, 0:2 * P], AX, ALU.max)
                        v.tensor_reduce(mx[:, 1, :], sc[:, :, 2 * P:2 * P + C + 1], AX, ALU.max).then_inc(s["max_done"], 1)
                        dve.wait_ge(s["max_done"], u + 1)
                        dve.wait_ge(s["rstd_kept"], u + 1)
                        v.scalar_tensor_tensor(nmx[:], mx[:], -1.0, bc(rstd_q[:], 1, 2), ALU.mult, ALU.mult).then_inc(s["nmax_ready"], 1)

                    def inverses(u):
                        dve.wait_ge(s["exps_done"], u + 1)
                        v.reciprocal(inv[:], sums[:]).then_inc(s["inv_ready"], 1)

                    def keep_sink(u):
                        dve.wait_ge(s["inv_ready"], u + 1)
                        v.tensor_tensor(sink_prob[:, tile_of(u), bass.ds(group_of(u) * HG, HG)], prob[:, :, 2 * P + C], inv[:, 1, :], ALU.mult).then_inc(s["sink_kept"], 1)

                    def low_parts(u):
                        dve.wait_ge(s["k_high"], u + 1)
                        at = bass.ds(par_of(u) * P, P)
                        v.tensor_tensor(keys[:, 1, :, at], psum[:, K_BANK, :].rearrange("p (h t) -> p h t", h=HG), keys[:, 0, :, at].bitcast(F32),
                                        ALU.subtract).then_inc(s["k_ready"], 1)
                        for part in range(2):
                            v.tensor_copy(keys[:, part, :, 2 * P + C], sink_split[:, part, bass.ds(group_of(u) * HG, HG)].bitcast(F32))
                        dve.wait_ge(s["q_high"], u + 1)
                        v.tensor_tensor(qT[:, 1, :, :], psum[:, T_BANK, :].rearrange("p (h t) -> p h t", h=HG), qT[:, 0, :, :].bitcast(F32),
                                        ALU.subtract).then_inc(s["qk_ready"], 1)

                    def low_weights(e):
                        dve.wait_ge(s["w_high"], e + 1)
                        at = bass.ds(tile_of(e) * WCH, WCH)
                        slot = group_of(e + NT) & 1
                        v.tensor_tensor(w_split[:, slot, 1, at], w_stage[:], w_split[:, slot, 0, at].bitcast(F32), ALU.subtract).then_inc(s["w_low"], 1)

                    def low_h(u):
                        dve.wait_ge(s["h_high"], u + 1)
                        v.tensor_tensor(h_now[:, 1, :, :], hT[:, :, bass.ds(tile_of(u) * P, P)], h_now[:, 0, :, :].bitcast(F32),
                                        ALU.subtract).then_inc(s["h_split"], 1)

                    def place_v(u):
                        dve.wait_ge(s["v_out"], u + 1)
                        dve.wait_ge(s["ctx_done"], u)
                        v.tensor_copy(v_ring[:, par_of(u), :], v_new[:, par_of(u), :]).then_inc(s["v_placed"], 1)

                    def accumulate(u):
                        dve.wait_ge(s["out_done"], u + 1)
                        i = tile_of(u)
                        v.tensor_tensor(x_acc[:, i, :], x_acc[:, i, :], psum[:, V_BANK, 0:HID], ALU.add).then_inc(s["acc_done"], 1)

                    def step(u, prev=True, nxt=True, nxt2=True, weights=True):
                        if prev:
                            inverses(u - 1)
                        keep_rstd(u)
                        if nxt:
                            bias(u + 1)
                        if prev:
                            keep_sink(u - 1)
                        if nxt:
                            mean_squares(u + 1)
                            rotate(u + 1)
                        maxima(u)
                        if weights:
                            low_weights(u + 1)
                        if nxt2:
                            low_h(u + 2)
                        place_v(u)
                        if nxt:
                            low_parts(u + 1)
                        if prev:
                            accumulate(u - 1)

                    dve.wait_ge(s["keys_set"], HG)
                    for h in range(HG):
                        v.tensor_tensor(keys[:, 1, h, 2 * P:2 * P + C], ckT[:], keys[:, 0, h, 2 * P:2 * P + C].bitcast(F32), ALU.subtract)
                    dve.wait_ge(s["bias_in"], 16)
                    low_h(0)
                    bias(0)
                    mean_squares(0)
                    rotate(0)
                    low_h(1)
                    low_parts(0)
                    low_weights(0)
                    run_steps(dve, step)
                    inverses(NU - 1)
                    keep_sink(NU - 1)
                    accumulate(NU - 1)

                @block.gpsimd
                def _(pool):
                    g = nc.gpsimd

                    def normalise(u):
                        pool.wait_ge(s["inv_ready"], u + 1)
                        for c, (lo, hi) in enumerate(((0, 2 * P), (2 * P, 2 * P + C))):
                            ins = g.tensor_tensor(prob[:, :, lo:hi], prob[:, :, lo:hi], bc(inv[:, c, :], 2, hi - lo), ALU.mult)
                        ins.then_inc(s["prob_ready"], 1)

                    def swap_parts(u):
                        pool.wait_ge(s["qk_biased"], u + 1)
                        i = tile_of(u)
                        g.tensor_tensor(qk_swp[:, :, :, 0:HALF], qk_tok[:, :, :, HALF:ROPE], bc(rope_swap[:, i, :, 0:HALF], 2, HG), ALU.mult)
                        g.tensor_tensor(qk_swp[:, :, :, HALF:ROPE], qk_tok[:, :, :, 0:HALF], bc(rope_swap[:, i, :, HALF:ROPE], 2, HG),
                                        ALU.mult).then_inc(s["swap_ready"], 1)

                    def scale_k(u):
                        pool.wait_ge(s["ms_ready"], u + 1)
                        pool.wait_ge(s["rstd_kept"], u)
                        g.tensor_tensor(rstd[:], ms_eps[:], half_const[:, 0:2 * HG].rearrange("p (m h) -> p m h", m=2), ALU.pow).then_inc(s["rstd_ready"], 1)
                        pool.wait_ge(s["rot_added"], u + 1)
                        pool.wait_ge(s["rstd_ready"], u + 1)
                        g.tensor_tensor(qk_rot[:, 0, :, :], qk_rot[:, 0, :, :], bc(rstd[:, 0, :], 2, HD), ALU.mult).then_inc(s["rot_ready"], 1)

                    def step(u, prev=True, nxt=True, nxt2=True, weights=True):
                        if prev:
                            normalise(u - 1)
                        if nxt:
                            swap_parts(u + 1)
                            scale_k(u + 1)

                    swap_parts(0)
                    scale_k(0)
                    run_steps(pool, step)
                    normalise(NU - 1)

        att.close()

        with ExitStack() as ff:
            h2 = sb("h2", [P, 2, KH, S], F32R, stack=ff)
            w_ff = sb("w_ff", [P, 2, 2, FCOLS], F32R, stack=ff)
            w_load = sb("w_load", [P, FCOLS], stack=ff)
            pick = sb("pick", [P, FW], F32R, stack=ff)
            combT = sb("combT", [P, 2, S], F32R, stack=ff)
            ff_in = sem("ff_in", ff)
            ff_high = sem("ff_high", ff)
            ff_split = sem("ff_split", ff)
            rt_in = sem("rt_in", ff)

            def load_chunk(sp, c):
                sp.wait_ge(ff_split, c)
                sp.dma_start(w_load[:], d["w_ff"][c]).then_inc(ff_in, 16)

            def split_chunk(pool, c):
                pool.wait_ge(ff_in, 16 * (c + 1))
                nc.gpsimd.tensor_scalar(w_ff[:, c % 2, 0, :], w_load[:], 1.0, 0.0, ALU.mult, ALU.add).then_inc(ff_high, 1)
                pool.wait_ge(ff_high, c + 1)
                nc.gpsimd.tensor_tensor(w_ff[:, c % 2, 1, :], w_load[:], w_ff[:, c % 2, 0, :].bitcast(F32), ALU.subtract).then_inc(ff_split, 1)

            def product(out, lhs, rhs, start, stop):
                nc.tensor.matmul(out, lhs[1], rhs[0], start=start, stop=False)
                nc.tensor.matmul(out, lhs[0], rhs[0], start=False, stop=False)
                return nc.tensor.matmul(out, lhs[0], rhs[1], start=False, stop=stop)

            with ExitStack() as rt:
                h_tok = sb("h_tok2", [P, 2, HID], stack=rt)
                spT = sb("spT", [NH, S], stack=rt)
                lgT = sb("lgT", [EG, S], stack=rt)
                lg = sb("lg", [P, NT, EG], stack=rt)
                pr = sb("pr", [P, NT, E + PADK], stack=rt)
                rep = sb("rep", [P, NT, E + PADK], stack=rt)
                top = sb("top", [P, NT, 8], stack=rt)
                comb = sb("comb", [P, NT, EG], stack=rt)
                w_rt = sb("w_rt", [P, KH * EG], stack=rt)
                w_rt_split = sb("w_rt_split", [P, 2, KH * EG + 1], F32R, stack=rt)
                pick_in = sb("pick_in", [P, FW], stack=rt)
                rt_high = sem("rt_high", rt)
                rt_split = sem("rt_split", rt)
                h2_high = sem("h2_high", rt)
                comb_high = sem("comb_high", rt)
                comb_zeroed = sem("comb_zeroed", rt)
                row_t = sb("row_t", [P, 4, NT], stack=rt)
                sp_turned = sem("sp_turned", rt)
                spT_ready = sem("spT_ready", rt)
                sink_added = sem("sink_added", rt)
                acc_step = sem("acc_step", rt)
                x1_ready = sem("x1_ready", rt)
                stats2 = sem("stats2", rt)
                var2 = sem("var2", rt)
                rstd2 = sem("rstd2", rt)
                step2 = sem("step2", rt)
                norm2 = sem("norm2", rt)
                h2_ready = sem("h2_ready", rt)
                h2_turned = sem("h2_turned", rt)
                h2T_ready = sem("h2T_ready", rt)
                lgT_done = sem("lgT_done", rt)
                lgT_ready = sem("lgT_ready", rt)
                lg_turned = sem("lg_turned", rt)
                lg_shifted = sem("lg_shifted", rt)
                lg_exp = sem("lg_exp", rt)
                comb_ready = sem("comb_ready", rt)
                comb_turned = sem("comb_turned", rt)
                combT_ready = sem("combT_ready", rt)
                with nc.Block() as block:
                    @block.sync
                    def _(sp):
                        sp.dma_start(w_rt[:].rearrange("p (k n) -> p k n", k=KH), d["w_rt"].rearrange("(k p) n -> p k n", p=P)).then_inc(rt_in, 16)
                        sp.dma_start(pick_in[:], d["pick"]).then_inc(rt_in, 16)
                        load_chunk(sp, 0)
                        load_chunk(sp, 1)
                        sp.wait_ge(rt_in, 32)

                    @block.tensor
                    def _(pe):
                        t = nc.tensor
                        for i in range(NT):
                            ins = t.transpose(psum[0:NH, i // 4, (i % 4) * P:(i % 4 + 1) * P], sink_prob[:, i, :], ident[:])
                        ins.then_inc(sp_turned, 1)
                        pe.wait_ge(spT_ready, 1)
                        for i in range(NT):
                            if i >= 2:
                                pe.wait_ge(sink_added, i - 1)
                            t.matmul(psum[:, 4 + i % 2, 0:HID], spT[:, i * P:(i + 1) * P], sink_out[:], start=True, stop=True).then_inc(acc_step, 1)
                        def pair(j):
                            for par in range(2):
                                pe.wait_ge(h2_ready, 2 * j + par + 1)
                                pe.wait_ge(h2T_ready, 2 * j + 0)
                                for k in range(KH):
                                    ins = t.transpose(psum[:, 6 + par, k * P:(k + 1) * P], h_tok[:, par, k * P:(k + 1) * P], ident[:])
                                ins.then_inc(h2_turned, 1)
                        pair(0)
                        with pe.Fori(1, NT // 2) as j:
                            pair(j)
                        pe.wait_ge(h2T_ready, NT)
                        pe.wait_ge(rt_split, 1)
                        for n in range(NTG):
                            for k in range(KH):
                                ins = product(psum[0:EG, n, :], [w_rt_split[:, part, k * EG:(k + 1) * EG] for part in range(2)],
                                              [h2[:, part, k, n * TG:(n + 1) * TG] for part in range(2)], k == 0, k == KH - 1)
                        ins.then_inc(lgT_done, 1)
                        pe.wait_ge(lgT_ready, 1)
                        for i in range(NT):
                            ins = t.transpose(psum[:, 4, i * 32:i * 32 + EG], lgT[:, i * P:(i + 1) * P], ident[0:EG, 0:EG])
                        ins.then_inc(lg_turned, 1)
                        pe.wait_ge(comb_ready, 1)
                        for i in range(NT):
                            ins = t.transpose(psum[0:EG, i // 4, (i % 4) * P:(i % 4 + 1) * P], comb[:, i, :], ident[:])
                        ins.then_inc(comb_turned, 1)

                    @block.scalar
                    def _(act):
                        a = nc.scalar
                        act.wait_ge(sp_turned, 1)
                        a.copy(spT[:], psum[0:NH, 0:4, :].rearrange("p a b -> p (a b)")).then_inc(spT_ready, 1)
                        act.wait_ge(rt_in, 32)
                        a.copy(w_rt_split[:, 0, 0:KH * EG], w_rt[:]).then_inc(rt_high, 1)
                        a.copy(pick[:], pick_in[:])
                        def pair(j):
                            for par in range(2):
                                act.wait_ge(h2_turned, 2 * j + par + 1)
                                a.copy(h2[:, 0, :, bass.ds((2 * j + par) * P, P)],
                                       psum[:, 6 + par, 0:2 * P].rearrange("p (k t) -> p k t", k=KH)).then_inc(h2_high, 1)
                        pair(0)
                        with act.Fori(1, NT // 2) as j:
                            pair(j)
                        act.wait_ge(lgT_done, 1)
                        a.copy(lgT[:], psum[0:EG, 0:4, :].rearrange("p a b -> p (a b)")).then_inc(lgT_ready, 1)
                        act.wait_ge(lg_shifted, 1)
                        a.activation(pr[:, :, 0:E], pr[:, :, 0:E], ACT.Exp)
                        a.activation(lg[:, :, E:EG], lg[:, :, E:EG], ACT.Exp, scale=-1.0).then_inc(lg_exp, 1)
                        act.wait_ge(comb_turned, 1)
                        act.wait_ge(comb_zeroed, 1)
                        a.copy(combT[0:EG, 0, :], psum[0:EG, 0:4, :].rearrange("p a b -> p (a b)")).then_inc(comb_high, 1)

                    @block.gpsimd
                    def _(pool):
                        pool.wait_ge(var2, 1)
                        nc.gpsimd.tensor_tensor(ln_rstd[:], ln_tmp[:, 2, :], half_const[:, 0:NT], ALU.pow).then_inc(rstd2, 1)
                        nc.gpsimd.memset(combT[:].bitcast(F32), 0.0).then_inc(comb_zeroed, 1)
                        nc.gpsimd.memset(hT[:], 0.0)
                        split_chunk(pool, 0)
                        split_chunk(pool, 1)

                    @block.vector
                    def _(dve):
                        v = nc.vector
                        link = chain_on(dve, step2)
                        for i in range(NT):
                            dve.wait_ge(acc_step, i + 1)
                            v.tensor_tensor(x_acc[:, i, :], x_acc[:, i, :], psum[:, 4 + i % 2, 0:HID], ALU.add).then_inc(sink_added, 1)
                        def tile(i):
                            dve.wait_ge(sink_added, NT)
                            v.tensor_tensor(x_acc[:, i, :], x_acc[:, i, :], out_bias[:], ALU.add).then_inc(x1_ready, 1)
                            dve.wait_ge(x1_ready, i + 1)
                            v.bn_stats(stats[:, i, :], x_acc[:, i, :]).then_inc(stats2, 1)
                        tile(0)
                        with dve.Fori(1, NT) as i:
                            tile(i)
                        layer_norm_stats_small(link, lambda: dve.wait_ge(stats2, NT)).then_inc(var2, 1)
                        dve.wait_ge(rt_high, 1)
                        v.tensor_tensor(w_rt_split[:, 1, 0:KH * EG], w_rt[:], w_rt_split[:, 0, 0:KH * EG].bitcast(F32), ALU.subtract).then_inc(rt_split, 1)
                        dve.wait_ge(rstd2, 1)

                        def low_h2(i, par):
                            dve.wait_ge(h2_high, i + 1)
                            at = bass.ds(i * P, P)
                            v.tensor_tensor(h2[:, 1, :, at], psum[:, 6 + par, 0:2 * P].rearrange("p (k t) -> p k t", k=KH),
                                            h2[:, 0, :, at].bitcast(F32), ALU.subtract).then_inc(h2T_ready, 1)

                        def pair(j):
                            for par in range(2):
                                i = 2 * j + par
                                h = h_tok[:, par, :]
                                dve.wait_ge(h2_turned, 2 * j + 0)
                                v.tensor_scalar(h, x_acc[:, i, :], ln_mean[:, bass.ds(i, 1)], ln_rstd[:, bass.ds(i, 1)],
                                                ALU.subtract, ALU.mult).then_inc(norm2, 1)
                                dve.wait_ge(norm2, 4 * j + 2 * par + 1)
                                v.tensor_tensor(h, h, mod[:, 4, :], ALU.mult).then_inc(norm2, 1)
                                dve.wait_ge(norm2, 4 * j + 2 * par + 2)
                                v.tensor_tensor(h, h, mod[:, 3, :], ALU.add).then_inc(h2_ready, 1)
                            for par in range(2):
                                low_h2(2 * j + par, par)
                        pair(0)
                        with dve.Fori(1, NT // 2) as j:
                            pair(j)
                        link(v.memset(pr[:], -1.0))
                        dve.wait_ge(lg_turned, 1)
                        link(v.tensor_copy(lg[:], psum[:, 4, :].rearrange("p (i e) -> p i e", e=32)[:, :, 0:EG]))
                        link(v.tensor_reduce(row_t[:, 0, :], lg[:, :, 0:E], AX, ALU.max))
                        v.tensor_tensor(pr[:, :, 0:E], lg[:, :, 0:E], bc(row_t[:, 0, :], 2, E), ALU.subtract).then_inc(lg_shifted, 1)
                        dve.wait_ge(lg_exp, 1)
                        link(v.tensor_reduce(row_t[:, 1, :], pr[:, :, 0:E], AX, ALU.add))
                        link(v.reciprocal(row_t[:, 2, :], row_t[:, 1, :]))
                        link(v.tensor_tensor(pr[:, :, 0:E], pr[:, :, 0:E], bc(row_t[:, 2, :], 2, E), ALU.mult))
                        for i in range(NT):
                            ins = v.max(top[:, i, :], pr[:, i, :])
                        link(ins)
                        link(v.memset(top[:, :, TOPK:8], -1.0))
                        for i in range(NT):
                            ins = v.match_replace(rep[:, i, :], top[:, i, :], pr[:, i, :], -2.0)
                        link(ins)
                        link(v.tensor_tensor(comb[:, :, 0:E], rep[:, :, 0:E], pr[:, :, 0:E], ALU.not_equal))
                        link(v.tensor_tensor(comb[:, :, 0:E], comb[:, :, 0:E], pr[:, :, 0:E], ALU.mult))
                        link(v.tensor_reduce(row_t[:, 1, :], comb[:, :, 0:E], AX, ALU.add))
                        link(v.tensor_scalar(row_t[:, 1, :], row_t[:, 1, :], 1e-9, None, ALU.max))
                        link(v.reciprocal(row_t[:, 2, :], row_t[:, 1, :]))
                        link(v.tensor_tensor(comb[:, :, 0:E], comb[:, :, 0:E], bc(row_t[:, 2, :], 2, E), ALU.mult))
                        link(v.tensor_scalar(lg[:, :, E:EG], lg[:, :, E:EG], 1.0, None, ALU.add))
                        v.reciprocal(comb[:, :, E:EG], lg[:, :, E:EG]).then_inc(comb_ready, 1)
                        dve.wait_ge(comb_high, 1)
                        v.tensor_tensor(combT[0:EG, 1, :], psum[0:EG, 0:4, :].rearrange("p a b -> p (a b)"), combT[0:EG, 0, :].bitcast(F32), ALU.subtract).then_inc(combT_ready, 1)

            y_acc = hT
            silu = sb("silu", [P, 2, TG], stack=ff)
            su = sb("su", [P, 2, TG], stack=ff)
            act_w = sb("act_w", [P, 2, TG], stack=ff)
            act_split = sb("act_split", [P, 2, 2, TG], F32R, stack=ff)
            y_part = sb("y_part", [P, KH, TG], stack=ff)
            yT = sb("yT", [P, KH, TG], stack=ff)
            y_tok = sb("y_tok", [P, 2, 2, HID], stack=ff)
            y_out = sb("y_out", [P, 2, 2, HID], stack=ff)
            names = ("gate_done up_done pick_done silu_done su_done act_ready act_high act_low down_done part_ready part_added "
                     "yT_ready y_turned y_gated y_ready y_stored0 y_stored1")
            f = {n: sem(n, ff) for n in names.split()}
            G_BANK, U_BANK, Y_BANK, W_BANK, X_BANK = 0, 2, 4, 6, 7

            def group_base(c, n):
                return (c * NTG + n) * CT

            def run_groups(eng, body):
                for c in range(NCH - 1):
                    if c == 0:
                        body(0, 0)
                    with eng.Fori(1 if c == 0 else 0, NTG - 1) as n:
                        body(c, n)
                    body(c, NTG - 1)
                for n in range(NTG):
                    body(NCH - 1, n)

            with nc.Block() as block:
                @block.sync
                def _(sp):
                    for c in range(2, NCH):
                        load_chunk(sp, c)
                    out = d["out"].rearrange("(t p) n -> p t n", p=P)
                    for r in range(2 * NTG):
                        sp.wait_ge(f["y_ready"], r + 1)
                        sp.dma_start(out[:, 2 * r:2 * r + 2, :], y_out[:, r % 2, :, :]).then_inc(f[f"y_stored{r % 2}"], 16)
                    for b in range(2):
                        sp.wait_ge(f[f"y_stored{b}"], 16 * NTG)

                @block.gpsimd
                def _(pool):
                    for c in range(2, NCH):
                        pool.wait_ge(f["down_done"], (c - 1) * NTG * CT)
                        split_chunk(pool, c)

                @block.tensor
                def _(pe):
                    t = nc.tensor

                    def up(c, n, j):
                        at = bass.ds(n * TG, TG)
                        rhs = [[h2[:, part, k, at] for part in range(2)] for k in range(KH)]
                        b, tile = j % 2, group_base(c, n) + j
                        pe.wait_ge(ff_split, c + 1)
                        if not (isinstance(tile, int) and tile < 2):
                            pe.wait_ge(f["act_ready"], tile - 1)
                        for m, bank, done in ((0, G_BANK, "gate_done"), (1, U_BANK, "up_done")):
                            for k in range(KH):
                                col = m * GU + k * CT * P + j * P
                                ins = product(psum[:, bank + b, :], [w_ff[:, c % 2, part, col:col + P] for part in range(2)], rhs[k],
                                              k == 0, k == KH - 1)
                            ins.then_inc(f[done], 1)
                        pe.wait_ge(f["act_ready"], tile)
                        row = (c * CT + j) * P
                        t.matmul(psum[:, W_BANK, :], pick[:, row:row + P], combT[:, 0, at], start=True, stop=False)
                        t.matmul(psum[:, W_BANK, :], pick[:, row:row + P], combT[:, 1, at], start=False, stop=True).then_inc(f["pick_done"], 1)

                    def down(c, n, j):
                        tile = group_base(c, n) + j
                        if j == 0:
                            pe.wait_ge(f["part_ready"], c * NTG + n)
                        pe.wait_ge(f["act_high"], tile + 1)
                        w = [[w_ff[:, c % 2, part, 2 * GU + j * HID + m * P:2 * GU + j * HID + (m + 1) * P] for part in range(2)] for m in range(KH)]
                        for m in range(KH):
                            t.matmul(psum[:, Y_BANK + m, :], w[m][1], act_split[:, j % 2, 0, :], start=(j == 0), stop=False)
                            t.matmul(psum[:, Y_BANK + m, :], w[m][0], act_split[:, j % 2, 0, :], start=False, stop=False)
                        pe.wait_ge(f["act_low"], tile + 1)
                        for m in range(KH):
                            ins = t.matmul(psum[:, Y_BANK + m, :], w[m][0], act_split[:, j % 2, 1, :], start=False, stop=(j == CT - 1))
                        ins.then_inc(f["down_done"], 1)

                    def turn_y(r):
                        pe.wait_ge(f["yT_ready"], r // 2 + 1)
                        pe.wait_ge(f["y_gated"], r)
                        for q in range(2):
                            for k in range(KH):
                                at = (r % 2) * 2 * P + q * P
                                ins = t.transpose(psum[:, X_BANK, q * HID + k * P:q * HID + (k + 1) * P], yT[:, k, at:at + P], ident[:])
                        ins.then_inc(f["y_turned"], 1)

                    def body(c, n):
                        end = isinstance(n, int) and n == NTG - 1
                        for j in range(CT):
                            if j + 1 < CT:
                                up(c, n, j + 1)
                            elif not end:
                                up(c, n + 1, 0)
                            elif c + 1 < NCH:
                                up(c + 1, 0, 0)
                            down(c, n, j)
                            if c == NCH - 1 and n > 0 and j in (1, 2):
                                turn_y(2 * (n - 1) + j - 1)

                    up(0, 0, 0)
                    run_groups(pe, body)
                    turn_y(2 * NTG - 2)
                    turn_y(2 * NTG - 1)

                @block.scalar
                def _(act):
                    a = nc.scalar

                    def gate(tile, j):
                        act.wait_ge(f["gate_done"], tile + 1)
                        if not (isinstance(tile, int) and tile < 2):
                            act.wait_ge(f["su_done"], tile - 1)
                        a.activation(silu[:, j % 2, :], psum[:, G_BANK + j % 2, :], ACT.Silu).then_inc(f["silu_done"], 1)

                    def high(tile, j):
                        act.wait_ge(f["act_ready"], tile + 1)
                        if not (isinstance(tile, int) and tile < 2):
                            act.wait_ge(f["down_done"], tile - 1)
                        a.copy(act_split[:, j % 2, 0, :], act_w[:, j % 2, :]).then_inc(f["act_high"], 1)

                    def take_part(c, n):
                        act.wait_ge(f["down_done"], group_base(c, n) + CT)
                        if c == NCH - 1 and n > 0:
                            act.wait_ge(f["yT_ready"], n)
                        else:
                            act.wait_ge(f["part_added"], c * NTG + n)
                        a.copy(y_part[:].rearrange("p k t -> p (k t)"), psum[:, Y_BANK:Y_BANK + 2, :].rearrange("p a b -> p (a b)")).then_inc(f["part_ready"], 1)

                    def body(c, n):
                        last = isinstance(n, int) and n == NTG - 1 and c == NCH - 1
                        for j in range(CT):
                            tile = group_base(c, n) + j
                            high(tile, j)
                            if not (last and j == CT - 1):
                                gate(tile + 1, (j + 1) % CT)
                        take_part(c, n)

                    gate(0, 0)
                    run_groups(act, body)

                @block.vector
                def _(dve):
                    v = nc.vector

                    def weigh(c, n, j):
                        tile = group_base(c, n) + j
                        dve.wait_ge(f["silu_done"], tile + 1)
                        dve.wait_ge(f["up_done"], tile + 1)
                        v.tensor_tensor(su[:, j % 2, :], silu[:, j % 2, :], psum[:, U_BANK + j % 2, :], ALU.mult).then_inc(f["su_done"], 1)
                        dve.wait_ge(f["su_done"], tile + 1)
                        dve.wait_ge(f["pick_done"], tile + 1)
                        v.tensor_tensor(act_w[:, j % 2, :], su[:, j % 2, :], psum[:, W_BANK, :], ALU.mult).then_inc(f["act_ready"], 1)
                        dve.wait_ge(f["act_high"], tile + 1)
                        v.tensor_tensor(act_split[:, j % 2, 1, :], act_w[:, j % 2, :], act_split[:, j % 2, 0, :].bitcast(F32),
                                        ALU.subtract).then_inc(f["act_low"], 1)

                    def add_part(p, slot):
                        dve.wait_ge(f["part_ready"], p + 1)
                        if not (isinstance(p, int) and p == 0):
                            dve.wait_ge(f["part_added"], p)
                        at = bass.ds(slot * TG, TG)
                        v.tensor_tensor(y_acc[:, :, at], y_acc[:, :, at], y_part[:], ALU.add).then_inc(f["part_added"], 1)

                    def complete(n):
                        p = (NCH - 1) * NTG + n
                        dve.wait_ge(f["part_ready"], p + 1)
                        dve.wait_ge(f["part_added"], (NCH - 1) * NTG)
                        if n:
                            dve.wait_ge(f["y_turned"], 2 * n)
                        v.tensor_tensor(yT[:], y_acc[:, :, n * TG:(n + 1) * TG], y_part[:], ALU.add).then_inc(f["yT_ready"], 1)

                    def finish(r):
                        b = r % 2
                        dve.wait_ge(f["y_turned"], r + 1)
                        if r >= 2:
                            dve.wait_ge(f["y_ready"], r - 1)
                        v.tensor_tensor(y_tok[:, b, :, :], psum[:, X_BANK, :].rearrange("p (q n) -> p q n", q=2), bc(mod[:, 5, :], 1, 2),
                                        ALU.mult).then_inc(f["y_gated"], 1)
                        dve.wait_ge(f["y_gated"], r + 1)
                        if r >= 2:
                            dve.wait_ge(f[f"y_stored{b}"], 16 * (r // 2))
                        v.tensor_tensor(y_out[:, b, :, :], y_tok[:, b, :, :], x_acc[:, 2 * r:2 * r + 2, :], ALU.add).then_inc(f["y_ready"], 1)

                    def body(c, n):
                        for j in range(CT):
                            weigh(c, n, j)
                            if j == 0 and c == NCH - 1 and n > 0:
                                complete(n - 1)
                            elif j == 0 and not (c == 0 and isinstance(n, int) and n == 0):
                                add_part(c * NTG + n - 1, (n + NTG - 1) & (NTG - 1))
                            if c == NCH - 1 and n > 0 and j in (2, 3):
                                finish(2 * (n - 1) + j - 2)

                    run_groups(dve, body)
                    complete(NTG - 1)
                    finish(2 * NTG - 2)
                    finish(2 * NTG - 1)


def shape_constants():
    bf16 = mybir.dt.np(BF16)
    f = np.float32
    half = np.arange(HALF, dtype=f)
    inv_freq = (f(1.0) / np.power(f(10000.0), half * f(2.0) / f(ROPE))).astype(f)
    pos = np.arange(S, dtype=f).reshape(NT, P)
    ends = (np.arange(C, dtype=f) * R + (R - 1)).reshape(1, C)
    ang = np.concatenate([pos, ends])[:, :, None] * inv_freq
    trig = np.stack([np.cos(ang), np.sin(ang), -np.sin(ang)], 2).transpose(1, 0, 2, 3)
    s = np.arange(P)[:, None]
    t = np.arange(P)[None, :]
    mask_keys = np.zeros((P, 4, 2, P), f)
    cur, prev = np.where(t <= s, 0, MASKED), np.where(s + P - t <= WIN, 0, MASKED)
    mask_keys[:, 0, 0], mask_keys[:, 0, 1] = cur, prev
    mask_keys[:, 1, 1], mask_keys[:, 1, 0] = cur, prev
    mask_keys[:, 2, 0], mask_keys[:, 2, 1] = cur, MASKED
    mask_ent = np.zeros((P, NT, LW - 2 * P), f)
    for i in range(NT):
        mask_ent[:, i, 0:C] = np.where(R * t + R - 1 <= P * i + s, 0, MASKED)
    owner = np.minimum(np.arange(FW) // I_MOE, E)
    pick = (owner[None, :] == np.arange(P)[:, None]).astype(f)
    return {"ident": np.eye(P, dtype=f), "ident_b": np.eye(P).astype(bf16), "pick": pick,
            "trig": np.ascontiguousarray(trig.astype(f)), "mask_keys": mask_keys.reshape(P, 4, 2 * P).astype(bf16), "mask_ent": mask_ent.astype(bf16)}


def kernel(**inputs):
    import concourse.bacc as bacc
    from concourse.bass_utils import run_bass_kernel_spmd

    a = {k.replace("L0_attn_", "").replace("L0_ffn_", ""): np.asarray(v) for k, v in inputs.items()}
    zeros = np.zeros((HID, FW - E * I_MOE - I_SH), np.float32)

    def up_layout(experts, shared):
        return np.concatenate([experts.transpose(1, 0, 2).reshape(HID, E * I_MOE), shared, zeros], 1)

    def up_chunks(w):
        return w.reshape(KH, P, NCH, CT * P).transpose(2, 1, 0, 3).reshape(NCH, P, GU)

    down = np.concatenate([a["w_down"].reshape(E * I_MOE, HID), a["sh_down"], zeros.T])
    w_ff = np.concatenate([up_chunks(up_layout(a["w_gate"], a["sh_gate"])), up_chunks(up_layout(a["w_up"], a["sh_up"])),
                           down.reshape(NCH, CT, P, HID).transpose(0, 2, 1, 3).reshape(NCH, P, CT * HID)], 2)
    w_groups = np.stack([a["Wlk"], a["Wq"], a["Wlv"]]).reshape(3, KH, P, NG, GW).transpose(3, 2, 0, 1, 4)
    w_groups = w_groups.reshape(NG, P, NT, WCH).transpose(0, 2, 1, 3)
    arrays = {
        "x": a["hidden_states"].reshape(S, HID), "w_groups": w_groups, "Wo": a["Wo"],
        "Wk": a["Wk"], "Wv": a["Wv"], "wcT": a["Wc"].reshape(KH, P).T, "bc": a["bc"],
        "bias_qk": np.concatenate([a["blk"].reshape(NG, GW), a["bq"].reshape(NG, GW)], 1),
        "rows": np.stack([a["bk"], a["bv"], a["kn_w"], a["qn_w"]]),
        "sink_kT": a["sink_k"].T, "sink_vT": a["sink_v"].T, "blvT": a["blv"].reshape(NH, HD).T, "bo": a["bo"],
        "w_rt": np.concatenate([a["router_w"].T, a["sh_gate_w"]], 1),
        "w_ff": w_ff,
        "cT": a["L0_c"].reshape(KH, P).T, "wmod": a["L0_wmod"],
    }
    arrays.update(shape_constants())
    nc = bacc.Bacc("TRN2", target_bir_lowering=False, num_devices=1)
    d, feed = {}, {}
    for name, arr in arrays.items():
        arr = np.ascontiguousarray(arr)
        feed[f"in_{name}"] = arr
        d[name] = nc.dram_tensor(f"in_{name}", arr.shape, mybir.dt.from_np(arr.dtype), kind="ExternalInput").ap()
    d["out"] = nc.dram_tensor("out_x", (S, HID), F32, kind="ExternalOutput").ap()
    build(nc, d)
    r = run_bass_kernel_spmd(nc, [feed], core_ids=[0])
    return r.results[0]["out_x"].reshape(1, S, HID)
```

```python
from contextlib import ExitStack

import numpy as np

import concourse.bass as bass
from concourse import mybir

P = 128
S = 2048
HID = 256
KH = HID // P
NH = 16
HD = 128
NT = S // P
HG = 4
NG = NH // HG
NU = NG * NT
GW = HG * HD
R = 16
C = S // R
WIN = 128
ROPE = HD // 2
HALF = ROPE // 2
EPS_RMS = 1e-6
EPS_LN = 1e-5
MASKED = -1e30
E = 16
TOPK = 4
I_MOE = 176
I_SH = 704
NF = -(-(E * I_MOE + I_SH) // P)
FW = NF * P
EG = E + 1
PADK = TOPK
TG = 512
NTG = S // TG
TPG = TG // P
LOW_ROW = 32
BIAS_ROW = NH
CT = 4
NCH = NF // CT
GU = KH * CT * P
FCOLS = 2 * GU + CT * HID
LW = 2 * P + C + 2
WCOLS = 3 * KH * GW
OCH = HG * HID // NT
WCH = WCOLS // NT

F32 = mybir.dt.float32
BF16 = mybir.dt.bfloat16
F32R = mybir.dt.float32r
ALU = mybir.AluOpType
ACT = mybir.ActivationFunctionType
AX = mybir.AxisListType.X


def bc(ap, dim, n):
    ap = ap.unsqueeze(dim)
    shape = list(ap.shape)
    shape[dim] = n
    return ap.to_broadcast(shape)


def build(nc, d):
    with ExitStack() as ctx:
        def sb(name, shape, dt=F32, stack=ctx):
            return stack.enter_context(nc.sbuf_tensor(name, shape, dt))

        def sem(name, stack=ctx):
            return stack.enter_context(nc.semaphore(name))

        psum = ctx.enter_context(nc.psum_tensor("psum", [P, 8, 512], F32))

        ident = sb("ident", [P, P])
        gates = sb("gates", [P, 2, HID])
        x_acc = sb("x_acc", [P, NT, HID])
        hT = sb("hT", [P, KH, S])
        modT = sb("modT", [P, 2, 2, KH])
        sink_out = sb("sink_out", [P, HID])
        sink_prob = sb("sink_prob", [P, NT, NH + 1])
        half_const = sb("half_const", [P, 32])
        stats = sb("stats", [P, NT, 6])
        ln_mean = sb("ln_mean", [P, NT])
        ln_rstd = sb("ln_rstd", [P, NT])
        ln_tmp = sb("ln_tmp", [P, 3, NT])

        def moments(chain, half):
            dv = nc.vector
            at = slice(half * NT // 2, (half + 1) * NT // 2)
            me, m2e, mo, m2o = (stats[:, at, c] for c in (1, 2, 4, 5))
            a, b, v = (ln_tmp[:, c, at] for c in range(3))
            dv.tensor_tensor(b, me, mo, ALU.subtract)
            chain(dv.tensor_tensor(a, me, mo, ALU.add))
            dv.tensor_scalar(ln_mean[:, at], a, 0.5, None, ALU.mult)
            chain(dv.tensor_tensor(b, b, b, ALU.mult))
            dv.tensor_tensor(a, m2e, m2o, ALU.add)
            chain(dv.tensor_scalar(b, b, 0.25, EPS_LN, ALU.mult, ALU.add))
            return dv.scalar_tensor_tensor(v, a, 1.0 / HID, b, ALU.mult, ALU.add)

        def rstd_half(half):
            at = slice(half * NT // 2, (half + 1) * NT // 2)
            return nc.gpsimd.tensor_tensor(ln_rstd[:, at], ln_tmp[:, 2, at], half_const[:, 0:NT // 2], ALU.pow)

        def standardise(out, i):
            return nc.vector.tensor_scalar(out, x_acc[:, i, :], ln_mean[:, i:i + 1], ln_rstd[:, i:i + 1], ALU.subtract, ALU.mult)

        def turn_group(src, bank):
            for k in range(KH):
                for j in range(TPG):
                    ins = nc.tensor.transpose(psum[:, bank + k, j * P:(j + 1) * P], src[:, j, k * P:(k + 1) * P], ident[:])
            return ins

        def chain_on(eng, s):
            n = [0]

            def link(ins):
                n[0] += 1
                ins.then_inc(s, 1)
                eng.wait_ge(s, n[0])
            return link

        att = ctx.enter_context(ExitStack())

        w_split = sb("w_split", [P, 2, 2, WCOLS], F32R, stack=att)
        w_out = sb("w_out", [P, 2, 2, HG * HID], F32R, stack=att)
        bias_qk = sb("bias_qk", [P, NG, 2 * GW], stack=att)
        rope_same = sb("rope_same", [P, NT, 2, ROPE], stack=att)
        norm_rest = sb("norm_rest", [P, 2, HD - ROPE], stack=att)
        rope_swap = sb("rope_swap", [P, NT, 2, ROPE], stack=att)
        ident_b = sb("ident_b", [P, P], BF16, stack=att)
        ckT = sb("ckT", [P, C], stack=att)
        cv_split = sb("cv_split", [P, 2, HD], F32R, stack=att)
        sink_split = sb("sink_split", [P, 2, NH], F32R, stack=att)
        keys = sb("keys", [P, 2, HG, LW], F32R, stack=att)
        v_ring = sb("v_ring", [P, 2, GW], stack=att)

        with ExitStack() as pre:
            cT = sb("cT", [P, KH], stack=pre)
            c_tmp = sb("c_tmp", [P, 3, KH], stack=pre)
            c_rep = sb("c_rep", [P, KH, P], stack=pre)
            w_mod = sb("w_mod", [P, KH, 6 * HID], stack=pre)
            mod = sb("mod", [P, 6, HID], stack=pre)
            cv = sb("cv", [P, HD], stack=pre)
            cv_ready = sem("cv_ready", pre)
            cv_high = sem("cv_high", pre)
            wcT = sb("wcT", [P, KH], stack=pre)
            wc_rep = sb("wc_rep", [P, KH, P], stack=pre)
            b_c = sb("b_c", [P, 1], stack=pre)
            w_kv = sb("w_kv", [P, 2, KH, HD], stack=pre)
            rows = sb("rows", [P, 4, HD], stack=pre)
            trig = sb("trig", [P, NT + 1, 3, HALF], stack=pre)
            sink_vT = sb("sink_vT", [P, NH], stack=pre)
            blvT = sb("blvT", [P, NH], stack=pre)
            bo_row = sb("bo_row", [P, HID], stack=pre)
            spare = bias_qk[:].rearrange("p g n -> p (g n)")
            sv_bias = spare[:, 0:NH * P].rearrange("p (h t) -> p h t", h=NH)
            pool_w = spare[:, NH * P:NH * P + S].rearrange("p (c r) -> p c r", r=R)
            wo_gated = sb("wo_gated", [P, 2, HG, HID], stack=pre)
            wo_buf = (0, 1, 1, 0)
            wo_load = (1, 1, 2, 2)
            work = sb("work", [P, 2 * TPG * HID], stack=pre)
            h_tok = work[:].rearrange("p (b j n) -> p b j n", b=2, j=TPG)
            gate_tmp = sb("gate_tmp", [P, 2, 2, HID], stack=pre)
            prod = work[:].rearrange("p (k c r) -> p k c r", k=KH, r=R)
            pool_m = sb("pool_m", [P, 2, C], stack=pre)
            entT = sb("entT", [P, KH, C], stack=pre)
            ck = sb("ck", [P, 2, HD], stack=pre)
            ck_t = sb("ck_t", [P, 4], stack=pre)
            ck_r = sb("ck_r", [P, 4, HALF], stack=pre)

            sink_kT = sb("sink_kT", [P, NH], stack=pre)
            w_first = w_mod[:].rearrange("p k n -> p (k n)")

            c_in = sem("c_in", pre)
            wmod_in = [sem(f"wmod_in{n}", pre) for n in range(3)]
            w_high = sem("w_high", pre)
            x_in = [sem("x_in0", pre), sem("x_in1", pre)]
            ident_in = sem("ident_in", pre)
            bo_zeroed = sem("bo_zeroed", pre)
            scale_ready = sem("scale_ready", pre)
            mod_turned = sem("mod_turned", pre)
            modT_ready = sem("modT_ready", pre)
            logits_out = sem("logits_out", pre)
            sv_ready = sem("sv_ready", pre)
            prod_ready = sem("prod_ready", pre)
            prod_used = sem("prod_used", pre)
            tables_in = sem("tables_in", pre)
            wo_in = [sem("wo_in0", pre), sem("wo_in1", pre)]
            sink_in = sem("sink_in", pre)
            wo_used = sem("wo_used", pre)
            out_high = sem("out_high", pre)
            out_low = sem("out_low", pre)
            late_in = sem("late_in", pre)
            exp_c = sem("exp_c", pre)
            c_spread = sem("c_spread", pre)
            mod_done = sem("mod_done", pre)
            mod_raw = sem("mod_raw", pre)
            dve_step = sem("dve_step", pre)
            stats_done = sem("stats_done", pre)
            var_done = sem("var_done", pre)
            rstd_done = sem("rstd_done", pre)
            pool_const = sem("pool_const", pre)
            h_ready = sem("h_ready", pre)
            h_turned = sem("h_turned", pre)
            hT_ready = sem("hT_ready", pre)
            wc_ready = sem("wc_ready", pre)
            logits_done = sem("logits_done", pre)
            shifted = sem("shifted", pre)
            exp_pool = sem("exp_pool", pre)
            ent_ready = sem("ent_ready", pre)
            kv_done = sem("kv_done", pre)
            ck_biased = sem("ck_biased", pre)
            ck_ss = sem("ck_ss", pre)
            ck_var = sem("ck_var", pre)
            ck_rstd = sem("ck_rstd", pre)
            ck_ready = sem("ck_ready", pre)
            ck_turned = sem("ck_turned", pre)
            ckT_ready = sem("ckT_ready", pre)
            wo_ready = sem("wo_ready", pre)
            evac = sem("evac", pre)
            zeroed = sem("zeroed", pre)

            with nc.Block() as block:
                @block.sync
                def _(sp):
                    sp.dma_start(cT[:], d["cT"]).then_inc(c_in, 16)
                    for n in range(3):
                        at = slice(n * 2 * HID, (n + 1) * 2 * HID)
                        sp.dma_start(w_mod[:, :, at], d["wmod"].rearrange("(k p) n -> p k n", p=P)[:, :, at]).then_inc(wmod_in[n], 16)
                    sp.dma_start(ident[:], d["ident"]).then_inc(ident_in, 16)
                    for half in range(2):
                        at = slice(half * NT // 2, (half + 1) * NT // 2)
                        sp.dma_start(x_acc[:, at, :], d["x"].rearrange("(t p) n -> p t n", p=P)[:, at, :]).then_inc(x_in[half], 16)
                    def load_wo(g):
                        sp.dma_start(wo_gated[:, wo_buf[g], :, :], d["Wo"][g * GW:(g + 1) * GW, :].rearrange("(h p) n -> p h n", p=P)).then_inc(wo_in[wo_buf[g]], 16)

                    load_wo(0)
                    load_wo(1)
                    sp.dma_start(sink_vT[:], d["sink_vT"]).then_inc(sink_in, 16)
                    sp.dma_start(blvT[:], d["blvT"]).then_inc(sink_in, 16)
                    sp.wait_ge(bo_zeroed, 1)
                    sp.dma_start(bo_row[BIAS_ROW:BIAS_ROW + 1, :], d["bo"]).then_inc(sink_in, 16)
                    sp.wait_ge(mod_turned, 1)
                    sp.dma_start(w_first.rearrange("p (c n) -> p c n", c=NT), d["w_groups"][0].rearrange("c p n -> p c n")).then_inc(late_in, 16)
                    sp.dma_start(sink_kT[:], d["sink_kT"]).then_inc(late_in, 16)
                    sp.dma_start(ident_b[:], d["ident_b"]).then_inc(late_in, 16)
                    sp.wait_ge(wo_used, 2)
                    load_wo(2)
                    sp.wait_ge(out_low, 1)
                    load_wo(3)
                    sp.wait_ge(late_in, 16 * 3)

                @block.scalar
                def _(act):
                    act.dma_start(wcT[:], d["wcT"]).then_inc(tables_in, 16)
                    act.dma_start(b_c[:], d["bc"].partition_broadcast(P)).then_inc(tables_in, 16)
                    act.dma_start(w_kv[:, 0, :, :], d["Wk"].rearrange("(k p) n -> p k n", p=P)).then_inc(tables_in, 16)
                    act.dma_start(w_kv[:, 1, :, :], d["Wv"].rearrange("(k p) n -> p k n", p=P)).then_inc(tables_in, 16)
                    act.dma_start(rows[:], d["rows"].partition_broadcast(P)).then_inc(tables_in, 16)
                    act.dma_start(trig[:], d["trig"]).then_inc(tables_in, 16)
                    act.wait_ge(c_in, 16)
                    nc.scalar.activation(c_tmp[:, 0, :], cT[:], ACT.Exp, scale=-1.0).then_inc(exp_c, 1)
                    act.wait_ge(mod_done, 1)
                    nc.scalar.copy(mod[:].rearrange("p a b -> p (a b)"), psum[:, 0:3, :].rearrange("p a b -> p (a b)")).then_inc(mod_raw, 1)

                    def modulate(n):
                        act.wait_ge(h_turned, n + 1)
                        for k in range(KH):
                            ins = nc.scalar.activation(hT[:, k, n * TG:(n + 1) * TG], psum[:, 4 + 2 * (n % 2) + k, :], ACT.Identity,
                                                       bias=modT[:, 0, 0, k:k + 1], scale=modT[:, 0, 1, k:k + 1])
                        ins.then_inc(hT_ready, 1)

                    def logits_evac(n):
                        act.wait_ge(logits_done, n + 1)
                        nc.scalar.activation(pool_w[:, n * TG // R:(n + 1) * TG // R, :].rearrange("p c r -> p (c r)"), psum[:, n, :],
                                             ACT.Identity, bias=b_c[:, 0:1]).then_inc(logits_out, 1)

                    act.wait_ge(modT_ready, 1)
                    act.wait_ge(tables_in, 96)
                    for n in range(NTG):
                        modulate(n)
                        if n >= 1:
                            logits_evac(n - 1)
                    logits_evac(NTG - 1)
                    nc.scalar.copy(norm_rest[:], rows[:, 2:4, ROPE:HD])
                    act.wait_ge(wo_ready, 1)
                    nc.scalar.copy(w_out[:, 0, 0, :], wo_gated[:, 0, :, :].rearrange("p h n -> p (h n)")).then_inc(out_high, 1)
                    for half in range(2):
                        act.wait_ge(shifted, half + 1)
                        part = pool_w[:, half * C // 2:(half + 1) * C // 2, :]
                        nc.scalar.activation(part, part, ACT.Exp).then_inc(exp_pool, 1)
                    act.wait_ge(late_in, 48)
                    nc.scalar.copy(w_split[:, 0, 0, :], w_first)
                    nc.scalar.copy(sink_split[:, 0, :], sink_kT[:]).then_inc(w_high, 1)
                    act.wait_ge(ck_biased, 1)
                    nc.scalar.activation(ck[:, 1, :], ck[:, 0, :], ACT.Square, accum_out=ck_t[:, 0:1]).then_inc(ck_ss, 1)
                    act.wait_ge(cv_ready, 1)
                    nc.scalar.copy(cv_split[:, 0, :], cv[:]).then_inc(cv_high, 1)
                    act.wait_ge(ck_turned, 1)
                    nc.scalar.copy(ckT[:], psum[:, 6, 0:C]).then_inc(ckT_ready, 1)

                @block.tensor
                def _(pe):
                    pe.wait_ge(c_spread, 1)
                    for n in range(3):
                        pe.wait_ge(wmod_in[n], 16)
                        for k in range(KH):
                            last = nc.tensor.matmul(psum[:, n, :], c_rep[:, k, :], w_mod[:, k, n * 512:(n + 1) * 512],
                                                    start=(k == 0), stop=(k == KH - 1))
                    last.then_inc(mod_done, 1)
                    pe.wait_ge(ident_in, 16)
                    pe.wait_ge(scale_ready, 1)
                    for n, row in enumerate((0, 3)):
                        for c in range(2):
                            for k in range(KH):
                                col = ((n * 2 + c) * KH + k) * (P // 2)
                                last = nc.tensor.transpose(psum[0:P, 3, col:col + P // 2], mod[0:P // 2, row + c, k * P:(k + 1) * P], ident[0:P // 2, 0:P // 2])
                    last.then_inc(mod_turned, 1)

                    def logits(n):
                        pe.wait_ge(wc_ready, 1)
                        pe.wait_ge(hT_ready, n + 1)
                        for k in range(KH):
                            last = nc.tensor.matmul(psum[:, n, :], wc_rep[:, k, :], hT[:, k, n * TG:(n + 1) * TG],
                                                    start=(k == 0), stop=(k == KH - 1))
                        last.then_inc(logits_done, 1)

                    pe.wait_ge(modT_ready, 1)
                    for n in range(NTG):
                        pe.wait_ge(h_ready, n + 1)
                        if n >= 2:
                            pe.wait_ge(hT_ready, n - 1)
                        turn_group(h_tok[:, n % 2, :, :], 4 + 2 * (n % 2)).then_inc(h_turned, 1)
                        if n >= 1:
                            logits(n - 1)
                    logits(NTG - 1)
                    pe.wait_ge(sv_ready, 1)

                    def sink_share(g):
                        pe.wait_ge(wo_ready, g + 1)
                        for h in range(HG):
                            last = nc.tensor.matmul(psum[:, 4, 0:HID], sv_bias[:, g * HG + h, :], wo_gated[:, wo_buf[g], h, :],
                                                    start=(g == 0 and h == 0), stop=(g == NG - 1 and h == HG - 1))
                        last.then_inc(wo_used, 1)

                    sink_share(0)
                    sink_share(1)
                    pe.wait_ge(ent_ready, 1)
                    for m in range(2):
                        for k in range(KH):
                            last = nc.tensor.matmul(psum[:, 6 + m, 0:HD], entT[:, k, :], w_kv[:, m, k, :],
                                                    start=(k == 0), stop=(k == KH - 1))
                    last.then_inc(kv_done, 1)
                    sink_share(2)
                    sink_share(3)
                    pe.wait_ge(ck_ready, 1)
                    nc.tensor.transpose(psum[:, 6, 0:C], ck[:, 1, :], ident[:]).then_inc(ck_turned, 1)

                @block.gpsimd
                def _(pool):
                    g = nc.gpsimd
                    g.memset(half_const[:], -0.5).then_inc(pool_const, 1)
                    g.memset(keys[:].bitcast(F32), 0.0).then_inc(zeroed, 1)
                    g.memset(v_ring[:], 0.0).then_inc(zeroed, 1)
                    g.memset(sink_prob[:], 1.0).then_inc(zeroed, 1)
                    pool.wait_ge(pool_const, 1)
                    for half in range(2):
                        pool.wait_ge(var_done, half + 1)
                        rstd_half(half).then_inc(rstd_done, 1)
                    pool.wait_ge(tables_in, 96)
                    cos, sin, nsin = (trig[:, 0:NT, c, :] for c in range(3))
                    for m in range(2):
                        w1, w2 = rows[:, 2 + m, 0:HALF], rows[:, 2 + m, HALF:ROPE]
                        g.tensor_tensor(rope_same[:, :, m, 0:HALF], cos, bc(w1, 1, NT), ALU.mult)
                        g.tensor_tensor(rope_same[:, :, m, HALF:ROPE], cos, bc(w2, 1, NT), ALU.mult)
                        g.tensor_tensor(rope_swap[:, :, m, 0:HALF], nsin, bc(w2, 1, NT), ALU.mult)
                        g.tensor_tensor(rope_swap[:, :, m, HALF:ROPE], sin, bc(w1, 1, NT), ALU.mult).then_inc(zeroed, 1)
                    for half in range(2):
                        at = slice(half * C // 2, (half + 1) * C // 2)
                        pool.wait_ge(exp_pool, half + 1)
                        if half:
                            pool.wait_ge(out_high, 1)
                            g.tensor_tensor(w_out[:, 0, 1, :], wo_gated[:, 0, :, :].rearrange("p h n -> p (h n)"), w_out[:, 0, 0, :].bitcast(F32),
                                            ALU.subtract).then_inc(out_low, 1)
                            pool.wait_ge(prod_used, 1)
                        g.tensor_tensor(prod[:, 1, :, :], hT[:, 1, half * S // 2:(half + 1) * S // 2].rearrange("p (c r) -> p c r", r=R),
                                        pool_w[:, at, :], ALU.mult).then_inc(prod_ready, 1)
                    pool.wait_ge(w_high, 1)
                    g.tensor_tensor(w_split[:, 0, 1, :], w_first, w_split[:, 0, 0, :].bitcast(F32), ALU.subtract)
                    g.tensor_tensor(sink_split[:, 1, :], sink_kT[:], sink_split[:, 0, :].bitcast(F32), ALU.subtract)
                    pool.wait_ge(ck_var, 1)
                    g.tensor_tensor(ck_t[:, 2:3], ck_t[:, 1:2], half_const[:, 0:1], ALU.pow).then_inc(ck_rstd, 1)

                @block.vector
                def _(dve):
                    v = nc.vector
                    link = chain_on(dve, dve_step)
                    v.memset(bo_row[:], 0.0).then_inc(bo_zeroed, 1)
                    dve.wait_ge(exp_c, 1)
                    link(v.tensor_scalar(c_tmp[:, 1, :], c_tmp[:, 0, :], 1.0, None, ALU.add))
                    link(v.reciprocal(c_tmp[:, 2, :], c_tmp[:, 1, :]))
                    link(v.tensor_tensor(c_tmp[:, 1, :], cT[:], c_tmp[:, 2, :], ALU.mult))
                    v.tensor_copy(c_rep[:], bc(c_tmp[:, 1, :], 2, P)).then_inc(c_spread, 1)
                    link(v.memset(sv_bias, 0.0))

                    def statistics(half):
                        dve.wait_ge(x_in[half], 16)
                        for i in range(half * NT // 2, (half + 1) * NT // 2):
                            v.bn_stats(stats[:, i, :], x_acc[:, i, :]).then_inc(stats_done, 1)
                        dve.wait_ge(stats_done, (half + 1) * NT // 2)
                        moments(link, half).then_inc(var_done, 1)

                    statistics(0)
                    dve.wait_ge(mod_raw, 1)
                    v.tensor_scalar(mod[:, 1::3, :], mod[:, 1::3, :], 1.0, None, ALU.add).then_inc(scale_ready, 1)
                    statistics(1)
                    dve.wait_ge(mod_turned, 1)
                    v.tensor_copy(modT[:].rearrange("p n c k -> p (n c k)"),
                                  psum[:, 3, :].rearrange("p (a t) -> p a t", t=P // 2)[:, :, 0]).then_inc(modT_ready, 1)

                    def keep_gates():
                        gate = mod[:, 2::3, :]
                        v.tensor_scalar(gate_tmp[:, 0, :, :], gate, 0.0, 2.0, ALU.is_ge, ALU.mult)
                        link(v.scalar_tensor_tensor(gate_tmp[:, 1, :, :], gate, -1.0, gate, ALU.mult, ALU.max))
                        link(v.tensor_scalar(gate_tmp[:, 1, :, :], gate_tmp[:, 1, :, :], 0.25, None, ALU.max))
                        link(v.scalar_tensor_tensor(gates[:], gate_tmp[:, 0, :, :], -1.0, gate_tmp[:, 1, :, :], ALU.add, ALU.mult))

                    for n in range(NTG):
                        dve.wait_ge(rstd_done, n // 2 + 1)
                        if n >= 2:
                            dve.wait_ge(h_turned, n - 1)
                        for j in range(TPG):
                            ins = standardise(h_tok[:, n % 2, j, :], n * TPG + j)
                        ins.then_inc(h_ready, 1)
                        if n == 1:
                            dve.wait_ge(tables_in, 96)
                            v.tensor_copy(wc_rep[:], bc(wcT[:], 2, P)).then_inc(wc_ready, 1)
                            keep_gates()
                    def gate_wo(g):
                        dve.wait_ge(wo_in[wo_buf[g]], 16 * wo_load[g])
                        rows_g = wo_gated[:, wo_buf[g], :, :]
                        v.scalar_tensor_tensor(rows_g, rows_g, 0.5, bc(gates[:, 0, :], 1, HG), ALU.mult, ALU.mult).then_inc(wo_ready, 1)

                    dve.wait_ge(sink_in, 48)
                    v.tensor_copy(sv_bias[:, :, BIAS_ROW], blvT[:])
                    v.tensor_copy(sv_bias.rearrange("p h t -> p (h t)")[:, 0:(NH - 1) * (P + 1) + 1:P + 1], sink_vT[:]).then_inc(sv_ready, 1)
                    gate_wo(0)
                    gate_wo(1)
                    link(v.tensor_tensor(bo_row[:], bo_row[:], gates[:, 0, :], ALU.mult))
                    halves = [slice(half * C // 2, (half + 1) * C // 2) for half in range(2)]
                    for half, at in enumerate(halves):
                        dve.wait_ge(logits_out, (half + 1) * NTG // 2)
                        link(v.tensor_reduce(pool_m[:, 0, at], pool_w[:, at, :], AX, ALU.max))
                        v.tensor_tensor(pool_w[:, at, :], pool_w[:, at, :], bc(pool_m[:, 0, at], 2, R), ALU.subtract).then_inc(shifted, 1)
                    dve.wait_ge(shifted, 2)
                    for half, at in enumerate(halves):
                        dve.wait_ge(exp_pool, half + 1)
                        v.tensor_reduce(pool_m[:, 0, at], pool_w[:, at, :], AX, ALU.add)
                        link(v.tensor_tensor(prod[:, 0, :, :], hT[:, 0, half * S // 2:(half + 1) * S // 2].rearrange("p (c r) -> p c r", r=R),
                                             pool_w[:, at, :], ALU.mult))
                        dve.wait_ge(prod_ready, half + 1)
                        v.tensor_reduce(entT[:, :, at], prod, AX, ALU.add).then_inc(prod_used, 1)
                        dve.wait_ge(prod_used, half + 1)
                    link(v.reciprocal(pool_m[:, 1, :], pool_m[:, 0, :]))
                    v.tensor_tensor(entT[:], entT[:], bc(pool_m[:, 1, :], 1, KH), ALU.mult).then_inc(ent_ready, 1)
                    gate_wo(2)
                    gate_wo(3)
                    dve.wait_ge(kv_done, 1)
                    v.tensor_tensor(ck[:, 0, :], psum[:, 6, 0:HD], rows[:, 0, :], ALU.add).then_inc(ck_biased, 1)
                    v.tensor_tensor(cv[:], psum[:, 7, 0:HD], rows[:, 1, :], ALU.add).then_inc(cv_ready, 1)
                    dve.wait_ge(ck_ss, 1)
                    v.tensor_scalar(ck_t[:, 1:2], ck_t[:, 0:1], 1.0 / HD, EPS_RMS, ALU.mult, ALU.add).then_inc(ck_var, 1)
                    dve.wait_ge(ck_rstd, 1)
                    dve.wait_ge(ck_biased, 1)
                    link(v.scalar_tensor_tensor(ck[:, 0, :], ck[:, 0, :], ck_t[:, 2:3], rows[:, 2, :], ALU.mult, ALU.mult))
                    x1, x2 = ck[:, 0, 0:HALF], ck[:, 0, HALF:ROPE]
                    cos, sin = trig[:, NT, 0, :], trig[:, NT, 1, :]
                    v.tensor_tensor(ck_r[:, 0, :], x1, cos, ALU.mult)
                    v.tensor_tensor(ck_r[:, 1, :], x2, sin, ALU.mult)
                    v.tensor_tensor(ck_r[:, 2, :], x1, sin, ALU.mult)
                    link(v.tensor_tensor(ck_r[:, 3, :], x2, cos, ALU.mult))
                    v.tensor_tensor(ck[:, 1, 0:HALF], ck_r[:, 0, :], ck_r[:, 1, :], ALU.subtract)
                    v.tensor_tensor(ck[:, 1, HALF:ROPE], ck_r[:, 2, :], ck_r[:, 3, :], ALU.add)
                    v.tensor_copy(ck[:, 1, ROPE:HD], ck[:, 0, ROPE:HD]).then_inc(ck_ready, 1)
                    dve.wait_ge(cv_high, 1)
                    v.tensor_tensor(cv_split[:, 1, :], cv[:], cv_split[:, 0, :].bitcast(F32), ALU.subtract)
                    dve.wait_ge(wo_used, NG)
                    v.tensor_tensor(sink_out[:], psum[:, 4, 0:HID], bo_row[:], ALU.add).then_inc(evac, 1)

        with ExitStack() as un:
            qk_tok = sb("qk_tok", [P, 2, HG, HD], stack=un)
            qk_rot = sb("qk_rot", [P, 2, HG, HD], stack=un)
            qk_swp = sb("qk_swp", [P, 2, HG, ROPE], stack=un)
            squares = sb("squares", [P, HG, HD], stack=un)
            ms = sb("ms", [P, 2, HG], stack=un)
            ms_eps = sb("ms_eps", [P, 2, HG], stack=un)
            rstd = sb("rstd", [P, 2, HG], stack=un)
            rstd_q = sb("rstd_q", [P, HG], stack=un)
            qT = sb("qT", [P, 2, HG, P], F32R, stack=un)
            v_new = sb("v_new", [P, 2, GW], stack=un)
            h_now = sb("h_now", [P, 2, KH, P], F32R, stack=un)
            mx = sb("mx", [P, 2, HG], stack=un)
            nmx = sb("nmx", [P, 2, HG], stack=un)
            sums = sb("sums", [P, 2, HG], stack=un)
            inv = sb("inv", [P, 2, HG], stack=un)
            prob = sb("prob", [P, HG, LW], stack=un)
            probT = sb("probT", [P, 2, HG, P], stack=un)
            probT_ent = sb("probT_ent", [P, 2, HG, P], F32R, stack=un)
            ctxT = sb("ctxT", [P, 2, HG, P], F32R, stack=un)
            mask = sb("mask", [P, NT, LW], BF16, stack=un)
            o_stage = sb("o_stage", [P, OCH], stack=un)
            o_gated = sb("o_gated", [P, OCH], stack=un)
            w_stage = sb("w_stage", [P, WCH], stack=un)

            names = ("bias_in mask_in keys_set w_staged w_high w_low o_staged o_gated o_high o_low h_high h_split k_projected v_projected "
                     "qk_biased qk_squared ms_ready rstd_ready rstd_kept swap_ready rot_own rot_added rot_ready k_turned q_turned k_high k_ready q_high qk_ready v_out v_placed "
                     "scored max_done nmax_ready exps_done inv_ready sink_kept prob_ready p_turned p_ready p_low ctx_done ctx_ready ctx_low "
                     "out_done acc_done")
            s = {n: sem(n, un) for n in names.split()}

            K_BANK, Q_BANK, V_BANK, SC_BANK, T_BANK = 0, 1, 2, 3, 7
            t_banks = (K_BANK, Q_BANK, T_BANK)
            t_order = (2, 0, 1)
            NPRE = NU - NT

            def tile_of(u):
                return u & (NT - 1)

            def group_of(u):
                return (u >> 4) & (NG - 1)

            def par_of(u):
                return u & 1

            def run_steps(eng, step):
                step(0, prev=False, outs=False)
                step(1)
                with eng.Fori(2, NPRE - 1) as u:
                    step(u)
                step(NPRE - 1, weights=False)
                step(NPRE, weights=False)
                with eng.Fori(NPRE + 1, NU - 2) as u:
                    step(u, weights=False, outs=False)
                step(NU - 2, weights=False, outs=False, nxt2=False)
                step(NU - 1, weights=False, outs=False, nxt2=False, nxt=False)

            with nc.Block() as block:
                @block.sync
                def _(sp):
                    def chunk(e):
                        sp.dma_start(w_stage[:], d["w_groups"][group_of(e + NT), tile_of(e), :, :]).then_inc(s["w_staged"], 16)

                    sp.dma_start(bias_qk[:], d["bias_qk"].partition_broadcast(P)).then_inc(s["bias_in"], 16)
                    def out_chunk(e):
                        sp.dma_start(o_stage[:], d["w_out"][group_of(e + NT), tile_of(e), :, :]).then_inc(s["o_staged"], 16)

                    chunk(0)
                    sp.dma_start(mask[:], d["mask"]).then_inc(s["mask_in"], 16)
                    for e in range(1, 3):
                        sp.wait_ge(s["w_low"], e)
                        chunk(e)
                    out_chunk(0)
                    with sp.Fori(3, NPRE) as e:
                        sp.wait_ge(s["w_low"], e)
                        chunk(e)
                        sp.wait_ge(s["o_low"], e - 2)
                        out_chunk(e - 2)
                    for e in range(NPRE - 2, NPRE):
                        sp.wait_ge(s["o_low"], e)
                        out_chunk(e)
                    sp.wait_ge(s["w_staged"], 16 * NPRE)
                    sp.wait_ge(s["o_staged"], 16 * NPRE)

                @block.tensor
                def _(pe):
                    t = nc.tensor

                    def project(u, parts, weights=True):
                        if parts[0] == 1:
                            pe.wait_ge(s["h_split"], u + 1)
                            if weights and not (isinstance(u, int) and u < 2):
                                pe.wait_ge(s["w_low"], u)
                        g = group_of(u)
                        for m in parts:
                            if m == 0:
                                pe.wait_ge(s["k_ready"], u)
                            if m == 2 and not (isinstance(u, int) and u < 2):
                                pe.wait_ge(s["acc_done"], u - 2)
                            for k in range(KH):
                                col = (m * KH + k) * GW
                                w = [w_split[:, g & 1, part, col:col + GW] for part in range(2)]
                                product(psum[:, m, :], [h_now[:, part, k, :] for part in range(2)], w, k == 0, k == KH - 1)
                                ins = last[0]
                            if m != 1:
                                ins.then_inc(s["v_projected" if m else "k_projected"], 1)

                    last = [None]

                    def product(out, lhs, rhs, start, stop):
                        t.matmul(out, lhs[1], rhs[0], start=start, stop=False)
                        t.matmul(out, lhs[0], rhs[0], start=False, stop=False)
                        last[0] = t.matmul(out, lhs[0], rhs[1], start=False, stop=stop)

                    def turn_qk(u):
                        pe.wait_ge(s["rot_ready"], u + 1)
                        for m, bank in ((0, K_BANK), (1, T_BANK)):
                            for h in range(HG):
                                ins = t.transpose(psum[:, bank, h * P:(h + 1) * P], qk_rot[:, m, h, :], ident[:])
                            ins.then_inc(s["q_turned" if m else "k_turned"], 1)

                    def score(u, heads):
                        i = tile_of(u)
                        if isinstance(u, int) and u == 0:
                            pe.wait_ge(s["mask_in"], 16)
                        if heads[0] == 0:
                            pe.wait_ge(s["qk_ready"], u + 1)
                            pe.wait_ge(s["keys_set"], HG)
                            pe.wait_ge(s["exps_done"], u)
                        for h in heads:
                            out = psum[:, SC_BANK + h, 0:LW]
                            t.matmul(out, ident_b[:], mask[:, i, :], start=True, stop=False)
                            product(out, [qT[:, part, h, :] for part in range(2)], [keys[:, part, h, :] for part in range(2)], False, True)
                        if heads[-1] == HG - 1:
                            last[0].then_inc(s["scored"], 1)

                    def turn_probs(u, parts, nxt2=True):
                        pe.wait_ge(s["prob_ready"], 2 * u + (1 if parts[0] == 2 else 2))
                        if nxt2 and parts[0] != 2:
                            pe.wait_ge(s["qk_biased"], u + 3)
                        for c in parts:
                            for h in range(HG):
                                ins = t.transpose(psum[:, t_banks[c], h * P:(h + 1) * P], prob[:, h, c * P:(c + 1) * P], ident[:])
                            ins.then_inc(s["p_turned"], 1)

                    def context(u, nxt2=True):
                        pe.wait_ge(s["v_placed"], u + 1)
                        pe.wait_ge(s["p_ready"], 3 * u + 1)
                        if nxt2:
                            pe.wait_ge(s["v_out"], u + 3)
                        ent = [probT_ent[:, part, :, :].rearrange("p h t -> p (h t)") for part in range(2)]
                        t.matmul(psum[:, V_BANK, :], cv_split[:, 0, :], ent[0], start=True, stop=True)
                        t.matmul(psum[:, V_BANK, :], cv_split[:, 1, :], ent[0], start=False, stop=True, skip_group_check=True)
                        for c in range(2):
                            pe.wait_ge(s["p_ready"], 3 * u + 2 + c)
                            for h in range(HG):
                                t.matmul(psum[:, V_BANK, h * P:(h + 1) * P], v_ring[:, c, h * HD:(h + 1) * HD], probT[:, c, h, :],
                                         start=False, stop=True, skip_group_check=True)
                        pe.wait_ge(s["p_low"], u + 1)
                        ins = t.matmul(psum[:, V_BANK, :], cv_split[:, 0, :], ent[1], start=False, stop=True, skip_group_check=True)
                        ins.then_inc(s["ctx_done"], 1)

                    def output(u, outs=True):
                        g = group_of(u)
                        if outs and not (isinstance(u, int) and u == 0):
                            pe.wait_ge(s["o_low"], u)
                        elif not outs:
                            pe.wait_ge(s["o_low"], NPRE)
                        pe.wait_ge(s["ctx_low"], u + 1)
                        for h in range(HG):
                            product(psum[:, V_BANK, 0:HID], [ctxT[:, part, h, :] for part in range(2)],
                                    [w_out[:, g & 1, part, h * HID:(h + 1) * HID] for part in range(2)], h == 0, h == HG - 1)
                        last[0].then_inc(s["out_done"], 1)

                    def step(u, prev=True, nxt=True, nxt2=True, weights=True, outs=True):
                        score(u, range(HG - 1))
                        if prev:
                            turn_probs(u - 1, t_order[:1], nxt)
                        score(u, (HG - 1,))
                        if prev:
                            turn_probs(u - 1, t_order[1:], nxt)
                            context(u - 1, nxt)
                        if nxt:
                            turn_qk(u + 1)
                        if nxt2:
                            project(u + 2, (1,), weights)
                        if prev:
                            output(u - 1, outs)
                        if nxt2:
                            project(u + 2, (0, 2), weights)

                    project(0, (1, 0, 2))
                    pe.wait_ge(s["qk_biased"], 1)
                    project(1, (1,))
                    turn_qk(0)
                    project(1, (0, 2))
                    run_steps(pe, step)
                    turn_probs(NU - 1, t_order[:1], False)
                    turn_probs(NU - 1, t_order[1:], False)
                    context(NU - 1, False)
                    output(NU - 1, False)

                @block.scalar
                def _(act):
                    a = nc.scalar

                    def split_weights(e):
                        act.wait_ge(s["w_staged"], 16 * e + 16)
                        act.wait_ge(s["v_projected"], e)
                        a.copy(w_split[:, group_of(e + NT) & 1, 0, bass.ds(tile_of(e) * WCH, WCH)], w_stage[:]).then_inc(s["w_high"], 1)

                    def split_h(u):
                        act.wait_ge(s["v_projected"], u)
                        a.copy(h_now[:, 0, :, :], hT[:, :, bass.ds(tile_of(u) * P, P)]).then_inc(s["h_high"], 1)

                    def square(u, m):
                        act.wait_ge(s["qk_biased"], u + 1)
                        if m == 1 or not (isinstance(u, int) and u == 0):
                            act.wait_ge(s["qk_squared"], 2 * u + m)
                        for h in range(HG):
                            ins = a.activation(squares[:, h, :], qk_tok[:, m, h, :], ACT.Square, accum_out=ms[:, m, h:h + 1])
                        ins.then_inc(s["qk_squared"], 1)

                    def v_evac(u):
                        act.wait_ge(s["v_projected"], u + 1)
                        if not (isinstance(u, int) and u < 2):
                            act.wait_ge(s["v_placed"], u - 1)
                        a.copy(v_new[:, par_of(u), :], psum[:, V_BANK, :]).then_inc(s["v_out"], 1)

                    def qk_evac(u):
                        act.wait_ge(s["k_turned"], u + 1)
                        a.copy(keys[:, 0, :, bass.ds(par_of(u) * P, P)], psum[:, K_BANK, :].rearrange("p (h t) -> p h t", h=HG)).then_inc(s["k_high"], 1)
                        act.wait_ge(s["q_turned"], u + 1)
                        a.copy(qT[:, 0, :, :], psum[:, T_BANK, :].rearrange("p (h t) -> p h t", h=HG)).then_inc(s["q_high"], 1)

                    def exps(u):
                        act.wait_ge(s["nmax_ready"], u + 1)
                        for c, (lo, hi) in enumerate(((0, 2 * P), (2 * P, 2 * P + C + 1))):
                            for h in range(HG):
                                ins = a.activation(prob[:, h, lo:hi], psum[:, SC_BANK + h, lo:hi], ACT.Exp, bias=nmx[:, c, h:h + 1],
                                                   scale=rstd_q[:, h:h + 1], accum_out=sums[:, c, h:h + 1])
                        ins.then_inc(s["exps_done"], 1)

                    def probs_evac(u, parts=range(3)):
                        for n in parts:
                            c = t_order[n]
                            act.wait_ge(s["p_turned"], 3 * u + n + 1)
                            to = probT_ent[:, 0, :, :] if c == 2 else probT[:, c, :, :]
                            a.copy(to.rearrange("p h t -> p (h t)"), psum[:, t_banks[c], :]).then_inc(s["p_ready"], 1)

                    def ctx_evac(u):
                        act.wait_ge(s["ctx_done"], u + 1)
                        a.copy(ctxT[:, 0, :, :].rearrange("p h t -> p (h t)"), psum[:, V_BANK, :]).then_inc(s["ctx_ready"], 1)

                    def split_out(e):
                        act.wait_ge(s["o_gated"], e + 1)
                        if not (isinstance(e, int) and e == 0):
                            act.wait_ge(s["out_done"], e)
                        a.copy(w_out[:, group_of(e + NT) & 1, 0, bass.ds(tile_of(e) * OCH, OCH)], o_gated[:]).then_inc(s["o_high"], 1)

                    def step(u, prev=True, nxt=True, nxt2=True, weights=True, outs=True):
                        if weights:
                            split_weights(u + 1)
                        if outs:
                            split_out(u - 1)
                        if nxt:
                            v_evac(u + 1)
                        if nxt2:
                            split_h(u + 2)
                        if nxt:
                            square(u + 1, 0)
                        if prev:
                            probs_evac(u - 1)
                        if nxt:
                            square(u + 1, 1)
                        if prev:
                            ctx_evac(u - 1)
                        if nxt:
                            qk_evac(u + 1)
                        exps(u)

                    split_h(0)
                    for h in range(HG):
                        a.copy(keys[:, 0, h, 2 * P:2 * P + C], ckT[:]).then_inc(s["keys_set"], 1)
                    split_h(1)
                    square(0, 0)
                    square(0, 1)
                    v_evac(0)
                    qk_evac(0)
                    split_weights(0)
                    run_steps(act, step)
                    probs_evac(NU - 1)
                    ctx_evac(NU - 1)

                @block.vector
                def _(dve):
                    v = nc.vector

                    def bias(u):
                        dve.wait_ge(s["k_projected"], u + 1)
                        v.tensor_tensor(qk_tok[:].rearrange("p m h d -> p (m h d)"), psum[:, 0:2, :].rearrange("p a b -> p (a b)"),
                                        bias_qk[:, group_of(u), :], ALU.add).then_inc(s["qk_biased"], 1)

                    def mean_square(u, m):
                        dve.wait_ge(s["qk_squared"], 2 * u + 1 + m)
                        if m == 0:
                            v.tensor_scalar(ms_eps[:, 0, :], ms[:, 0, :], 1.0 / HD, EPS_RMS, ALU.mult, ALU.add).then_inc(s["ms_ready"], 1)
                        else:
                            v.tensor_scalar(ms_eps[:, 1, :], ms[:, 1, :], EPS_RMS * HD, None, ALU.add).then_inc(s["ms_ready"], 1)

                    def rotate_own(u):
                        v.tensor_tensor(qk_rot[:, :, :, 0:ROPE], qk_tok[:, :, :, 0:ROPE], bc(rope_same[:, tile_of(u), :, :], 2, HG), ALU.mult)
                        v.tensor_tensor(qk_rot[:, :, :, ROPE:HD], qk_tok[:, :, :, ROPE:HD], bc(norm_rest[:], 2, HG), ALU.mult).then_inc(s["rot_own"], 1)

                    def swap_parts(u):
                        i = tile_of(u)
                        v.tensor_tensor(qk_swp[:, :, :, 0:HALF], qk_tok[:, :, :, HALF:ROPE], bc(rope_swap[:, i, :, 0:HALF], 2, HG), ALU.mult)
                        v.tensor_tensor(qk_swp[:, :, :, HALF:ROPE], qk_tok[:, :, :, 0:HALF], bc(rope_swap[:, i, :, HALF:ROPE], 2, HG),
                                        ALU.mult).then_inc(s["swap_ready"], 1)

                    def rotate_add(u):
                        dve.wait_ge(s["swap_ready"], u + 1)
                        dve.wait_ge(s["rot_own"], u + 1)
                        v.tensor_tensor(qk_rot[:, :, :, 0:ROPE], qk_rot[:, :, :, 0:ROPE], qk_swp[:], ALU.add).then_inc(s["rot_added"], 1)

                    def keep_rstd(u):
                        dve.wait_ge(s["rstd_ready"], 2 * u + 2)
                        dve.wait_ge(s["exps_done"], u)
                        v.tensor_copy(rstd_q[:], rstd[:, 1, :]).then_inc(s["rstd_kept"], 1)

                    def maxima(u):
                        dve.wait_ge(s["scored"], u + 1)
                        sc = psum[:, SC_BANK:SC_BANK + HG, :]
                        v.tensor_reduce(mx[:, 0, :], sc[:, :, 0:2 * P], AX, ALU.max)
                        v.tensor_reduce(mx[:, 1, :], sc[:, :, 2 * P:2 * P + C + 1], AX, ALU.max).then_inc(s["max_done"], 1)
                        dve.wait_ge(s["max_done"], u + 1)
                        dve.wait_ge(s["rstd_kept"], u + 1)
                        v.scalar_tensor_tensor(nmx[:], mx[:], -1.0, bc(rstd_q[:], 1, 2), ALU.mult, ALU.mult).then_inc(s["nmax_ready"], 1)

                    def inverses(u):
                        dve.wait_ge(s["exps_done"], u + 1)
                        v.reciprocal(inv[:], sums[:]).then_inc(s["inv_ready"], 1)

                    def keep_sink(u):
                        dve.wait_ge(s["inv_ready"], u + 1)
                        v.tensor_tensor(sink_prob[:, tile_of(u), bass.ds(group_of(u) * HG, HG)], prob[:, :, 2 * P + C], inv[:, 1, :], ALU.mult).then_inc(s["sink_kept"], 1)

                    def low_parts(u):
                        dve.wait_ge(s["k_high"], u + 1)
                        at = bass.ds(par_of(u) * P, P)
                        v.tensor_tensor(keys[:, 1, :, at], psum[:, K_BANK, :].rearrange("p (h t) -> p h t", h=HG), keys[:, 0, :, at].bitcast(F32),
                                        ALU.subtract).then_inc(s["k_ready"], 1)
                        for part in range(2):
                            v.tensor_copy(keys[:, part, :, 2 * P + C], sink_split[:, part, bass.ds(group_of(u) * HG, HG)].bitcast(F32))
                        dve.wait_ge(s["q_high"], u + 1)
                        v.tensor_tensor(qT[:, 1, :, :], psum[:, T_BANK, :].rearrange("p (h t) -> p h t", h=HG), qT[:, 0, :, :].bitcast(F32),
                                        ALU.subtract).then_inc(s["qk_ready"], 1)

                    def low_weights(e):
                        dve.wait_ge(s["w_high"], e + 1)
                        at = bass.ds(tile_of(e) * WCH, WCH)
                        slot = group_of(e + NT) & 1
                        v.tensor_tensor(w_split[:, slot, 1, at], w_stage[:], w_split[:, slot, 0, at].bitcast(F32), ALU.subtract).then_inc(s["w_low"], 1)

                    def gate_out(e):
                        dve.wait_ge(s["o_staged"], 16 * e + 16)
                        if not (isinstance(e, int) and e == 0):
                            dve.wait_ge(s["o_low"], e)
                        v.scalar_tensor_tensor(o_gated[:], o_stage[:], 0.5, gates[:, 0, bass.ds((e & (HID // OCH - 1)) * OCH, OCH)],
                                               ALU.mult, ALU.mult).then_inc(s["o_gated"], 1)

                    def low_out(e):
                        dve.wait_ge(s["o_high"], e + 1)
                        at = bass.ds(tile_of(e) * OCH, OCH)
                        slot = group_of(e + NT) & 1
                        v.tensor_tensor(w_out[:, slot, 1, at], o_gated[:], w_out[:, slot, 0, at].bitcast(F32), ALU.subtract).then_inc(s["o_low"], 1)

                    def low_probs(u):
                        dve.wait_ge(s["p_ready"], 3 * u + 1)
                        v.tensor_tensor(probT_ent[:, 1, :, :].rearrange("p h t -> p (h t)"), psum[:, T_BANK, :],
                                        probT_ent[:, 0, :, :].rearrange("p h t -> p (h t)").bitcast(F32), ALU.subtract).then_inc(s["p_low"], 1)

                    def low_ctx(u):
                        dve.wait_ge(s["ctx_ready"], u + 1)
                        v.tensor_tensor(ctxT[:, 1, :, :].rearrange("p h t -> p (h t)"), psum[:, V_BANK, :],
                                        ctxT[:, 0, :, :].rearrange("p h t -> p (h t)").bitcast(F32), ALU.subtract).then_inc(s["ctx_low"], 1)

                    def low_h(u):
                        dve.wait_ge(s["h_high"], u + 1)
                        v.tensor_tensor(h_now[:, 1, :, :], hT[:, :, bass.ds(tile_of(u) * P, P)], h_now[:, 0, :, :].bitcast(F32),
                                        ALU.subtract).then_inc(s["h_split"], 1)

                    def place_v(u):
                        dve.wait_ge(s["v_out"], u + 1)
                        dve.wait_ge(s["ctx_done"], u)
                        v.tensor_copy(v_ring[:, par_of(u), :], v_new[:, par_of(u), :]).then_inc(s["v_placed"], 1)

                    def accumulate(u):
                        dve.wait_ge(s["out_done"], u + 1)
                        i = tile_of(u)
                        v.tensor_tensor(x_acc[:, i, :], x_acc[:, i, :], psum[:, V_BANK, 0:HID], ALU.add).then_inc(s["acc_done"], 1)

                    def step(u, prev=True, nxt=True, nxt2=True, weights=True, outs=True):
                        if outs:
                            gate_out(u - 1)
                        if prev:
                            inverses(u - 1)
                        if nxt:
                            bias(u + 1)
                        keep_rstd(u)
                        if weights:
                            low_weights(u + 1)
                        if nxt:
                            dve.wait_ge(s["qk_biased"], u + 2)
                            rotate_own(u + 1)
                            swap_parts(u + 1)
                        if prev:
                            keep_sink(u - 1)
                        if nxt:
                            mean_square(u + 1, 0)
                            rotate_add(u + 1)
                        if prev:
                            low_probs(u - 1)
                        if nxt2:
                            low_h(u + 2)
                        if outs:
                            low_out(u - 1)
                        maxima(u)
                        if nxt:
                            mean_square(u + 1, 1)
                        if prev:
                            low_ctx(u - 1)
                        place_v(u)
                        if nxt:
                            low_parts(u + 1)
                        if prev:
                            accumulate(u - 1)

                    low_h(0)
                    dve.wait_ge(s["keys_set"], HG)
                    for h in range(HG):
                        v.tensor_tensor(keys[:, 1, h, 2 * P:2 * P + C], ckT[:], keys[:, 0, h, 2 * P:2 * P + C].bitcast(F32), ALU.subtract)
                    dve.wait_ge(s["bias_in"], 16)
                    bias(0)
                    dve.wait_ge(s["qk_biased"], 1)
                    rotate_own(0)
                    swap_parts(0)
                    mean_square(0, 0)
                    rotate_add(0)
                    low_h(1)
                    mean_square(0, 1)
                    low_parts(0)
                    low_weights(0)
                    run_steps(dve, step)
                    inverses(NU - 1)
                    keep_sink(NU - 1)
                    low_probs(NU - 1)
                    low_ctx(NU - 1)
                    accumulate(NU - 1)

                @block.gpsimd
                def _(pool):
                    g = nc.gpsimd

                    def normalise(u):
                        pool.wait_ge(s["inv_ready"], u + 1)
                        for c, lo, hi in ((1, 2 * P, 2 * P + C), (0, 0, 2 * P)):
                            g.tensor_tensor(prob[:, :, lo:hi], prob[:, :, lo:hi], bc(inv[:, c, :], 2, hi - lo), ALU.mult).then_inc(s["prob_ready"], 1)

                    def scale_k(u):
                        pool.wait_ge(s["ms_ready"], 2 * u + 1)
                        g.tensor_tensor(rstd[:, 0, :], ms_eps[:, 0, :], half_const[:, 0:HG], ALU.pow).then_inc(s["rstd_ready"], 1)
                        pool.wait_ge(s["rot_added"], u + 1)
                        pool.wait_ge(s["rstd_ready"], 2 * u + 1)
                        g.tensor_tensor(qk_rot[:, 0, :, :], qk_rot[:, 0, :, :], bc(rstd[:, 0, :], 2, HD), ALU.mult).then_inc(s["rot_ready"], 1)

                    def factor_q(u):
                        pool.wait_ge(s["ms_ready"], 2 * u + 2)
                        pool.wait_ge(s["rstd_kept"], u)
                        g.tensor_tensor(rstd[:, 1, :], ms_eps[:, 1, :], half_const[:, 0:HG], ALU.pow).then_inc(s["rstd_ready"], 1)

                    def step(u, prev=True, nxt=True, nxt2=True, weights=True, outs=True):
                        if prev:
                            normalise(u - 1)
                        if nxt:
                            scale_k(u + 1)
                            factor_q(u + 1)

                    scale_k(0)
                    factor_q(0)
                    run_steps(pool, step)
                    normalise(NU - 1)

        att.close()

        with ExitStack() as ff:
            h2 = sb("h2", [P, 2, KH, S], F32R, stack=ff)
            w_ff = sb("w_ff", [P, 2, 2, FCOLS], F32R, stack=ff)
            w_load = sb("w_load", [P, FCOLS], stack=ff)
            pick = sb("pick", [P, FW], F32R, stack=ff)
            combT = sb("combT", [P, S], F32R, stack=ff)
            ff_in = sem("ff_in", ff)
            ff_high = sem("ff_high", ff)
            ff_split = sem("ff_split", ff)
            rt_in = sem("rt_in", ff)

            def load_chunk(sp, c):
                sp.wait_ge(ff_split, c)
                sp.dma_start(w_load[:], d["w_ff"][c]).then_inc(ff_in, 16)

            def split_high(pool, c):
                pool.wait_ge(ff_in, 16 * (c + 1))
                nc.gpsimd.tensor_scalar(w_ff[:, c % 2, 0, :], w_load[:], 1.0, 0.0, ALU.mult, ALU.add).then_inc(ff_high, 1)

            def split_low(pool, c, half):
                if half == 0:
                    pool.wait_ge(ff_high, c + 1)
                at = slice(half * FCOLS // 2, (half + 1) * FCOLS // 2)
                ins = nc.gpsimd.tensor_tensor(w_ff[:, c % 2, 1, at], w_load[:, at], w_ff[:, c % 2, 0, at].bitcast(F32), ALU.subtract)
                if half:
                    ins.then_inc(ff_split, 1)

            def split_chunk(pool, c):
                split_high(pool, c)
                split_low(pool, c, 0)
                split_low(pool, c, 1)

            def product(out, lhs, rhs, start, stop):
                nc.tensor.matmul(out, lhs[1], rhs[0], start=start, stop=False)
                nc.tensor.matmul(out, lhs[0], rhs[0], start=False, stop=False)
                return nc.tensor.matmul(out, lhs[0], rhs[1], start=False, stop=stop)

            with ExitStack() as rt:
                work = sb("work2", [P, 2, 2 * TPG * HID], stack=rt)
                pick_in = work[:].rearrange("p a n -> p (a n)")[:, 0:FW]
                h_tok = work[:, 0, :].rearrange("p (b j n) -> p b j n", b=2, j=TPG)
                h_full = work[:, 1, :].rearrange("p (b k t) -> p b k t", b=2, k=KH)
                spT = sb("spT", [NH + 1, S], stack=rt)
                full_ready = sem("full_ready", rt)
                lgT = sb("lgT", [EG, S], stack=rt)
                lg = sb("lg", [P, NT, EG], stack=rt)
                pr = sb("pr", [P, NT, E + PADK], stack=rt)
                rep = sb("rep", [P, NT, E + PADK], stack=rt)
                top = sb("top", [P, NT, 8], stack=rt)
                comb = sb("comb", [P, NT, EG], stack=rt)
                w_rt = sb("w_rt", [P, KH * EG], stack=rt)
                w_rt_split = sb("w_rt_split", [P, 2, KH * EG + 1], F32R, stack=rt)
                rt_high = sem("rt_high", rt)
                rt_split = sem("rt_split", rt)
                h2_high = sem("h2_high", rt)
                comb_high = sem("comb_high", rt)
                comb_zeroed = sem("comb_zeroed", rt)
                row_t = sb("row_t", [P, 4, NT], stack=rt)
                table_call = sb("table_call", [P, 1], stack=rt)
                sp_turned = sem("sp_turned", rt)
                spT_ready = sem("spT_ready", rt)
                sink_added = sem("sink_added", rt)
                acc_step = sem("acc_step", rt)
                stats2 = sem("stats2", rt)
                var2 = sem("var2", rt)
                rstd2 = sem("rstd2", rt)
                step2 = sem("step2", rt)
                h2_ready = sem("h2_ready", rt)
                h2_turned = sem("h2_turned", rt)
                h2T_ready = sem("h2T_ready", rt)
                lgT_done = sem("lgT_done", rt)
                lgT_ready = sem("lgT_ready", rt)
                lg_turned = sem("lg_turned", rt)
                lg_shifted = sem("lg_shifted", rt)
                lg_exp = sem("lg_exp", rt)
                comb_ready = sem("comb_ready", rt)
                comb_turned = sem("comb_turned", rt)
                combT_ready = sem("combT_ready", rt)
                with nc.Block() as block:
                    @block.sync
                    def _(sp):
                        sp.dma_start(w_rt[:].rearrange("p (k n) -> p k n", k=KH), d["w_rt"].rearrange("(k p) n -> p k n", p=P)).then_inc(rt_in, 16)
                        load_chunk(sp, 0)
                        sp.dma_start(pick_in, d["pick"]).then_inc(rt_in, 16)
                        load_chunk(sp, 1)
                        sp.wait_ge(rt_in, 32)

                    @block.tensor
                    def _(pe):
                        t = nc.tensor
                        for i in range(NT):
                            ins = t.transpose(psum[0:NH + 1, i // TPG, (i % TPG) * P:(i % TPG + 1) * P], sink_prob[:, i, :], ident[:])
                            if i % TPG == TPG - 1:
                                ins.then_inc(sp_turned, 1)
                        for p in range(NT // 2):
                            pe.wait_ge(spT_ready, 2 * p // TPG + 1)
                            for j in range(2):
                                i = 2 * p + j
                                ins = t.matmul(psum[:, (4 + p) % 8, j * HID:(j + 1) * HID], spT[:, i * P:(i + 1) * P], sink_out[0:NH + 1, :], start=True, stop=True)
                            ins.then_inc(acc_step, 1)

                        def logits(n):
                            pe.wait_ge(h2T_ready, n + 1)
                            for k in range(KH):
                                ins = product(psum[0:EG, n, :], [w_rt_split[:, part, k * EG:(k + 1) * EG] for part in range(2)],
                                              [h2[:, part, k, n * TG:(n + 1) * TG] for part in range(2)], k == 0, k == KH - 1)
                            ins.then_inc(lgT_done, 1)

                        pe.wait_ge(rt_split, 1)
                        for n in range(NTG):
                            pe.wait_ge(h2_ready, n + 1)
                            if n >= 2:
                                pe.wait_ge(full_ready, n - 1)
                            turn_group(h_tok[:, n % 2, :, :], 4 + 2 * (n % 2)).then_inc(h2_turned, 1)
                            if n >= 1:
                                logits(n - 1)
                        logits(NTG - 1)
                        pe.wait_ge(lgT_ready, NTG)
                        for i in range(NT):
                            ins = t.transpose(psum[:, 4, i * 32:i * 32 + EG], lgT[:, i * P:(i + 1) * P], ident[0:EG, 0:EG])
                        ins.then_inc(lg_turned, 1)
                        pe.wait_ge(comb_ready, 1)
                        for i in range(NT):
                            ins = t.transpose(psum[0:EG, i // TPG, (i % TPG) * P:(i % TPG + 1) * P], comb[:, i, :], ident[:])
                            if i % TPG == TPG - 1:
                                ins.then_inc(comb_turned, 1)

                    @block.scalar
                    def _(act):
                        a = nc.scalar
                        for b in range(NTG):
                            act.wait_ge(sp_turned, b + 1)
                            a.copy(spT[:, b * TG:(b + 1) * TG], psum[0:NH + 1, b, :]).then_inc(spT_ready, 1)
                        act.wait_ge(rt_in, 32)
                        a.copy(pick[:], pick_in)
                        a.copy(w_rt_split[:, 0, 0:KH * EG], w_rt[:]).then_inc(rt_high, 1)

                        def modulate(n):
                            act.wait_ge(h2_turned, n + 1)
                            if n >= 2:
                                act.wait_ge(h2T_ready, n - 1)
                            for k in range(KH):
                                ins = a.activation(h_full[:, n % 2, k, :], psum[:, 4 + 2 * (n % 2) + k, :], ACT.Identity,
                                                   bias=modT[:, 1, 0, k:k + 1], scale=modT[:, 1, 1, k:k + 1])
                            ins.then_inc(full_ready, 1)
                            act.wait_ge(full_ready, n + 1)
                            a.copy(h2[:, 0, :, n * TG:(n + 1) * TG], h_full[:, n % 2, :, :]).then_inc(h2_high, 1)

                        def logits_evac(n):
                            act.wait_ge(lgT_done, n + 1)
                            a.copy(lgT[:, n * TG:(n + 1) * TG], psum[0:EG, n, :]).then_inc(lgT_ready, 1)

                        for n in range(NTG):
                            modulate(n)
                            if n >= 1:
                                logits_evac(n - 1)
                        logits_evac(NTG - 1)
                        act.wait_ge(lg_shifted, 1)
                        a.activation(pr[:, :, 0:E], pr[:, :, 0:E], ACT.Exp)
                        a.activation(lg[:, :, E:EG], lg[:, :, E:EG], ACT.Exp, scale=-1.0).then_inc(lg_exp, 1)
                        a.activation(table_call[:], half_const[:, 0:1], ACT.Silu)
                        act.wait_ge(comb_zeroed, 1)
                        for n in range(NTG):
                            act.wait_ge(comb_turned, n + 1)
                            a.copy(combT[0:EG, n * TG:(n + 1) * TG], psum[0:EG, n, :]).then_inc(comb_high, 1)

                    @block.gpsimd
                    def _(pool):
                        nc.gpsimd.memset(combT[:].bitcast(F32), 0.0).then_inc(comb_zeroed, 1)
                        nc.gpsimd.memset(hT[:], 0.0)
                        split_high(pool, 0)
                        for half in range(2):
                            pool.wait_ge(var2, half + 1)
                            rstd_half(half).then_inc(rstd2, 1)
                            split_low(pool, 0, half)
                        split_chunk(pool, 1)

                    @block.vector
                    def _(dve):
                        v = nc.vector
                        link = chain_on(dve, step2)

                        def add_share(p):
                            dve.wait_ge(acc_step, p + 1)
                            x2 = x_acc[:, 2 * p:2 * p + 2, :].rearrange("p a n -> p (a n)")
                            v.tensor_tensor(x2, x2, psum[:, (4 + p) % 8, :], ALU.add).then_inc(sink_added, 1)

                        def statistics(p):
                            dve.wait_ge(sink_added, p + 1)
                            for i in (2 * p, 2 * p + 1):
                                v.bn_stats(stats[:, i, :], x_acc[:, i, :]).then_inc(stats2, 1)

                        for half in range(2):
                            first = half * NT // 4
                            add_share(first)
                            for p in range(first + 1, first + NT // 4):
                                add_share(p)
                                statistics(p - 1)
                            statistics(first + NT // 4 - 1)
                            dve.wait_ge(stats2, (half + 1) * NT // 2)
                            moments(link, half).then_inc(var2, 1)
                        dve.wait_ge(rt_high, 1)
                        v.tensor_tensor(w_rt_split[:, 1, 0:KH * EG], w_rt[:], w_rt_split[:, 0, 0:KH * EG].bitcast(F32), ALU.subtract).then_inc(rt_split, 1)

                        def norm(n):
                            dve.wait_ge(rstd2, n // 2 + 1)
                            if n >= 2:
                                dve.wait_ge(h2_turned, n - 1)
                            for j in range(TPG):
                                ins = standardise(h_tok[:, n % 2, j, :], n * TPG + j)
                            ins.then_inc(h2_ready, 1)

                        def low_h2(n):
                            dve.wait_ge(h2_high, n + 1)
                            at = slice(n * TG, (n + 1) * TG)
                            v.tensor_tensor(h2[:, 1, :, at], h_full[:, n % 2, :, :], h2[:, 0, :, at].bitcast(F32), ALU.subtract).then_inc(h2T_ready, 1)

                        norm(0)
                        for n in range(1, NTG):
                            norm(n)
                            low_h2(n - 1)
                        low_h2(NTG - 1)
                        link(v.memset(pr[:], -1.0))
                        dve.wait_ge(lg_turned, 1)
                        link(v.tensor_copy(lg[:], psum[:, 4, :].rearrange("p (i e) -> p i e", e=32)[:, :, 0:EG]))
                        link(v.tensor_reduce(row_t[:, 0, :], lg[:, :, 0:E], AX, ALU.max))
                        v.tensor_tensor(pr[:, :, 0:E], lg[:, :, 0:E], bc(row_t[:, 0, :], 2, E), ALU.subtract).then_inc(lg_shifted, 1)
                        dve.wait_ge(lg_exp, 1)
                        link(v.tensor_reduce(row_t[:, 1, :], pr[:, :, 0:E], AX, ALU.add))
                        link(v.reciprocal(row_t[:, 2, :], row_t[:, 1, :]))
                        link(v.tensor_tensor(pr[:, :, 0:E], pr[:, :, 0:E], bc(row_t[:, 2, :], 2, E), ALU.mult))
                        for i in range(NT):
                            ins = v.max(top[:, i, :], pr[:, i, :])
                        link(ins)
                        link(v.memset(top[:, :, TOPK:8], -1.0))
                        for i in range(NT):
                            ins = v.match_replace(rep[:, i, :], top[:, i, :], pr[:, i, :], -2.0)
                        link(ins)
                        link(v.tensor_tensor(comb[:, :, 0:E], rep[:, :, 0:E], pr[:, :, 0:E], ALU.not_equal))
                        link(v.tensor_tensor(comb[:, :, 0:E], comb[:, :, 0:E], pr[:, :, 0:E], ALU.mult))
                        link(v.tensor_reduce(row_t[:, 1, :], comb[:, :, 0:E], AX, ALU.add))
                        link(v.tensor_scalar(row_t[:, 1, :], row_t[:, 1, :], 1e-9, None, ALU.max))
                        link(v.reciprocal(row_t[:, 2, :], row_t[:, 1, :]))
                        link(v.tensor_tensor(comb[:, :, 0:E], comb[:, :, 0:E], bc(row_t[:, 2, :], 2, E), ALU.mult))
                        link(v.tensor_scalar(lg[:, :, E:EG], lg[:, :, E:EG], 1.0, None, ALU.add))
                        v.reciprocal(comb[:, :, E:EG], lg[:, :, E:EG]).then_inc(comb_ready, 1)
                        for n in range(NTG):
                            dve.wait_ge(comb_high, n + 1)
                            at = slice(n * TG, (n + 1) * TG)
                            v.tensor_tensor(combT[LOW_ROW:LOW_ROW + EG, at], psum[0:EG, n, :], combT[0:EG, at].bitcast(F32), ALU.subtract).then_inc(combT_ready, 1)

            y_acc = hT
            silu = sb("silu", [P, 2, TG], stack=ff)
            su = sb("su", [P, 2, TG], stack=ff)
            act_w = sb("act_w", [P, 2, TG], stack=ff)
            act_split = sb("act_split", [P, 2, 2, TG], F32R, stack=ff)
            y_part = sb("y_part", [P, KH, TG], stack=ff)
            yT = sb("yT", [P, KH, TG], stack=ff)
            y_tok = sb("y_tok", [P, 2, 2, HID], stack=ff)
            y_out = sb("y_out", [P, 2, 2, HID], stack=ff)
            names = ("gate_done up_done pick_done silu_done su_done act_ready act_high act_low down_done part_ready part_added "
                     "yT_ready y_turned y_gated y_ready y_stored0 y_stored1")
            f = {n: sem(n, ff) for n in names.split()}
            G_BANK, U_BANK, Y_BANK, W_BANK, X_BANK = 0, 2, 4, 6, 7

            def group_base(c, n):
                return (c * NTG + n) * CT

            def run_groups(eng, body):
                for c in range(NCH - 1):
                    if c == 0:
                        body(0, 0)
                    with eng.Fori(1 if c == 0 else 0, NTG - 1) as n:
                        body(c, n)
                    body(c, NTG - 1)
                for n in range(NTG):
                    body(NCH - 1, n)

            with nc.Block() as block:
                @block.sync
                def _(sp):
                    for c in range(2, NCH):
                        load_chunk(sp, c)
                    out = d["out"].rearrange("(t p) n -> p t n", p=P)
                    for r in range(2 * NTG):
                        sp.wait_ge(f["y_ready"], r + 1)
                        sp.dma_start(out[:, 2 * r:2 * r + 2, :], y_out[:, r % 2, :, :]).then_inc(f[f"y_stored{r % 2}"], 16)
                    for b in range(2):
                        sp.wait_ge(f[f"y_stored{b}"], 16 * NTG)

                @block.gpsimd
                def _(pool):
                    for c in range(2, NCH):
                        pool.wait_ge(f["down_done"], (c - 1) * NTG * CT)
                        split_chunk(pool, c)

                @block.tensor
                def _(pe):
                    t = nc.tensor

                    def up(c, n, j):
                        at = bass.ds(n * TG, TG)
                        rhs = [[h2[:, part, k, at] for part in range(2)] for k in range(KH)]
                        b, tile = j % 2, group_base(c, n) + j
                        pe.wait_ge(ff_split, c + 1)
                        if not (isinstance(tile, int) and tile < 2):
                            pe.wait_ge(f["act_ready"], tile - 1)
                        for m, bank, done in ((0, G_BANK, "gate_done"), (1, U_BANK, "up_done")):
                            for k in range(KH):
                                col = m * GU + k * CT * P + j * P
                                ins = product(psum[:, bank + b, :], [w_ff[:, c % 2, part, col:col + P] for part in range(2)], rhs[k],
                                              k == 0, k == KH - 1)
                            ins.then_inc(f[done], 1)
                        pe.wait_ge(f["act_ready"], tile)
                        row = (c * CT + j) * P
                        t.matmul(psum[:, W_BANK, :], pick[:, row:row + P], combT[:, at], start=True, stop=True).then_inc(f["pick_done"], 1)

                    def down(c, n, j):
                        tile = group_base(c, n) + j
                        if j == 0:
                            pe.wait_ge(f["part_ready"], c * NTG + n)
                        pe.wait_ge(f["act_high"], tile + 1)
                        w = [[w_ff[:, c % 2, part, 2 * GU + j * HID + m * P:2 * GU + j * HID + (m + 1) * P] for part in range(2)] for m in range(KH)]
                        for m in range(KH):
                            t.matmul(psum[:, Y_BANK + m, :], w[m][1], act_split[:, j % 2, 0, :], start=(j == 0), stop=False)
                            t.matmul(psum[:, Y_BANK + m, :], w[m][0], act_split[:, j % 2, 0, :], start=False, stop=False)
                        pe.wait_ge(f["act_low"], tile + 1)
                        for m in range(KH):
                            ins = t.matmul(psum[:, Y_BANK + m, :], w[m][0], act_split[:, j % 2, 1, :], start=False, stop=(j == CT - 1))
                        ins.then_inc(f["down_done"], 1)

                    def turn_y(r):
                        pe.wait_ge(f["yT_ready"], r // 2 + 1)
                        pe.wait_ge(f["y_gated"], r)
                        for q in range(2):
                            for k in range(KH):
                                at = (r % 2) * 2 * P + q * P
                                ins = t.transpose(psum[:, X_BANK, q * HID + k * P:q * HID + (k + 1) * P], yT[:, k, at:at + P], ident[:])
                        ins.then_inc(f["y_turned"], 1)

                    def body(c, n):
                        end = isinstance(n, int) and n == NTG - 1
                        for j in range(CT):
                            if j + 1 < CT:
                                up(c, n, j + 1)
                            elif not end:
                                up(c, n + 1, 0)
                            elif c + 1 < NCH:
                                up(c + 1, 0, 0)
                            down(c, n, j)
                            if c == NCH - 1 and n > 0 and j in (1, 2):
                                turn_y(2 * (n - 1) + j - 1)

                    up(0, 0, 0)
                    run_groups(pe, body)
                    turn_y(2 * NTG - 2)
                    turn_y(2 * NTG - 1)

                @block.scalar
                def _(act):
                    a = nc.scalar

                    def gate(tile, j):
                        act.wait_ge(f["gate_done"], tile + 1)
                        if not (isinstance(tile, int) and tile < 2):
                            act.wait_ge(f["su_done"], tile - 1)
                        a.activation(silu[:, j % 2, :], psum[:, G_BANK + j % 2, :], ACT.Silu).then_inc(f["silu_done"], 1)

                    def high(tile, j):
                        act.wait_ge(f["act_ready"], tile + 1)
                        if not (isinstance(tile, int) and tile < 2):
                            act.wait_ge(f["down_done"], tile - 1)
                        a.copy(act_split[:, j % 2, 0, :], act_w[:, j % 2, :]).then_inc(f["act_high"], 1)

                    def take_part(c, n):
                        act.wait_ge(f["down_done"], group_base(c, n) + CT)
                        if c == NCH - 1 and n > 0:
                            act.wait_ge(f["yT_ready"], n)
                        else:
                            act.wait_ge(f["part_added"], c * NTG + n)
                        a.copy(y_part[:].rearrange("p k t -> p (k t)"), psum[:, Y_BANK:Y_BANK + 2, :].rearrange("p a b -> p (a b)")).then_inc(f["part_ready"], 1)

                    def body(c, n):
                        last = isinstance(n, int) and n == NTG - 1 and c == NCH - 1
                        for j in range(CT):
                            tile = group_base(c, n) + j
                            high(tile, j)
                            if not (last and j == CT - 1):
                                gate(tile + 1, (j + 1) % CT)
                        take_part(c, n)

                    gate(0, 0)
                    run_groups(act, body)

                @block.vector
                def _(dve):
                    v = nc.vector

                    def weigh(c, n, j):
                        tile = group_base(c, n) + j
                        dve.wait_ge(f["silu_done"], tile + 1)
                        dve.wait_ge(f["up_done"], tile + 1)
                        v.tensor_tensor(su[:, j % 2, :], silu[:, j % 2, :], psum[:, U_BANK + j % 2, :], ALU.mult).then_inc(f["su_done"], 1)
                        dve.wait_ge(f["su_done"], tile + 1)
                        dve.wait_ge(f["pick_done"], tile + 1)
                        v.tensor_tensor(act_w[:, j % 2, :], su[:, j % 2, :], psum[:, W_BANK, :], ALU.mult).then_inc(f["act_ready"], 1)
                        dve.wait_ge(f["act_high"], tile + 1)
                        v.tensor_tensor(act_split[:, j % 2, 1, :], act_w[:, j % 2, :], act_split[:, j % 2, 0, :].bitcast(F32),
                                        ALU.subtract).then_inc(f["act_low"], 1)

                    def add_part(p, slot):
                        dve.wait_ge(f["part_ready"], p + 1)
                        if not (isinstance(p, int) and p == 0):
                            dve.wait_ge(f["part_added"], p)
                        at = bass.ds(slot * TG, TG)
                        v.tensor_tensor(y_acc[:, :, at], y_acc[:, :, at], y_part[:], ALU.add).then_inc(f["part_added"], 1)

                    def complete(n):
                        p = (NCH - 1) * NTG + n
                        dve.wait_ge(f["part_ready"], p + 1)
                        dve.wait_ge(f["part_added"], (NCH - 1) * NTG)
                        if n:
                            dve.wait_ge(f["y_turned"], 2 * n)
                        v.tensor_tensor(yT[:], y_acc[:, :, n * TG:(n + 1) * TG], y_part[:], ALU.add).then_inc(f["yT_ready"], 1)

                    def finish(r):
                        b = r % 2
                        dve.wait_ge(f["y_turned"], r + 1)
                        if r >= 2:
                            dve.wait_ge(f["y_ready"], r - 1)
                        v.tensor_tensor(y_tok[:, b, :, :], psum[:, X_BANK, :].rearrange("p (q n) -> p q n", q=2), bc(gates[:, 1, :], 1, 2),
                                        ALU.mult).then_inc(f["y_gated"], 1)
                        dve.wait_ge(f["y_gated"], r + 1)
                        if r >= 2:
                            dve.wait_ge(f[f"y_stored{b}"], 16 * (r // 2))
                        v.tensor_tensor(y_out[:, b, :, :], y_tok[:, b, :, :], x_acc[:, 2 * r:2 * r + 2, :], ALU.add).then_inc(f["y_ready"], 1)

                    def body(c, n):
                        for j in range(CT):
                            weigh(c, n, j)
                            if j == 0 and c == NCH - 1 and n > 0:
                                complete(n - 1)
                            elif j == 0 and not (c == 0 and isinstance(n, int) and n == 0):
                                add_part(c * NTG + n - 1, (n + NTG - 1) & (NTG - 1))
                            if c == NCH - 1 and n > 0 and j in (2, 3):
                                finish(2 * (n - 1) + j - 2)

                    run_groups(dve, body)
                    complete(NTG - 1)
                    finish(2 * NTG - 2)
                    finish(2 * NTG - 1)


def shape_constants():
    bf16 = mybir.dt.np(BF16)
    f = np.float32
    half = np.arange(HALF, dtype=f)
    inv_freq = (f(1.0) / np.power(f(10000.0), half * f(2.0) / f(ROPE))).astype(f)
    pos = np.arange(S, dtype=f).reshape(NT, P)
    ends = (np.arange(C, dtype=f) * R + (R - 1)).reshape(1, C)
    ang = np.concatenate([pos, ends])[:, :, None] * inv_freq
    trig = np.stack([np.cos(ang), np.sin(ang), -np.sin(ang)], 2).transpose(1, 0, 2, 3)
    s = np.arange(P)[:, None]
    t = np.arange(P)[None, :]
    mask = np.zeros((P, NT, LW), f)
    cur, prev = np.where(t <= s, 0, MASKED), np.where(s + P - t <= WIN, 0, MASKED)
    for i in range(NT):
        own, other = (i % 2) * P, (1 - i % 2) * P
        mask[:, i, own:own + P] = cur
        mask[:, i, other:other + P] = prev if i else MASKED
        mask[:, i, 2 * P:2 * P + C] = np.where(R * t + R - 1 <= P * i + s, 0, MASKED)
    owner = np.minimum(np.arange(FW) // I_MOE, E)
    pick = (owner[None, :] == (np.arange(P) % LOW_ROW)[:, None]).astype(f)
    pick[LOW_ROW + EG:] = 0
    return {"ident": np.eye(P, dtype=f), "ident_b": np.eye(P).astype(bf16), "pick": pick,
            "trig": np.ascontiguousarray(trig.astype(f)), "mask": mask.astype(bf16)}


def kernel(**inputs):
    import concourse.bacc as bacc
    from concourse.bass_utils import run_bass_kernel_spmd

    a = {k.replace("L0_attn_", "").replace("L0_ffn_", ""): np.asarray(v) for k, v in inputs.items()}
    zeros = np.zeros((HID, FW - E * I_MOE - I_SH), np.float32)

    def up_layout(experts, shared):
        return np.concatenate([experts.transpose(1, 0, 2).reshape(HID, E * I_MOE), shared, zeros], 1)

    def up_chunks(w):
        return w.reshape(KH, P, NCH, CT * P).transpose(2, 1, 0, 3).reshape(NCH, P, GU)

    down = np.concatenate([a["w_down"].reshape(E * I_MOE, HID), a["sh_down"], zeros.T])
    w_ff = np.concatenate([up_chunks(up_layout(a["w_gate"], a["sh_gate"])), up_chunks(up_layout(a["w_up"], a["sh_up"])),
                           down.reshape(NCH, CT, P, HID).transpose(0, 2, 1, 3).reshape(NCH, P, CT * HID)], 2)
    w_groups = np.stack([a["Wlk"], a["Wq"], a["Wlv"]]).reshape(3, KH, P, NG, GW).transpose(3, 2, 0, 1, 4)
    w_groups = w_groups.reshape(NG, P, NT, WCH).transpose(0, 2, 1, 3)
    w_out = a["Wo"].reshape(NG, HG, P, HID).transpose(0, 2, 1, 3).reshape(NG, P, NT, OCH).transpose(0, 2, 1, 3)
    arrays = {
        "x": a["hidden_states"].reshape(S, HID), "w_groups": w_groups, "Wo": a["Wo"], "w_out": w_out,
        "Wk": a["Wk"], "Wv": a["Wv"], "wcT": a["Wc"].reshape(KH, P).T, "bc": a["bc"],
        "bias_qk": np.concatenate([a["blk"].reshape(NG, GW), a["bq"].reshape(NG, GW)], 1),
        "rows": np.stack([a["bk"], a["bv"], a["kn_w"], a["qn_w"]]),
        "sink_kT": a["sink_k"].T, "sink_vT": a["sink_v"].T, "blvT": a["blv"].reshape(NH, HD).T, "bo": a["bo"],
        "w_rt": np.concatenate([a["router_w"].T, a["sh_gate_w"]], 1),
        "w_ff": w_ff,
        "cT": a["L0_c"].reshape(KH, P).T, "wmod": a["L0_wmod"],
    }
    arrays.update(shape_constants())
    nc = bacc.Bacc("TRN2", target_bir_lowering=False, num_devices=1)
    d, feed = {}, {}
    for name, arr in arrays.items():
        arr = np.ascontiguousarray(arr)
        feed[f"in_{name}"] = arr
        d[name] = nc.dram_tensor(f"in_{name}", arr.shape, mybir.dt.from_np(arr.dtype), kind="ExternalInput").ap()
    d["out"] = nc.dram_tensor("out_x", (S, HID), F32, kind="ExternalOutput").ap()
    build(nc, d)
    r = run_bass_kernel_spmd(nc, [feed], core_ids=[0])
    return r.results[0]["out_x"].reshape(1, S, HID)
```
